# Optimizing a Trainium2 kernel written in Bass

```python
import numpy as np
import jax
import jax.numpy as jnp

def _softmax(x, axis=-1):
    return jax.nn.softmax(x, axis=axis)

def _gelu(x):
    return jax.nn.gelu(x, approximate=True)

def _silu(x):
    return jax.nn.silu(x)

def _sigmoid(x):
    return jax.nn.sigmoid(x)

def _layernorm(x, axis=-1, eps=1e-05):
    m = jnp.mean(x, axis=axis, keepdims=True)
    v = jnp.var(x, axis=axis, keepdims=True)
    return (x - m) / jnp.sqrt(v + eps)

def _scatter_add(tgt, idx, src, axis=0):
    return tgt.at[idx].add(src)

def _segment_sum(src, seg, n):
    return jax.ops.segment_sum(src, seg, n)
kernel_name = 'mk_gnn_preln_d2_gnn_r64_d1f9e3'

def setup_inputs(seed: int=0):
    np.random.seed(seed)
    _w = jnp.asarray

    def _rec_inputs():
        import jax
        import jax.numpy as jnp
        _gk = jax.random.key(seed)
        x = -0.0005121 + 1.001 * jax.random.normal(jax.random.fold_in(_gk, 1), (50000, 64), jnp.float32)
        src = jax.random.randint(jax.random.fold_in(_gk, 2), (25000,), 0, 50000, jnp.int32)
        dst = jnp.minimum((50000 * jax.random.uniform(jax.random.fold_in(_gk, 3), (25000,)) ** 2.0).astype(jnp.int32), 49999)
        _o = jnp.argsort(dst, stable=True)
        src = src[_o]
        dst = dst[_o]
        edge_attr_16 = 0.000398945 + 1.00003 * jax.random.normal(jax.random.fold_in(_gk, 12), (25000, 16), jnp.float32)
        edge_attr_64 = -0.000129727 + 1.00004 * jax.random.normal(jax.random.fold_in(_gk, 13), (25000, 64), jnp.float32)
        return (x, src, dst, edge_attr_16, edge_attr_64)
    x, src, dst, edge_attr_16, edge_attr_64 = _rec_inputs()

    def _L0_gnn_setup():
        import jax, jax.numpy as jnp
        import numpy as np
        N, E, C, H, DE, B = (50000, 6250, 64, 4, 16, 64)
        EPS = 1e-05
        NEG_SLOPE = 0.2
        NBLOCKS = 2

        def _segment_mean(v, seg, num):
            s = jax.ops.segment_sum(v, seg, num_segments=num)
            cnt = jax.ops.segment_sum(jnp.ones((v.shape[0], 1), v.dtype), seg, num_segments=num)
            return s / jnp.maximum(cnt, 1.0)

        def _graph_norm(x, batch, w, b, ms):
            mean = _segment_mean(x, batch, B)
            sub = x - ms * mean[batch]
            var = _segment_mean(sub * sub, batch, B)
            return sub / jnp.sqrt(var[batch] + EPS) * w + b

        def _gatv2(x, src, dst, ea, Wl, Wr, We, att, bias):
            xl = (x @ Wl).reshape(N, H, C)
            xr = (x @ Wr).reshape(N, H, C)
            ee = (ea @ We).reshape(-1, H, C)
            f = jax.nn.leaky_relu(xl[src] + xr[dst] + ee, NEG_SLOPE)
            logits = jnp.einsum('ehc,hc->eh', f, att)
            m = jax.ops.segment_max(logits, dst, num_segments=N)
            a = jnp.exp(logits - m[dst])
            denom = jax.ops.segment_sum(a, dst, num_segments=N)
            alpha = a / denom[dst]
            out = jax.ops.segment_sum(xl[src] * alpha[:, :, None], dst, num_segments=N)
            return out.mean(axis=1) + bias
        key = jax.random.key(seed)
        ks = jax.random.split(key, 8)
        x = jax.random.normal(ks[0], (N, C), jnp.float32)
        edge_index = jax.random.randint(ks[1], (2, E), 0, N, dtype=jnp.int64)
        edge_attr = jax.random.normal(ks[2], (E, DE), jnp.float32)
        batch = jnp.sort(jax.random.randint(ks[3], (N,), 0, B, dtype=jnp.int64))
        s = 1.0 / np.sqrt(C)
        Wl = jax.random.normal(ks[4], (NBLOCKS, C, H * C), jnp.float32) * s
        Wr = jax.random.normal(ks[5], (NBLOCKS, C, H * C), jnp.float32) * s
        We = jax.random.normal(ks[6], (NBLOCKS, DE, H * C), jnp.float32) * (1.0 / np.sqrt(DE))
        att = jax.random.normal(ks[7], (NBLOCKS, H, C), jnp.float32) * s
        gat_bias = jnp.zeros((NBLOCKS, C), jnp.float32)
        gn_weight = jnp.ones((NBLOCKS, C), jnp.float32)
        gn_bias = jnp.zeros((NBLOCKS, C), jnp.float32)
        gn_mean_scale = jnp.ones((NBLOCKS, C), jnp.float32)
        return dict(x=x, edge_index=edge_index, edge_attr=edge_attr, batch=batch, Wl=Wl, Wr=Wr, We=We, att=att, gat_bias=gat_bias, gn_weight=gn_weight, gn_bias=gn_bias, gn_mean_scale=gn_mean_scale)
    _L0_gnn_all = _L0_gnn_setup()
    _L0_gnn_in = {k: v for k, v in _L0_gnn_all.items() if k in ('Wl', 'Wr', 'We', 'att', 'gat_bias', 'gn_weight', 'gn_bias', 'gn_mean_scale')}
    del _L0_gnn_all

    def _L1_gnn_setup():
        import jax, jax.numpy as jnp
        import numpy as np
        N, E = (100000, 12500)
        INPUTS, HIDDEN = (64, 64)
        EPS = 1e-05

        def _mlp(h, W1, b1, g, be, W2, b2):
            h = h @ W1 + b1
            mu = jnp.mean(h, axis=0)
            var = jnp.var(h, axis=0)
            h = (h - mu) * jax.lax.rsqrt(var + EPS) * g + be
            h = jax.nn.relu(h)
            return h @ W2 + b2
        key = jax.random.key(seed)
        ks = jax.random.split(key, 16)
        d_in = INPUTS + HIDDEN

        def lin_init(k, fan_in, fan_out):
            kw, kb = jax.random.split(k)
            bound = 1.0 / np.sqrt(fan_in)
            W = jax.random.uniform(kw, (fan_in, fan_out), jnp.float32, -bound, bound)
            b = jax.random.uniform(kb, (fan_out,), jnp.float32, -bound, bound)
            return (W, b)
        W1a, b1a = lin_init(ks[0], d_in, HIDDEN)
        W2a, b2a = lin_init(ks[1], HIDDEN, HIDDEN)
        W1b, b1b = lin_init(ks[2], d_in, HIDDEN)
        W2b, b2b = lin_init(ks[3], HIDDEN, HIDDEN)
        return {'x': jax.random.normal(ks[4], (N, INPUTS), jnp.float32), 'edge_index': jax.random.randint(ks[5], (2, E), 0, N, jnp.int64), 'edge_attr': jax.random.normal(ks[6], (E, HIDDEN), jnp.float32), 'u': jax.random.normal(ks[7], (1, 8), jnp.float32), 'batch': jnp.zeros((N,), jnp.int64), 'W1a': W1a, 'b1a': b1a, 'g1': jnp.ones((HIDDEN,), jnp.float32), 'be1': jnp.zeros((HIDDEN,), jnp.float32), 'W2a': W2a, 'b2a': b2a, 'W1b': W1b, 'b1b': b1b, 'g2': jnp.ones((HIDDEN,), jnp.float32), 'be2': jnp.zeros((HIDDEN,), jnp.float32), 'W2b': W2b, 'b2b': b2b}
    _L1_gnn_all = _L1_gnn_setup()
    _L1_gnn_in = {k: v for k, v in _L1_gnn_all.items() if k in ('u', 'W1a', 'b1a', 'g1', 'be1', 'W2a', 'b2a', 'W1b', 'b1b', 'g2', 'be2', 'W2b', 'b2b')}
    del _L1_gnn_all
    return {'x': x, 'src': src, 'dst': dst, 'edge_attr_16': edge_attr_16, 'edge_attr_64': edge_attr_64, 'L0_gnn_Wl': _L0_gnn_in['Wl'], 'L0_gnn_Wr': _L0_gnn_in['Wr'], 'L0_gnn_We': _L0_gnn_in['We'], 'L0_gnn_att': _L0_gnn_in['att'], 'L0_gnn_gat_bias': _L0_gnn_in['gat_bias'], 'L0_gnn_gn_weight': _L0_gnn_in['gn_weight'], 'L0_gnn_gn_bias': _L0_gnn_in['gn_bias'], 'L0_gnn_gn_mean_scale': _L0_gnn_in['gn_mean_scale'], 'L1_gnn_u': _L1_gnn_in['u'], 'L1_gnn_W1a': _L1_gnn_in['W1a'], 'L1_gnn_b1a': _L1_gnn_in['b1a'], 'L1_gnn_g1': _L1_gnn_in['g1'], 'L1_gnn_be1': _L1_gnn_in['be1'], 'L1_gnn_W2a': _L1_gnn_in['W2a'], 'L1_gnn_b2a': _L1_gnn_in['b2a'], 'L1_gnn_W1b': _L1_gnn_in['W1b'], 'L1_gnn_b1b': _L1_gnn_in['b1b'], 'L1_gnn_g2': _L1_gnn_in['g2'], 'L1_gnn_be2': _L1_gnn_in['be2'], 'L1_gnn_W2b': _L1_gnn_in['W2b'], 'L1_gnn_b2b': _L1_gnn_in['b2b']}

def reference(x, src, dst, edge_attr_16, edge_attr_64, L0_gnn_Wl, L0_gnn_Wr, L0_gnn_We, L0_gnn_att, L0_gnn_gat_bias, L0_gnn_gn_weight, L0_gnn_gn_bias, L0_gnn_gn_mean_scale, L1_gnn_u, L1_gnn_W1a, L1_gnn_b1a, L1_gnn_g1, L1_gnn_be1, L1_gnn_W2a, L1_gnn_b2a, L1_gnn_W1b, L1_gnn_b1b, L1_gnn_g2, L1_gnn_be2, L1_gnn_W2b, L1_gnn_b2b):
    import jax
    import jax.numpy as jnp

    def _L0_gnn_ref(x, edge_index, edge_attr, batch, Wl, Wr, We, att, gat_bias, gn_weight, gn_bias, gn_mean_scale):
        import jax, jax.numpy as jnp
        import numpy as np
        N, E, C, H, DE, B = (50000, 6250, 64, 4, 16, 64)
        EPS = 1e-05
        NEG_SLOPE = 0.2
        NBLOCKS = 2

        def _segment_mean(v, seg, num):
            s = jax.ops.segment_sum(v, seg, num_segments=num)
            cnt = jax.ops.segment_sum(jnp.ones((v.shape[0], 1), v.dtype), seg, num_segments=num)
            return s / jnp.maximum(cnt, 1.0)

        def _graph_norm(x, batch, w, b, ms):
            mean = _segment_mean(x, batch, B)
            sub = x - ms * mean[batch]
            var = _segment_mean(sub * sub, batch, B)
            return sub / jnp.sqrt(var[batch] + EPS) * w + b

        def _gatv2(x, src, dst, ea, Wl, Wr, We, att, bias):
            xl = (x @ Wl).reshape(N, H, C)
            xr = (x @ Wr).reshape(N, H, C)
            ee = (ea @ We).reshape(-1, H, C)
            f = jax.nn.leaky_relu(xl[src] + xr[dst] + ee, NEG_SLOPE)
            logits = jnp.einsum('ehc,hc->eh', f, att)
            m = jax.ops.segment_max(logits, dst, num_segments=N)
            a = jnp.exp(logits - m[dst])
            denom = jax.ops.segment_sum(a, dst, num_segments=N)
            alpha = a / denom[dst]
            out = jax.ops.segment_sum(xl[src] * alpha[:, :, None], dst, num_segments=N)
            return out.mean(axis=1) + bias
        loop = jnp.arange(N, dtype=edge_index.dtype)
        src = jnp.concatenate([edge_index[0], loop])
        dst = jnp.concatenate([edge_index[1], loop])
        ea = jnp.concatenate([edge_attr, jnp.broadcast_to(edge_attr.mean(axis=0), (N, DE))])
        residual = x
        for i in range(NBLOCKS):
            h = _graph_norm(x, batch, gn_weight[i], gn_bias[i], gn_mean_scale[i])
            h = jax.nn.relu(h)
            x = _gatv2(h, src, dst, ea, Wl[i], Wr[i], We[i], att[i], gat_bias[i])
        return x + residual

    def _L1_gnn_ref(x, edge_index, edge_attr, u, batch, W1a, b1a, g1, be1, W2a, b2a, W1b, b1b, g2, be2, W2b, b2b):
        import jax, jax.numpy as jnp
        import numpy as np
        N, E = (100000, 12500)
        INPUTS, HIDDEN = (64, 64)
        EPS = 1e-05

        def _mlp(h, W1, b1, g, be, W2, b2):
            h = h @ W1 + b1
            mu = jnp.mean(h, axis=0)
            var = jnp.var(h, axis=0)
            h = (h - mu) * jax.lax.rsqrt(var + EPS) * g + be
            h = jax.nn.relu(h)
            return h @ W2 + b2
        row, col = (edge_index[0], edge_index[1])
        n = x.shape[0]
        out = jnp.concatenate([x[row], edge_attr], axis=1)
        out = _mlp(out, W1a, b1a, g1, be1, W2a, b2a)
        summed = jax.ops.segment_sum(out, col, num_segments=n)
        cnt = jax.ops.segment_sum(jnp.ones((out.shape[0],), out.dtype), col, num_segments=n)
        mean = summed / jnp.maximum(cnt, 1.0)[:, None]
        out = jnp.concatenate([x, mean], axis=1)
        return _mlp(out, W1b, b1b, g2, be2, W2b, b2b)
    edge_index = jnp.stack([src, dst])
    batch0 = jnp.zeros((50000,), jnp.int32)
    h = jnp.maximum(_layernorm(x, axis=-1), 0.0)
    x = x + _L0_gnn_ref(h, edge_index, edge_attr_16, batch0, L0_gnn_Wl, L0_gnn_Wr, L0_gnn_We, L0_gnn_att, L0_gnn_gat_bias, L0_gnn_gn_weight, L0_gnn_gn_bias, L0_gnn_gn_mean_scale)
    h = jnp.maximum(_layernorm(x, axis=-1), 0.0)
    x = x + _L1_gnn_ref(h, edge_index, edge_attr_64, L1_gnn_u, batch0, L1_gnn_W1a, L1_gnn_b1a, L1_gnn_g1, L1_gnn_be1, L1_gnn_W2a, L1_gnn_b2a, L1_gnn_W1b, L1_gnn_b1b, L1_gnn_g2, L1_gnn_be2, L1_gnn_W2b, L1_gnn_b2b)
    return x

_drawn_inputs = setup_inputs


def setup_inputs(seed=0):
    import zlib

    import numpy as np

    out = dict(_drawn_inputs(seed))
    spreads = {'L0_gnn_gat_bias': (0.0, 0.1),
     'L0_gnn_gn_weight': (1.0, 0.2),
     'L0_gnn_gn_bias': (0.0, 0.34),
     'L0_gnn_gn_mean_scale': (1.0, 0.56),
     'L1_gnn_g1': (1.0, 0.6),
     'L1_gnn_be1': (0.0, 0.8),
     'L1_gnn_g2': (1.0, 0.2),
     'L1_gnn_be2': (0.0, 0.302)}
    factors = {'L0_gnn_Wr': 5.893, 'L1_gnn_b1a': 8.0, 'L1_gnn_b2a': 4.373, 'L1_gnn_b1b': 8.0}
    for name, (base, spread) in spreads.items():
        noise = np.random.default_rng([zlib.crc32(name.encode()), seed]).standard_normal(out[name].shape)
        drawn = base * np.exp(spread * noise) if base else spread * noise
        out[name] = jnp.asarray(drawn.astype(out[name].dtype))
    for name, factor in factors.items():
        out[name] = (out[name] * factor).astype(out[name].dtype)
    return out
```

```python
from contextlib import ExitStack

import numpy as np

import concourse.bass as bass
from concourse import mybir

F32 = mybir.dt.float32
I32 = mybir.dt.int32
BF16 = mybir.dt.bfloat16
ALU = mybir.AluOpType
ACT = mybir.ActivationFunctionType
AX = mybir.AxisListType.X

N, C, H, DE, E = 50000, 64, 4, 16, 25000
NBLOCKS = 2
EPS = 1e-5
SLOPE = 0.2
P = 128
GRID = N // P
TAIL = N - P * GRID
SUP, SUB = 30, 6
NSUP, NSUB = GRID // SUP, GRID // SUB
TILES, CT = 200, 4
CH = CT * P
NCH = TILES // CT
EP = TILES * P
RG = 2
RT = TILES // RG
FAR = 1 << 20
BIG = float(2.0**100)
WIN = E // NCH


def grid_view(table):
    return table[0:P * GRID, :].rearrange("(p t) c -> p t c", p=P)


def start_of(eng, i, k, size):
    return (2 * i + k) * size if isinstance(i, int) else eng.snap((2 * i + k) * size)


def build(nc, a, out):
    with ExitStack() as ctx:
        def sb(name, shape, dt=F32):
            return ctx.enter_context(nc.sbuf_tensor(name, shape, dt))

        def dram(name, shape, dt=F32):
            return nc.dram_tensor(name, shape, dt, kind="Internal").ap()

        m = {}
        m["bank"] = [ctx.enter_context(nc.psum_tensor(f"bank{n}", [P, 512], F32)) for n in range(8)]
        m["T"] = [dram(f"table_x{n}", [N, C]) for n in range(NBLOCKS + 1)]
        m["H2"] = dram("table_h2", [N, C])
        m["XA"] = dram("table_xa", [N, C])
        m["MEAN"] = dram("table_mean", [N, C])
        m["alpha_rows"] = [dram(f"alpha_rows{n}", [H, EP]) for n in range(NBLOCKS)]
        m["cont_row"] = dram("cont_row", [EP], BF16)

        m["ident"] = sb("ident", [P, P])
        m["gidx"] = sb("gidx", [P, TILES, 2], I32)
        m["sidx"] = sb("sidx", [P, TILES], I32)
        for n in ("cF", "nF", "cB", "nB"):
            m[n] = sb(n, [RT, RG, H, P], BF16)
        for n in ("inF", "nInF", "inB", "nInB"):
            m[n] = sb(n, [RT, RG, P])
        for n in ("wF", "wB", "nWF", "nWB"):
            m[n] = sb(n, [H, TILES])
        m["AB"] = sb("AB", [P, 2])
        m["stats"] = sb("stats", [P, 2 * NSUB + 1, 6])
        m["small"] = sb("small", [C, 16])

        stage(setup_edges, nc, a, m)
        stage(dense_norm, nc, m, "h0", [a["x"]], None, m["T"][0], stats=True)
        for b in range(NBLOCKS):
            with ExitStack() as w:
                stage(gat_weights, nc, a, m, b, w)
                if b:
                    stage(table_stats, nc, m, b)
                stage(norm_coefficients, nc, m, f"gn{b}", a["gn_weight"][b:b + 1, :], a["gn_bias"][b:b + 1, :],
                                  a["gn_mean_scale"][b:b + 1, :])
                stage(gat_base, nc, m, b)
                m["HT"] = w.enter_context(nc.sbuf_tensor(f"HT{b}", [P, EP], F32))
                with ExitStack() as logits:
                    m["logits"] = logits.enter_context(nc.sbuf_tensor(f"logits{b}", [P, TILES, 2 * H], F32))
                    stage(gat_logits, nc, a, m, b)
                    stage(gat_softmax, nc, m, b)
                stage(gat_values, nc, m, b)
        stage(dense_norm, nc, m, "h2", [a["x"], m["T"][2], m["T"][0]], m["XA"], m["H2"], stats=False)
        with ExitStack() as w:
            stage(node_weights, nc, a, m, w)
            with ExitStack() as hidden:
                m["ZE"] = hidden.enter_context(nc.sbuf_tensor("edge_z", [C, EP], F32))
                stage(edge_hidden, nc, a, m)
                stage(norm_coefficients, nc, m, "bn1", a["g1"], a["be1"], None, chunks=NCH)
                stage(edge_means, nc, m)
            m["ZN"] = w.enter_context(nc.sbuf_tensor("node_z", [P, NSUB * SUB // 2 * P + TAIL], F32))
            stage(node_hidden, nc, m)
            stage(norm_coefficients, nc, m, "bn2", a["g2"], a["be2"], None)
            stage(node_out, nc, m, out)


def stage(function, nc, *args, **kwargs):
    function(nc, *args, **kwargs)
    nc.all_engine_barrier()


def sems(ctx, nc, stage, *names):
    made = [nc.alloc_semaphore(f"{stage}_{n}") for n in names]
    ctx.callback(nc.clear_and_free_semaphores, made)
    return made


def pair(ctx, nc, stage, name):
    return sems(ctx, nc, stage, f"{name}0", f"{name}1")


def in_order(eng, sem):
    n = [0]

    def step(ins):
        n[0] += 1
        ins.then_inc(sem, 1)
        eng.wait_ge(sem, n[0])

    return step


def later(i):
    return not (isinstance(i, int) and i == 0)


def two_by_two(eng, count, *parts, tail=None, peel=False):
    for part in parts if peel else ():
        for k in range(2):
            part(0, k)
    with eng.Fori(int(peel), count // 2) as i:
        for part in parts:
            for k in range(2):
                part(i, k)
    rest = [{}] * (count % 2) + ([{"tail": True}] if tail else [])
    for part in parts:
        for k, kind in enumerate(rest):
            part(count // 2, k, **kind)


def setup_edges(nc, a, m):
    with ExitStack() as ctx:
        loaded, made, stored, dv, pv, tr, tc = sems(
            ctx, nc, "edges", "loaded", "made", "stored", "dve_chain", "pool_chain", "turned", "copied")
        pt = ctx.enter_context(nc.sbuf_tensor("pt", [P, 4, TILES], I32))
        ptf = ctx.enter_context(nc.sbuf_tensor("ptf", [P, 3, TILES], F32))
        rows = ctx.enter_context(nc.sbuf_tensor("rows", [RT, 3, RG, P], I32))
        rowf = ctx.enter_context(nc.sbuf_tensor("rowf", [RT, 3, RG, P], F32))
        cont = ctx.enter_context(nc.sbuf_tensor("cont", [RT, 4, RG, P], F32))
        controw = ctx.enter_context(nc.sbuf_tensor("controw", [RT, RG, P], BF16))
        edgeF = ctx.enter_context(nc.sbuf_tensor("edgeF", [RT, RG, P], F32))
        edgeB = ctx.enter_context(nc.sbuf_tensor("edgeB", [RT, RG, P], F32))
        wcol = ctx.enter_context(nc.sbuf_tensor("wcol", [RT, 2, RG, H], F32))
        ident = m["ident"]
        bank = m["bank"][0]
        with nc.Block() as block:

            @block.sync
            def _(sp):
                for n, name in enumerate(("src_pt", "dstg_pt", "dst_pt", "dnext_pt")):
                    sp.dma_start(pt[:, n, :], a[name]).then_inc(loaded, 16)
                for n, name in enumerate(("dst_rows", "dprev_rows", "dnext_rows")):
                    sp.dma_start(rows[:, n, :, :], a[name]).then_inc(loaded, 16)
                sp.wait_ge(made, 1)
                for g in range(RG):
                    sp.dma_start(m["cont_row"].rearrange("(g t p) -> g t p", g=RG, p=P)[g], controw[:, g, :]).then_inc(stored, 16)
                sp.wait_ge(stored, 16 * RG)

            @block.gpsimd
            def _(pool):
                step = in_order(pool, pv)
                step(nc.gpsimd.memset(ident[:, :], 0.0))
                step(nc.gpsimd.affine_select(out=ident[:, :], in_=ident[:, :], compare_op=ALU.not_equal, fill=1.0,
                                             base=0, pattern=[[-1, P]], channel_multiplier=1))

            @block.vector
            def _(dve):
                step = in_order(dve, dv)
                dve.wait_ge(loaded, 16 * 7)
                nc.vector.tensor_copy(m["gidx"][:, :, 0], pt[:, 0, :])
                nc.vector.tensor_copy(m["gidx"][:, :, 1], pt[:, 1, :])
                step(nc.vector.tensor_copy(ptf[:, 0:2, :], pt[:, 2:4, :]))
                step(nc.vector.tensor_tensor(ptf[:, 2, :], ptf[:, 0, :], ptf[:, 1, :], ALU.is_equal))
                step(nc.vector.scalar_tensor_tensor(ptf[:, 1, :], ptf[:, 2, :], float(FAR), ptf[:, 0, :], ALU.mult, ALU.add))
                step(nc.vector.tensor_copy(m["sidx"][:, :], ptf[:, 1, :]))
                step(nc.vector.tensor_copy(rowf[:, :, :, :], rows[:, :, :, :]))
                step(nc.vector.tensor_tensor(cont[:, 0], rowf[:, 0], rowf[:, 1], ALU.is_equal))
                step(nc.vector.tensor_tensor(cont[:, 1], rowf[:, 0], rowf[:, 2], ALU.is_equal))
                nc.vector.tensor_copy(controw[:, :, :], cont[:, 0]).then_inc(made, 1)
                step(nc.vector.tensor_copy(cont[:, 2:4], cont[:, 0:2]))
                step(nc.vector.memset(cont[:, 2, :, 0:1], 0.0))
                step(nc.vector.memset(cont[:, 3, :, P - 1:P], 0.0))
                step(nc.vector.memset(edgeF[:, :, :], 0.0))
                step(nc.vector.memset(edgeB[:, :, :], 0.0))
                step(nc.vector.tensor_copy(edgeF[:, :, 0:1], cont[:, 0, :, 0:1]))
                step(nc.vector.tensor_copy(edgeB[:, :, P - 1:P], cont[:, 1, :, P - 1:P]))
                flat = lambda t: t.rearrange("t g p -> t (g p)")
                step(nc.vector.tensor_tensor_scan(flat(m["inF"][:, :, :]), flat(cont[:, 2]), flat(edgeF[:, :, :]),
                                                  0.0, ALU.mult, ALU.add))
                step(nc.vector.tensor_tensor_scan(flat(m["inB"][:, :, :])[:, ::-1], flat(cont[:, 3])[:, ::-1],
                                                  flat(edgeB[:, :, :])[:, ::-1], 0.0, ALU.mult, ALU.add))
                for to, of in (("nInF", m["inF"]), ("nInB", m["inB"])):
                    step(nc.vector.tensor_scalar(m[to][:, :, :], of[:, :, :], -1.0, BIG, ALU.add, ALU.mult))
                for n, (c, neg) in enumerate((("cF", "nF"), ("cB", "nB"))):
                    for h in range(H):
                        step(nc.vector.tensor_copy(m[c][:, :, h, :], cont[:, 2 + n]))
                    step(nc.vector.tensor_scalar(m[neg][:, :, :, :], m[c][:, :, :, :], -1.0, BIG, ALU.add, ALU.mult))
                step(nc.vector.tensor_copy(wcol[:, 0], m["inF"][:, :, P - 1:P].to_broadcast([RT, RG, H])))
                nc.vector.tensor_copy(wcol[:, 1], m["inB"][:, :, 0:1].to_broadcast([RT, RG, H])).then_inc(tr, 1)
                dve.wait_ge(tc, 1)
                step(nc.vector.tensor_copy(m["wF"][:, :], bank[0:H, 0:TILES]))
                step(nc.vector.tensor_copy(m["wB"][:, :], bank[0:H, TILES:2 * TILES]))
                step(nc.vector.tensor_scalar(m["nWF"][:, :], m["wF"][:, :], -1.0, BIG, ALU.add, ALU.mult))
                step(nc.vector.tensor_scalar(m["nWB"][:, :], m["wB"][:, :], -1.0, BIG, ALU.add, ALU.mult))

            @block.tensor
            def _(pe):
                pe.wait_ge(pv, 2)
                pe.wait_ge(tr, 1)
                for n in range(2):
                    for g in range(RG):
                        at = n * TILES + g * RT
                        last = nc.tensor.transpose(bank[0:H, at:at + RT], wcol[:, n, g, :], ident[0:RT, 0:RT])
                last.then_inc(tc, 1)


def dense_norm(nc, m, stage, sources, sum_table, table, stats):
    with ExitStack() as ctx:
        def bufs(name, *shape):
            return [ctx.enter_context(nc.sbuf_tensor(f"{stage}_{name}{k}", [P, *shape], F32)) for k in range(2)]

        n_in = len(sources)
        X, CEN, SQ, HN, OUT = [bufs(n, SUP, C) for n in ("sum", "centred", "squares", "scaled", "out")]
        MORE = [bufs(f"more{q}", SUP, C) for q in range(1, n_in)]
        R = bufs("rows", 4, SUP)
        added, meaned, centred, squared, varied, rooted, inverted, scaled, normed, turned, counted, begun = sems(
            ctx, nc, stage, "added", "meaned", "centred", "squared", "varied", "rooted", "inverted", "scaled", "normed", "turned", "counted", "begun")
        loaded, stored, sum_stored = [pair(ctx, nc, stage, n) for n in ("loaded", "stored", "sum_stored")]
        banks = m["bank"]
        NB = SUP // SUB
        USES = 2 * NB

        def shape(tail):
            return (TAIL, 1) if tail else (P, SUP)

        def of(table, start, tail):
            if tail:
                return table[P * GRID:N, :].rearrange("(p t) c -> p t c", t=1)
            return grid_view(table)[:, bass.ds(start, SUP), :]

        with nc.Block() as block:

            @block.sync
            def _(sp):
                def load(i, k, tail=False):
                    p, t = shape(tail)
                    start = start_of(sp, i, k, SUP)
                    sp.wait_ge(centred, 2 * i + k + 1)
                    if sum_table is not None and later(i):
                        sp.sem_inc(begun, 1)
                        sp.wait_ge(sum_stored[k], 16 * i)
                    for q, source in enumerate(sources):
                        to = X[k] if q == 0 else MORE[q - 1][k]
                        sp.dma_start(to[0:p, 0:t, :], of(source, start, tail)).then_inc(loaded[k], 16)

                two_by_two(sp, NSUP, load, tail=True, peel=True)
                for k in range(2):
                    sp.wait_ge(stored[k], 16 * (NSUP // 2 + 1))
                    if sum_table is not None:
                        sp.wait_ge(sum_stored[k], 16 * (NSUP // 2 + 1))

            @block.vector
            def _(dve):
                dve.sem_inc(counted, USES)

                def mean(i, k, tail=False):
                    p, t = shape(tail)
                    s = 2 * i + k
                    x, r = X[k][0:p, 0:t, :], R[k]
                    dve.wait_ge(loaded[k], 16 * n_in * (i + 1))
                    for q in range(1, n_in):
                        nc.vector.tensor_tensor(x, x, MORE[q - 1][k][0:p, 0:t, :], ALU.add).then_inc(added, 1)
                        dve.wait_ge(added, (n_in - 1) * s + q)
                    dve.wait_ge(scaled, s + 1)
                    nc.vector.tensor_reduce(r[0:p, 0, 0:t], x, AX, ALU.add).then_inc(meaned, 1)
                    dve.wait_ge(meaned, 2 * s + 1)
                    nc.vector.tensor_scalar(r[0:p, 1, 0:t], r[0:p, 0, 0:t], -1.0 / C, None, ALU.mult).then_inc(meaned, 1)

                def variance(i, k, tail=False):
                    p, t = shape(tail)
                    s = 2 * i + k
                    r = R[k]
                    dve.wait_ge(squared, s + 1)
                    nc.vector.tensor_reduce(r[0:p, 2, 0:t], SQ[k][0:p, 0:t, :], AX, ALU.add).then_inc(varied, 1)
                    dve.wait_ge(varied, 2 * s + 1)
                    nc.vector.tensor_scalar(r[0:p, 2, 0:t], r[0:p, 2, 0:t], 1.0 / C, EPS, ALU.mult, ALU.add).then_inc(varied, 1)

                def invert(i, k, tail=False):
                    p, t = shape(tail)
                    s = 2 * i + k
                    dve.wait_ge(rooted, s + 1)
                    nc.vector.reciprocal(R[k][0:p, 3, 0:t], R[k][0:p, 3, 0:t]).then_inc(inverted, 1)

                def count(i, k, tail=False):
                    for q in range(1 if tail else NB):
                        u = k * NB + q
                        dve.wait_ge(turned, USES * i + u + 1)
                        if tail:
                            nc.vector.bn_stats(m["stats"][0:C, 2 * NSUB, :], banks[u % 8][0:C, 0:TAIL]).then_inc(counted, 1)
                        else:
                            nc.vector.bn_stats(m["stats"][:, bass.ds((2 * i + k) * NB + q, 1), :],
                                               banks[u % 8][:, 0:SUB // 2 * P]).then_inc(counted, 1)

                two_by_two(dve, NSUP, mean, variance, invert, *([count] if stats else []), tail=True)

            @block.gpsimd
            def _(pool):
                pool.sem_inc(centred, 2)
                pool.sem_inc(scaled, 2)

                def centre(i, k, tail=False):
                    p, t = shape(tail)
                    s = 2 * i + k
                    pool.wait_ge(meaned, 2 * s + 2)
                    pool.wait_ge(scaled, s + 1)
                    nc.gpsimd.tensor_tensor(CEN[k][0:p, 0:t, :], X[k][0:p, 0:t, :],
                                            R[k][0:p, 1, 0:t].unsqueeze(2).to_broadcast([p, t, C]), ALU.add).then_inc(centred, 1)

                def scale(i, k, tail=False):
                    p, t = shape(tail)
                    s = 2 * i + k
                    pool.wait_ge(centred, s + 3)
                    pool.wait_ge(inverted, s + 1)
                    pool.wait_ge(normed, s + 1)
                    nc.gpsimd.tensor_tensor(HN[k][0:p, 0:t, :], CEN[k][0:p, 0:t, :],
                                            R[k][0:p, 3, 0:t].unsqueeze(2).to_broadcast([p, t, C]), ALU.mult).then_inc(scaled, 1)

                two_by_two(pool, NSUP, centre, scale, tail=True)

            @block.scalar
            def _(act):
                act.sem_inc(normed, 2)

                def square(i, k, tail=False):
                    p, t = shape(tail)
                    s = 2 * i + k
                    start = start_of(act, i, k, SUP)
                    act.wait_ge(centred, s + 3)
                    nc.scalar.activation(SQ[k][0:p, 0:t, :], CEN[k][0:p, 0:t, :], ACT.Square).then_inc(squared, 1)
                    if sum_table is not None:
                        act.dma_start(of(sum_table, start, tail), X[k][0:p, 0:t, :]).then_inc(sum_stored[k], 16)

                def root(i, k, tail=False):
                    p, t = shape(tail)
                    s = 2 * i + k
                    act.wait_ge(varied, 2 * s + 2)
                    nc.scalar.activation(R[k][0:p, 3, 0:t], R[k][0:p, 2, 0:t], ACT.Sqrt).then_inc(rooted, 1)

                def rectify(i, k, tail=False):
                    p, t = shape(tail)
                    s = 2 * i + k
                    start = start_of(act, i, k, SUP)
                    act.wait_ge(scaled, s + 3)
                    if later(i):
                        act.wait_ge(stored[k], 16 * i)
                    if stats:
                        act.wait_ge(counted, USES * i + NB * (k + 1))
                    nc.scalar.activation(OUT[k][0:p, 0:t, :], HN[k][0:p, 0:t, :], ACT.Relu).then_inc(normed, 1)
                    act.wait_ge(normed, s + 3)
                    act.dma_start(of(table, start, tail), OUT[k][0:p, 0:t, :]).then_inc(stored[k], 16)

                two_by_two(act, NSUP, square, root, rectify, tail=True, peel=True)

            @block.tensor
            def _(pe):
                def turn(i, k, tail=False):
                    pe.wait_ge(normed, 2 * i + k + 3)
                    for q in range(1 if tail else NB):
                        u = k * NB + q
                        before = u - 8 if u >= 8 else u + 8 - USES if u + 8 < USES else u - USES
                        pe.wait_ge(counted, USES * i + before + 1 + USES)
                        if tail:
                            last = nc.tensor.transpose(banks[u % 8][0:C, 0:TAIL], OUT[k][0:TAIL, 0, :], m["ident"][0:TAIL, 0:TAIL])
                        for j in range(0 if tail else SUB // 2):
                            two = OUT[k][:, q * SUB + 2 * j:q * SUB + 2 * j + 2, :].rearrange("p t c -> p (t c)")
                            last = nc.tensor.transpose(banks[u % 8][:, j * P:(j + 1) * P], two, m["ident"][:, :])
                        last.then_inc(turned, 1)

                if stats:
                    two_by_two(pe, NSUP, turn, tail=True)


def table_stats(nc, m, b):
    stage = f"ts{b}"
    table = m["T"][b]
    with ExitStack() as ctx:
        X = [ctx.enter_context(nc.sbuf_tensor(f"{stage}_rows{k}", [P, SUP, C], F32)) for k in range(2)]
        loaded = pair(ctx, nc, stage, "loaded")
        turned, counted = sems(ctx, nc, stage, "turned", "counted")
        banks = m["bank"]
        NB = SUP // SUB
        USES = 2 * NB
        with nc.Block() as block:

            @block.sync
            def _(sp):
                def load(i, k, tail=False):
                    start = start_of(sp, i, k, SUP)
                    sp.wait_ge(counted, USES * i + k * NB + NB)
                    if tail:
                        sp.dma_start(X[k][0:TAIL, 0, :], table[P * GRID:N, :]).then_inc(loaded[k], 16)
                    else:
                        sp.dma_start(X[k][:, :, :], grid_view(table)[:, bass.ds(start, SUP), :]).then_inc(loaded[k], 16)

                two_by_two(sp, NSUP, load, tail=True)

            @block.tensor
            def _(pe):
                def turn(i, k, tail=False):
                    pe.wait_ge(loaded[k], 16 * i + 16)
                    for q in range(1 if tail else NB):
                        u = k * NB + q
                        before = u - 8 if u >= 8 else u + 8 - USES if u + 8 < USES else u - USES
                        pe.wait_ge(counted, USES * i + before + 1 + USES)
                        if tail:
                            last = nc.tensor.transpose(banks[u % 8][0:C, 0:TAIL], X[k][0:TAIL, 0, :], m["ident"][0:TAIL, 0:TAIL])
                        for j in range(0 if tail else SUB // 2):
                            two = X[k][:, q * SUB + 2 * j:q * SUB + 2 * j + 2, :].rearrange("p t c -> p (t c)")
                            last = nc.tensor.transpose(banks[u % 8][:, j * P:(j + 1) * P], two, m["ident"][:, :])
                        last.then_inc(turned, 1)

                two_by_two(pe, NSUP, turn, tail=True)

            @block.vector
            def _(dve):
                dve.sem_inc(counted, USES)

                def count(i, k, tail=False):
                    for q in range(1 if tail else NB):
                        u = k * NB + q
                        dve.wait_ge(turned, USES * i + u + 1)
                        if tail:
                            nc.vector.bn_stats(m["stats"][0:C, 2 * NSUB, :], banks[u % 8][0:C, 0:TAIL]).then_inc(counted, 1)
                        else:
                            nc.vector.bn_stats(m["stats"][:, bass.ds((2 * i + k) * NB + q, 1), :],
                                               banks[u % 8][:, 0:SUB // 2 * P]).then_inc(counted, 1)

                two_by_two(dve, NSUP, count, tail=True)


def norm_coefficients(nc, m, stage, weight, bias, mean_scale, chunks=None):
    with ExitStack() as ctx:
        moved, loaded, varied, rooted, made, spread, dv = sems(
            ctx, nc, stage, "moved", "loaded", "varied", "rooted", "made", "spread", "dve_chain")
        v = m["small"]
        stats, AB = m["stats"], m["AB"]
        with nc.Block() as block:

            @block.sync
            def _(sp):
                sp.dma_start(v[:, 2:3], weight.rearrange("a c -> c a")).then_inc(loaded, 16)
                sp.dma_start(v[:, 3:4], bias.rearrange("a c -> c a")).then_inc(loaded, 16)
                if mean_scale is not None:
                    sp.dma_start(v[:, 4:5], mean_scale.rearrange("a c -> c a")).then_inc(loaded, 16)
                if chunks is None:
                    sp.dma_start(stats[0:C, NSUB:2 * NSUB, :], stats[C:P, 0:NSUB, :]).then_inc(moved, 16)
                sp.wait_ge(made, 1)
                sp.dma_start(AB[C:P, :], AB[0:C, :]).then_inc(spread, 16)
                sp.wait_ge(spread, 16)

            @block.scalar
            def _(act):
                act.wait_ge(varied, 1)
                nc.scalar.activation(v[:, 7:8], v[:, 6:7], ACT.Sqrt).then_inc(rooted, 1)

            @block.vector
            def _(dve):
                step = in_order(dve, dv)
                if chunks is None:
                    dve.wait_ge(moved, 16)
                step(nc.vector.bn_aggr(v[:, 0:2], stats[0:C, 0:chunks or 2 * NSUB + 1, :].rearrange("c n s -> c (n s)")))
                dve.wait_ge(loaded, 16 * (2 if mean_scale is None else 3))
                mean, var, w, b, scaled, t = (v[:, n:n + 1] for n in (0, 1, 2, 3, 5, 6))
                if mean_scale is None:
                    step(nc.vector.tensor_copy(scaled, mean))
                else:
                    step(nc.vector.tensor_tensor(scaled, mean, v[:, 4:5], ALU.mult))
                    step(nc.vector.tensor_tensor(t, mean, scaled, ALU.subtract))
                    step(nc.vector.tensor_tensor(t, t, t, ALU.mult))
                    step(nc.vector.tensor_tensor(var, var, t, ALU.add))
                nc.vector.tensor_scalar(t, var, EPS, None, ALU.add).then_inc(varied, 1)
                dve.wait_ge(rooted, 1)
                step(nc.vector.reciprocal(t, v[:, 7:8]))
                step(nc.vector.tensor_tensor(AB[0:C, 0:1], t, w, ALU.mult))
                step(nc.vector.tensor_tensor(t, scaled, AB[0:C, 0:1], ALU.mult))
                nc.vector.tensor_tensor(AB[0:C, 1:2], b, t, ALU.subtract).then_inc(made, 1)


def gat_weights(nc, a, m, b, keep):
    stage = f"gw{b}"
    with ExitStack() as ctx:
        def kept(name, shape):
            m[name] = keep.enter_context(nc.sbuf_tensor(f"{stage}_{name}", shape, F32))
            return m[name]

        def tmp(name, shape):
            return ctx.enter_context(nc.sbuf_tensor(f"{stage}_{name}", shape, F32))

        wsd = kept("wsd", [P, H * C])
        wself = kept("wself", [P, H * C])
        we = kept("we", [DE + 1, H * C])
        att = kept("att", [P, 2, 2 * H])
        atts = kept("atts", [P, 2, 2 * H])
        lin = kept("lin", [P, 2 * H])
        line = kept("line", [DE + 1, 2 * H])
        eem = kept("eem", [P, 2])
        wout = kept("wout", [P, 2, C])
        wmean = kept("wmean", [P, P])
        diff = kept("diff", [P, P])
        heads = kept("heads", [H, 2, P])
        biasb = kept("biasb", [P, C])
        wl2 = tmp("wl2", [P, H * C])
        attc = tmp("attc", [P, 2, H])
        eseg = tmp("eseg", [P, E // 8])
        esum = tmp("esum", [P, 1])
        wes = tmp("wes", [P, H * C])
        wT = tmp("wT", [P, 2, 2, P])
        weT = tmp("weT", [P, 2, DE + 1])
        emT = tmp("emT", [P, 2, DE + 1])
        headsT = tmp("headsT", [P, 2, H])
        zeroed, loaded, dv, ready, turned, back, folded, pv = sems(
            ctx, nc, stage, "zeroed", "loaded", "dve_chain", "ready", "turned", "back", "folded", "pool_chain")
        Wl, Wr, We, attd = (a[n] for n in ("Wl", "Wr", "We", "att"))
        banks = m["bank"]
        ident = m["ident"]
        with nc.Block() as block:

            @block.gpsimd
            def _(pool):
                for t in (wself[:, :], we[:, :], attc[:, :, :], wmean[:, :], att[:, :, :], atts[:, :, :],
                          emT[:, :, :], weT[:, :, :], headsT[:, :, :], lin[:, :]):
                    nc.gpsimd.memset(t, 0.0).then_inc(zeroed, 1)

            @block.sync
            def _(sp):
                sp.wait_ge(zeroed, 10)
                n = 0
                for to, of in ((wsd[0:C, :], Wl[b]), (wsd[C:P, :], Wr[b]), (we[1:DE + 1, :], We[b]), (wl2[0:C, :], Wl[b]),
                               (wl2[C:P, :], Wl[b]), (biasb[:, :], a["gat_bias"][b, :].partition_broadcast(P))):
                    sp.dma_start(to, of).then_inc(loaded, 16)
                    n += 1
                for h in range(H):
                    at = (h % 2) * C
                    sp.dma_start(attc[at:at + C, h // 2, h:h + 1], attd[b, h:h + 1, :].rearrange("a c -> c a")).then_inc(loaded, 16)
                    sp.dma_start(wout[at:at + C, h // 2, :], Wl[b, :, h * C:(h + 1) * C]).then_inc(loaded, 16)
                    n += 2
                for s in range(8):
                    sp.dma_start(eseg[s * DE:(s + 1) * DE, :], a["ea16T"][1:DE + 1, s * (E // 8):(s + 1) * (E // 8)]).then_inc(loaded, 16)
                    sp.dma_start(wes[s * DE:(s + 1) * DE, :], We[b]).then_inc(loaded, 16)
                    n += 2
                assert n == 30

            @block.vector
            def _(dve):
                step = in_order(dve, dv)
                dve.wait_ge(loaded, 16 * 30)
                step(nc.vector.tensor_tensor(wself[C:P, :], wsd[C:P, :], wl2[C:P, :], ALU.add))
                for at in (0, C):
                    r = slice(at, at + C)
                    to = wmean[r, at:at + C]
                    step(nc.vector.tensor_tensor(to, wl2[r, 0:C], wl2[r, C:2 * C], ALU.add))
                    for h in range(2, H):
                        step(nc.vector.tensor_tensor(to, to, wl2[r, h * C:(h + 1) * C], ALU.add))
                    step(nc.vector.tensor_scalar(to, to, 1.0 / H, None, ALU.mult))
                step(nc.vector.tensor_scalar(wout[:, :, :], wout[:, :, :], 1.0 / H, None, ALU.mult))
                step(nc.vector.tensor_scalar(att[:, :, 0:H], attc[:, :, :], 1.0 - SLOPE, None, ALU.mult))
                step(nc.vector.tensor_scalar(atts[:, :, H:2 * H], attc[:, :, :], 1.0 - SLOPE, None, ALU.mult))
                step(nc.vector.tensor_scalar(attc[:, :, :], attc[:, :, :], SLOPE, None, ALU.mult))
                for at in (0, C):
                    step(nc.vector.tensor_copy(diff[0:C, at:at + C], ident[0:C, 0:C]))
                    step(nc.vector.tensor_scalar(diff[C:P, at:at + C], ident[C:P, C:P], -1.0, None, ALU.mult))
                for f in range(2):
                    for e in range(2):
                        step(nc.vector.memset(headsT[e * C:(e + 1) * C, f, 2 * f + e:2 * f + e + 1], 1.0))
                step(nc.vector.tensor_reduce(esum[:, :], eseg[:, :], AX, ALU.add))
                nc.vector.tensor_scalar(esum[:, :], esum[:, :], 1.0 / E, None, ALU.mult).then_inc(ready, 1)
                dve.wait_ge(turned, 1)
                for n in range(2):
                    step(nc.vector.tensor_copy(wT[:, n, :, :].rearrange("p f c -> p (f c)"), banks[n][:, 0:2 * P]))
                for f in range(2):
                    step(nc.vector.tensor_copy(weT[:, f, :], banks[2][:, f * 32:f * 32 + DE + 1]))
                    step(nc.vector.tensor_copy(eem[:, f:f + 1], banks[3][:, f:f + 1]))
                    step(nc.vector.tensor_copy(emT[:, f, 0:1], eem[:, f:f + 1]))
                    last = nc.vector.tensor_copy(heads[:, f, :], banks[4][0:H, f * P:(f + 1) * P])
                last.then_inc(back, 1)
                dve.wait_ge(folded, 1)
                step(nc.vector.tensor_copy(lin[:, :], banks[5][:, 0:2 * H]))
                step(nc.vector.tensor_copy(line[:, :], banks[6][0:DE + 1, 0:2 * H]))

            @block.tensor
            def _(pe):
                pe.wait_ge(ready, 1)
                for f in range(2):
                    nc.tensor.transpose(banks[0][:, f * P:(f + 1) * P], wsd[:, f * P:(f + 1) * P], ident[:, :])
                    nc.tensor.transpose(banks[1][:, f * P:(f + 1) * P], wself[:, f * P:(f + 1) * P], ident[:, :])
                    nc.tensor.transpose(banks[2][:, f * 32:f * 32 + DE + 1], we[:, f * P:(f + 1) * P], ident[0:DE + 1, 0:DE + 1])
                    nc.tensor.matmul(banks[3][:, f:f + 1], wes[:, f * P:(f + 1) * P], esum[:, :], start=True, stop=True)
                    last = nc.tensor.transpose(banks[4][0:H, f * P:(f + 1) * P], headsT[:, f, :], ident[:, :])
                last.then_inc(turned, 1)
                pe.wait_ge(back, 1)
                for n in range(2):
                    for f in range(2):
                        nc.tensor.matmul(banks[5][:, n * H:(n + 1) * H], wT[:, n, f, :], attc[:, f, :], start=f == 0, stop=f == 1)
                for n, t in enumerate((weT, emT)):
                    for f in range(2):
                        last = nc.tensor.matmul(banks[6][0:DE + 1, n * H:(n + 1) * H], t[:, f, :], attc[:, f, :],
                                                start=f == 0, stop=f == 1)
                last.then_inc(folded, 1)


def gat_base(nc, m, b):
    stage = f"gb{b}"
    source, table = m["T"][b], m["T"][b + 1]
    with ExitStack() as ctx:
        X = [ctx.enter_context(nc.sbuf_tensor(f"{stage}_rows{k}", [P, SUP, C], F32)) for k in range(2)]
        Y = [ctx.enter_context(nc.sbuf_tensor(f"{stage}_next{k}", [P, SUP, C], F32)) for k in range(2)]
        HC = [ctx.enter_context(nc.sbuf_tensor(f"{stage}_hidden{k}", [P, SUB // 2 * P], F32)) for k in range(4)]
        loaded, stored = pair(ctx, nc, stage, "loaded"), pair(ctx, nc, stage, "stored")
        turned, hidden, mixed, out = sems(ctx, nc, stage, "turned", "hidden", "mixed", "out")
        banks, AB = m["bank"], m["AB"]
        NB = SUP // SUB
        USES = 2 * NB
        W = SUB // 2 * P

        def before(u, ring):
            return u - ring if u >= ring else u % ring + (USES - 1 - u % ring) // ring * ring - USES

        with nc.Block() as block:

            @block.sync
            def _(sp):
                def load(i, k, tail=False):
                    start = start_of(sp, i, k, SUP)
                    sp.wait_ge(hidden, USES * i + k * NB + NB)
                    if tail:
                        sp.dma_start(X[k][0:TAIL, 0, :], source[P * GRID:N, :]).then_inc(loaded[k], 16)
                    else:
                        sp.dma_start(X[k][:, :, :], grid_view(source)[:, bass.ds(start, SUP), :]).then_inc(loaded[k], 16)

                two_by_two(sp, NSUP, load, tail=True)

            @block.tensor
            def _(pe):
                pe.sem_inc(mixed, USES)

                def turn(i, k, q, tail):
                    u = k * NB + q
                    if q == 0:
                        pe.wait_ge(loaded[k], 16 * i + 16)
                    pe.wait_ge(hidden, USES * i + before(u, 4) + 1 + USES)
                    if tail:
                        last = nc.tensor.transpose(banks[u % 4][0:C, 0:TAIL], X[k][0:TAIL, 0, :], m["ident"][0:TAIL, 0:TAIL])
                    for j in range(0 if tail else SUB // 2):
                        two = X[k][:, q * SUB + 2 * j:q * SUB + 2 * j + 2, :].rearrange("p t c -> p (t c)")
                        last = nc.tensor.transpose(banks[u % 4][:, j * P:(j + 1) * P], two, m["ident"][:, :])
                    last.then_inc(turned, 1)

                def mix(i, k, q, tail):
                    u = k * NB + q
                    pe.wait_ge(hidden, USES * i + u + 1 + USES)
                    pe.wait_ge(out, USES * i + before(u, 4) + 1 + USES)
                    if tail:
                        last = nc.tensor.matmul(banks[4 + u % 4][0:TAIL, 0:C], HC[u % 4][0:C, 0:TAIL], m["wmean"][0:C, 0:C],
                                                start=True, stop=True)
                    for j in range(0 if tail else SUB // 2):
                        last = nc.tensor.matmul(banks[4 + u % 4][:, j * P:(j + 1) * P], HC[u % 4][:, j * P:(j + 1) * P],
                                                m["wmean"][:, :], start=True, stop=True)
                    last.then_inc(mixed, 1)

                def step(i, k, tail=False):
                    n = 1 if tail else NB
                    for q in range(n + 2):
                        if q < n:
                            turn(i, k, q, tail)
                        if q >= 2:
                            mix(i, k, q - 2, tail)

                two_by_two(pe, NSUP, step, tail=True)

            @block.scalar
            def _(act):
                act.sem_inc(hidden, USES)

                def step(i, k, tail=False):
                    for q in range(1 if tail else NB):
                        u = k * NB + q
                        act.wait_ge(turned, USES * i + u + 1)
                        act.wait_ge(mixed, USES * i + before(u, 4) + 1 + USES)
                        p, w = (C, TAIL) if tail else (P, W)
                        nc.scalar.activation(HC[u % 4][0:p, 0:w], banks[u % 4][0:p, 0:w], ACT.Relu, bias=AB[0:p, 1:2],
                                             scale=AB[0:p, 0:1]).then_inc(hidden, 1)

                two_by_two(act, NSUP, step, tail=True)

            @block.vector
            def _(dve):
                dve.sem_inc(out, USES)

                def step(i, k, tail=False):
                    if later(i):
                        dve.wait_ge(stored[k], 16 * i)
                    for q in range(1 if tail else NB):
                        u = k * NB + q
                        dve.wait_ge(mixed, USES * i + u + 1 + USES)
                        p, t = (TAIL, 1) if tail else (P, SUB)
                        nc.vector.tensor_tensor(
                            Y[k][0:p, q * SUB:q * SUB + t, :], banks[4 + u % 4][0:p, 0:t * C].rearrange("p (t c) -> p t c", c=C),
                            m["biasb"][0:p, :].unsqueeze(1).to_broadcast([p, t, C]), ALU.add).then_inc(out, 1)

                two_by_two(dve, NSUP, step, tail=True, peel=True)

            @block.gpsimd
            def _(pool):
                def store(i, k, tail=False):
                    n = 1 if tail else NB
                    start = start_of(pool, i, k, SUP)
                    pool.wait_ge(out, USES * i + k * NB + n + USES)
                    if tail:
                        pool.dma_start(table[P * GRID:N, :], Y[k][0:TAIL, 0, :]).then_inc(stored[k], 16)
                    else:
                        pool.dma_start(grid_view(table)[:, bass.ds(start, SUP), :], Y[k][:, :, :]).then_inc(stored[k], 16)

                two_by_two(pool, NSUP, store, tail=True)
                for k in range(2):
                    pool.wait_ge(stored[k], 16 * (NSUP // 2 + 1))


def gat_logits(nc, a, m, b):
    stage = f"gl{b}"
    table = m["T"][b]
    with ExitStack() as ctx:
        def bufs(name, *shape, dt=F32):
            return [ctx.enter_context(nc.sbuf_tensor(f"{stage}_{name}{k}", list(shape), dt)) for k in range(2)]

        G = bufs("gathered", P, CT, P)
        IDX = bufs("idx", P, CT, 2, dt=I32)
        HC = bufs("hidden", P, CH)
        EA = bufs("attributes", DE + 1, CH)
        RE = bufs("relu_edge", P, 2, CH)
        RS = bufs("relu_self", P, 2, CH)
        gathered, loaded = pair(ctx, nc, stage, "gathered"), pair(ctx, nc, stage, "loaded")
        picked, begun, turned, hidden, saved, ze, zs, re, rs, logit, kept = sems(
            ctx, nc, stage, "picked", "begun", "turned", "hidden", "saved", "z_edge", "z_self", "relu_edge", "relu_self",
            "logits", "kept")
        banks, AB = m["bank"], m["AB"]
        with nc.Block() as block:

            @block.gpsimd
            def _(pool):
                def gather(i, k):
                    c = 2 * i + k
                    pool.wait_ge(turned, c + 1)
                    nc.gpsimd.tensor_copy(IDX[k][:, :, :], m["gidx"][:, bass.ds(c * CT, CT), :]).then_inc(picked, 1)
                    pool.wait_ge(picked, c + 1)
                    pool.sem_inc(begun, 1)
                    for j in range(CT):
                        for side in range(2):
                            pool.indirect_dma_start(G[k][:, j, side * C:(side + 1) * C], None, table[:, :],
                                                    bass.IndirectOffsetOnAxis(ap=IDX[k][:, j, side:side + 1], axis=0)
                                                    ).then_inc(gathered[k], 16)

                two_by_two(pool, NCH, gather)

            @block.sync
            def _(sp):
                def load(i, k):
                    start = start_of(sp, i, k, CH)
                    sp.wait_ge(logit, 2 * i + k + 1)
                    sp.dma_start(EA[k][:, :], a["ea16T"][:, bass.ds(start, CH)]).then_inc(loaded[k], 16)

                two_by_two(sp, NCH, load)

            @block.tensor
            def _(pe):
                pe.sem_inc(turned, 2)
                pe.sem_inc(logit, 2)

                def turn(i, k):
                    pe.wait_ge(gathered[k], 16 * 2 * CT * (i + 1))
                    pe.wait_ge(saved, 2 * i + k + 1)
                    for j in range(CT):
                        last = nc.tensor.transpose(banks[k][:, j * P:(j + 1) * P], G[k][:, j, :], m["ident"][:, :])
                    last.then_inc(turned, 1)

                def project(i, k):
                    c = 2 * i + k
                    pe.wait_ge(hidden, c + 1)
                    pe.wait_ge(loaded[k], 16 * i + 16)
                    for f in range(2):
                        w = slice(f * P, (f + 1) * P)
                        pe.wait_ge(re, 2 * c + f + 1)
                        nc.tensor.matmul(banks[2 + f][:, :], m["wsd"][:, w], HC[k][:, :], start=True, stop=False)
                        nc.tensor.matmul(banks[2 + f][:, :], m["we"][:, w], EA[k][:, :], start=False, stop=True).then_inc(ze, 1)
                        pe.wait_ge(rs, 2 * c + f + 1)
                        nc.tensor.matmul(banks[4 + f][:, :], m["wself"][:, w], HC[k][:, :], start=True, stop=True).then_inc(zs, 1)

                def logits(i, k):
                    c = 2 * i + k
                    pe.wait_ge(re, 2 * c + 4)
                    pe.wait_ge(rs, 2 * c + 4)
                    pe.wait_ge(kept, c + 1)
                    for j in range(CT):
                        t = slice(j * P, (j + 1) * P)
                        parts = [(HC[k][:, t], m["lin"][:, :]), (EA[k][:, t], m["line"][:, :])]
                        parts += [(RE[k][:, f, t], m["att"][:, f, :]) for f in range(2)]
                        parts += [(RS[k][:, f, t], m["atts"][:, f, :]) for f in range(2)]
                        for n, (left, right) in enumerate(parts):
                            last = nc.tensor.matmul(banks[6 + k][:, j * 2 * H:(j + 1) * 2 * H], left, right,
                                                    start=n == 0, stop=n == len(parts) - 1)
                    last.then_inc(logit, 1)

                def step(i, first=False, last=False):
                    project(i, 0)
                    if not first:
                        logits(i - 1, 1)
                    project(i, 1)
                    logits(i, 0)
                    if not last:
                        for k in range(2):
                            turn(i + 1, k)

                for k in range(2):
                    turn(0, k)
                step(0, first=True)
                with pe.Fori(1, NCH // 2 - 1) as i:
                    step(i)
                step(NCH // 2 - 1, last=True)
                logits(NCH // 2 - 1, 1)

            @block.scalar
            def _(act):
                act.sem_inc(saved, 2)
                act.sem_inc(re, 2)

                def hide(i, k):
                    c = 2 * i + k
                    act.wait_ge(turned, c + 3)
                    act.wait_ge(logit, c + 1)
                    nc.scalar.activation(HC[k][:, :], banks[k][:, :], ACT.Relu, bias=AB[:, 1:2], scale=AB[:, 0:1]).then_inc(hidden, 1)
                    nc.scalar.activation(m["HT"][:, bass.ds(c * CH, CH)], banks[k][:, :], ACT.Relu, bias=AB[:, 1:2],
                                         scale=AB[:, 0:1]).then_inc(saved, 1)

                def rectify(i, k):
                    c = 2 * i + k
                    for f in range(2):
                        act.wait_ge(ze, 2 * c + f + 1)
                        nc.scalar.activation(RE[k][:, f, :], banks[2 + f][:, :], ACT.Relu).then_inc(re, 1)

                two_by_two(act, NCH, hide, rectify)

            @block.vector
            def _(dve):
                dve.sem_inc(rs, 2)
                dve.sem_inc(kept, 2)

                def rectify(i, k):
                    c = 2 * i + k
                    dve.wait_ge(logit, c + 1)
                    for f in range(2):
                        dve.wait_ge(zs, 2 * c + f + 1)
                        nc.vector.tensor_scalar(RS[k][:, f, :], banks[4 + f][:, :], m["eem"][:, f:f + 1], 0.0,
                                                ALU.add, ALU.max).then_inc(rs, 1)

                def keep(i, k):
                    c = 2 * i + k
                    dve.wait_ge(logit, c + 3)
                    nc.vector.tensor_copy(m["logits"][:, bass.ds(c * CT, CT), :],
                                          banks[6 + k][:, 0:CT * 2 * H].rearrange("p (t h) -> p t h", h=2 * H)).then_inc(kept, 1)

                two_by_two(dve, NCH, rectify, keep)


def gat_softmax(nc, m, b):
    stage = f"sm{b}"
    with ExitStack() as ctx:
        def rows(name):
            return ctx.enter_context(nc.sbuf_tensor(f"{stage}_{name}", [RT, RG, H, P], F32))

        L, S, U, F, B, T, X = [rows(n) for n in ("edge", "self", "both", "forward", "backward", "whole", "carried")]
        SF = ctx.enter_context(nc.sbuf_tensor(f"{stage}_tiles_forward", [H, TILES + 1], F32))
        SB = ctx.enter_context(nc.sbuf_tensor(f"{stage}_tiles_backward", [H, TILES + 1], F32))
        turned, copied, ends, carries, shifted, powers, done, dv = sems(
            ctx, nc, stage, "turned", "copied", "ends", "carries", "shifted", "powers", "done", "dve_chain")
        stored = sems(ctx, nc, stage, "stored")[0]
        banks, ident = m["bank"], m["ident"]
        flat = lambda t: t[:, :, :, :].rearrange("t g h p -> t (g h p)")
        with nc.Block() as block:

            @block.tensor
            def _(pe):
                for g in range(RG):
                    for s in range(2):
                        for h in range(H):
                            last = nc.tensor.transpose(banks[2 * g + s][0:RT, h * P:(h + 1) * P],
                                                       m["logits"][:, g * RT:(g + 1) * RT, s * H + h], ident[:, :])
                last.then_inc(turned, 1)
                for n in range(2):
                    pe.wait_ge(ends, 2 * n + 1)
                    for g in range(RG):
                        nc.tensor.transpose(banks[4][0:H, g * RT:(g + 1) * RT], F[:, g, :, P - 1], ident[0:RT, 0:RT])
                        last = nc.tensor.transpose(banks[5][0:H, g * RT:(g + 1) * RT], B[:, g, :, 0], ident[0:RT, 0:RT])
                    last.then_inc(carries, 1)
                    pe.wait_ge(ends, 2 * n + 2)
                    for g in range(RG):
                        nc.tensor.transpose(banks[6][0:RT, g * H:(g + 1) * H], SF[:, g * RT:(g + 1) * RT], ident[0:H, 0:H])
                        last = nc.tensor.transpose(banks[7][0:RT, g * H:(g + 1) * H], SB[:, g * RT + 1:(g + 1) * RT + 1], ident[0:H, 0:H])
                    last.then_inc(carries, 1)

            @block.scalar
            def _(act):
                act.wait_ge(turned, 1)
                for g in range(RG):
                    for s, to in enumerate((L, S)):
                        nc.scalar.activation(to[:, g, :, :], banks[2 * g + s][0:RT, :].rearrange("t (h p) -> t h p", p=P),
                                             ACT.Copy).then_inc(copied, 1)
                act.wait_ge(shifted, 1)
                nc.scalar.activation(flat(L), flat(L), ACT.Exp).then_inc(powers, 1)
                nc.scalar.activation(flat(S), flat(S), ACT.Exp).then_inc(powers, 1)

            @block.vector
            def _(dve):
                step = in_order(dve, dv)

                def over_destination(n, x, forward, backward, tiles_forward, tiles_backward, inside, op0, op1, mask0, mask1):
                    step(nc.vector.tensor_tensor_scan(flat(F), flat(forward), flat(x), 0.0, op0, op1))
                    nc.vector.tensor_tensor_scan(flat(B)[:, ::-1], flat(backward)[:, ::-1], flat(x)[:, ::-1],
                                                 0.0, op0, op1).then_inc(ends, 1)
                    dve.wait_ge(ends, 2 * n + 1)
                    step(nc.vector.tensor_tensor(flat(T), flat(F), flat(B), op1))
                    if inside:
                        step(nc.vector.tensor_tensor(flat(T), flat(T), flat(x), ALU.subtract))
                    dve.wait_ge(carries, 2 * n + 1)
                    step(nc.vector.tensor_tensor_scan(SF[:, 1:TILES + 1], tiles_forward[:, :], banks[4][0:H, 0:TILES], 0.0, op0, op1))
                    nc.vector.tensor_tensor_scan(SB[:, 0:TILES][:, ::-1], tiles_backward[:, :][:, ::-1],
                                                 banks[5][0:H, 0:TILES][:, ::-1], 0.0, op0, op1).then_inc(ends, 1)
                    dve.wait_ge(carries, 2 * n + 2)
                    for bank, mask in ((banks[6], mask0), (banks[7], mask1)):
                        for g in range(RG):
                            step(nc.vector.tensor_tensor(
                                X[:, g], mask[:, g, :].unsqueeze(1).to_broadcast([RT, H, P]),
                                bank[0:RT, g * H:(g + 1) * H].unsqueeze(2).to_broadcast([RT, H, P]), op0))
                        step(nc.vector.tensor_tensor(flat(T), flat(T), flat(X), op1))

                step(nc.vector.memset(SF[:, 0:1], 0.0))
                step(nc.vector.memset(SB[:, TILES:TILES + 1], 0.0))
                dve.wait_ge(copied, 4)
                step(nc.vector.tensor_tensor(flat(U), flat(L), flat(S), ALU.max))
                over_destination(0, U, m["nF"], m["nB"], m["nWF"], m["nWB"], False, ALU.add, ALU.max, m["nInF"], m["nInB"])
                step(nc.vector.tensor_tensor(flat(L), flat(L), flat(T), ALU.subtract))
                nc.vector.tensor_tensor(flat(S), flat(S), flat(T), ALU.subtract).then_inc(shifted, 1)
                dve.wait_ge(powers, 2)
                over_destination(1, L, m["cF"], m["cB"], m["wF"], m["wB"], True, ALU.mult, ALU.add, m["inF"], m["inB"])
                step(nc.vector.tensor_tensor(flat(T), flat(T), flat(S), ALU.add))
                step(nc.vector.reciprocal(flat(T), flat(T)))
                nc.vector.tensor_tensor(flat(L), flat(L), flat(T), ALU.mult).then_inc(done, 1)

            @block.sync
            def _(sp):
                sp.wait_ge(done, 1)
                for g in range(RG):
                    sp.dma_start(m["alpha_rows"][b].rearrange("h (g t p) -> g t h p", g=RG, p=P)[g], L[:, g, :, :]).then_inc(stored, 16)
                sp.wait_ge(stored, 16 * RG)


def gat_values(nc, m, b):
    stage = f"gv{b}"
    table = m["T"][b + 1]
    with ExitStack() as ctx:
        def bufs(name, *shape, dt=F32):
            return [ctx.enter_context(nc.sbuf_tensor(f"{stage}_{name}{k}", list(shape), dt)) for k in range(2)]

        IDX = bufs("idx", P, CT, dt=I32)
        AR = bufs("alpha", H, CH)
        CB = bufs("goes_on", P, CH, dt=BF16)
        HC = bufs("hidden", P, CH)
        D = bufs("difference", P, CH)
        M = bufs("weighted", P, 2, CH)
        Y = bufs("summed", P, 2, CH)
        OE = bufs("out", P, CT, C)
        loaded, scattered = pair(ctx, nc, stage, "loaded"), pair(ctx, nc, stage, "scattered")
        picked, begun, copied, spread, diffed, moved, weighted, summed, mixed, out = sems(
            ctx, nc, stage, "picked", "begun", "copied", "spread", "differences", "moved", "weighted", "summed", "mixed", "out")
        banks = m["bank"]
        with nc.Block() as block:

            @block.sync
            def _(sp):
                def load(i, k):
                    c = 2 * i + k
                    start = start_of(sp, i, k, CH)
                    sp.wait_ge(summed, 2 * c + 2)
                    sp.dma_start(AR[k][:, :], m["alpha_rows"][b][:, bass.ds(start, CH)]).then_inc(loaded[k], 16)
                    sp.dma_start(CB[k][:, :], m["cont_row"][bass.ds(start, CH)].partition_broadcast(P)).then_inc(loaded[k], 16)

                two_by_two(sp, NCH, load)

            @block.scalar
            def _(act):
                act.sem_inc(moved, 2)

                def copy(i, k):
                    c = 2 * i + k
                    act.wait_ge(mixed, c + 1)
                    nc.scalar.activation(HC[k][:, :], m["HT"][:, bass.ds(c * CH, CH)], ACT.Copy).then_inc(copied, 1)

                def move(i, k):
                    c = 2 * i + k
                    act.wait_ge(diffed, c + 1)
                    act.wait_ge(weighted, 2 * c + 2)
                    nc.scalar.activation(D[k][:, :], banks[4 + k][:, :], ACT.Copy).then_inc(moved, 1)

                two_by_two(act, NCH, copy, move)

            @block.tensor
            def _(pe):
                pe.sem_inc(mixed, 2)

                def spread_weights(i, k):
                    c = 2 * i + k
                    pe.wait_ge(copied, c + 1)
                    pe.wait_ge(moved, c + 1)
                    nc.tensor.matmul(banks[4 + k][:, :], m["diff"][:, :], HC[k][:, :], start=True, stop=True).then_inc(diffed, 1)
                    pe.wait_ge(loaded[k], 32 * i + 32)
                    pe.wait_ge(weighted, 2 * c + 2)
                    for f in range(2):
                        nc.tensor.matmul(banks[2 * k + f][:, :], m["heads"][:, f, :], AR[k][:, :], start=True, stop=True).then_inc(spread, 1)

                def mix(i, k):
                    c = 2 * i + k
                    pe.wait_ge(summed, 2 * c + 6)
                    pe.wait_ge(out, c + 1)
                    for j in range(CT):
                        t = slice(j * P, (j + 1) * P)
                        o = banks[6 + k][:, j * C:(j + 1) * C]
                        nc.tensor.matmul(o, HC[k][:, t], m["wmean"][:, C:P], start=True, stop=False)
                        nc.tensor.matmul(o, Y[k][:, 0, t], m["wout"][:, 0, :], start=False, stop=False)
                        last = nc.tensor.matmul(o, Y[k][:, 1, t], m["wout"][:, 1, :], start=False, stop=True)
                    last.then_inc(mixed, 1)

                two_by_two(pe, NCH, spread_weights, mix)

            @block.vector
            def _(dve):
                dve.sem_inc(weighted, 4)
                dve.sem_inc(summed, 4 - 1)
                dve.sem_inc(out, 2)
                nc.vector.memset(Y[1][:, :, :], 0.0).then_inc(summed, 1)

                def add_up(i, k):
                    c = 2 * i + k
                    dve.wait_ge(moved, c + 3)
                    for f in range(2):
                        dve.wait_ge(spread, 2 * c + f + 1)
                        nc.vector.tensor_tensor(M[k][:, f, :], banks[2 * k + f][:, :], D[k][:, :], ALU.mult).then_inc(weighted, 1)
                    dve.wait_ge(mixed, c + 1)
                    dve.wait_ge(summed, 2 * c + 4)
                    dve.wait_ge(loaded[k], 32 * i + 32)
                    for f in range(2):
                        dve.wait_ge(weighted, 2 * c + f + 5)
                        nc.vector.tensor_tensor_scan(Y[k][:, f, :], CB[k][:, :], M[k][:, f, :], Y[1 - k][:, f, CH - 1:CH],
                                                     ALU.mult, ALU.add).then_inc(summed, 1)

                def put_out(i, k):
                    c = 2 * i + k
                    dve.wait_ge(mixed, c + 3)
                    if later(i):
                        dve.wait_ge(scattered[k], 16 * CT * i)
                    nc.vector.tensor_tensor(OE[k][:, :, :], banks[6 + k][:, 0:CT * C].rearrange("p (t c) -> p t c", c=C),
                                            m["biasb"][:, :].unsqueeze(1).to_broadcast([P, CT, C]), ALU.add).then_inc(out, 1)

                two_by_two(dve, NCH, add_up, put_out, peel=True)

            @block.gpsimd
            def _(pool):
                scatter_loop(nc, pool, m, table, IDX, OE, scattered, picked, begun, out)


def scatter_loop(nc, pool, m, table, IDX, OE, scattered, picked, begun, out):
    def scatter(i, k):
        c = 2 * i + k
        if later(i):
            pool.wait_ge(scattered[k], 16 * CT * i)
        nc.gpsimd.tensor_copy(IDX[k][:, :], m["sidx"][:, bass.ds(c * CT, CT)]).then_inc(picked, 1)
        pool.wait_ge(picked, c + 1)
        pool.wait_ge(out, c + 3)
        pool.sem_inc(begun, 1)
        for j in range(CT):
            pool.indirect_dma_start(table[:, :], bass.IndirectOffsetOnAxis(ap=IDX[k][:, j:j + 1], axis=0), OE[k][:, j, :], None,
                                    bounds_check=N - 1, oob_is_err=False).then_inc(scattered[k], 16)

    two_by_two(pool, NCH, scatter, peel=True)
    for k in range(2):
        pool.wait_ge(scattered[k], 16 * CT * (NCH // 2))


def node_weights(nc, a, m, keep):
    with ExitStack() as ctx:
        def kept(name, shape):
            m[name] = keep.enter_context(nc.sbuf_tensor(f"nw_{name}", shape, F32))
            return m[name]

        w1a, w1b = kept("w1a", [P, C]), kept("w1b", [P, C])
        w2a = kept("w2a", [C + 1, C + 1])
        w2b = kept("w2b", [P, P])
        b1a, b1b = kept("b1a", [C, 1]), kept("b1b", [P, 1])
        b2b = kept("b2b", [P, C])
        zeroed, loaded = sems(ctx, nc, "nw", "zeroed", "loaded")
        with nc.Block() as block:

            @block.vector
            def _(dve):
                nc.vector.memset(w2a[:, :], 0.0).then_inc(zeroed, 1)
                nc.vector.memset(w2b[:, :], 0.0).then_inc(zeroed, 1)
                dve.wait_ge(zeroed, 2)
                nc.vector.memset(w2a[C:C + 1, C:C + 1], 1.0).then_inc(zeroed, 1)

            @block.sync
            def _(sp):
                sp.wait_ge(zeroed, 3)
                loads = ((w1a[:, :], a["W1a"]), (w1b[:, :], a["W1b"]), (w2a[0:C, 0:C], a["W2a"]), (w2a[C:C + 1, 0:C], a["b2a"]),
                         (w2b[0:C, 0:C], a["W2b"]), (w2b[C:P, C:P], a["W2b"]), (b1a[:, :], a["b1a"].rearrange("a c -> c a")),
                         (b1b[0:C, :], a["b1b"].rearrange("a c -> c a")), (b1b[C:P, :], a["b1b"].rearrange("a c -> c a")),
                         (b2b[:, :], a["b2b"][0, :].partition_broadcast(P)))
                for to, of in loads:
                    sp.dma_start(to, of).then_inc(loaded, 16)
                sp.wait_ge(loaded, 16 * len(loads))


def edge_hidden(nc, a, m):
    stage = "eh"
    with ExitStack() as ctx:
        def bufs(name, *shape, dt=F32):
            return [ctx.enter_context(nc.sbuf_tensor(f"{stage}_{name}{k}", list(shape), dt)) for k in range(2)]

        G = bufs("gathered", P, CT, P)
        IDX = bufs("idx", P, CT, dt=I32)
        HC = bufs("hidden", P, CH)
        zero = ctx.enter_context(nc.sbuf_tensor(f"{stage}_zero", [P, SUP * C], F32))
        gathered, loaded = pair(ctx, nc, stage, "gathered"), pair(ctx, nc, stage, "loaded")
        picked, begun, turned, hidden, z, saved, zeroed, cleared = sems(
            ctx, nc, stage, "picked", "begun", "turned", "hidden", "z", "saved", "zeroed", "cleared")
        banks, ZE = m["bank"], m["ZE"]
        with nc.Block() as block:

            @block.gpsimd
            def _(pool):
                def gather(i, k):
                    c = 2 * i + k
                    pool.wait_ge(turned, c + 1)
                    nc.gpsimd.tensor_copy(IDX[k][:, :], m["gidx"][:, bass.ds(c * CT, CT), 0]).then_inc(picked, 1)
                    pool.wait_ge(picked, c + 1)
                    pool.sem_inc(begun, 1)
                    for j in range(CT):
                        pool.indirect_dma_start(G[k][:, j, 0:C], None, m["H2"][:, :],
                                                bass.IndirectOffsetOnAxis(ap=IDX[k][:, j:j + 1], axis=0)).then_inc(gathered[k], 16)

                two_by_two(pool, NCH, gather)

            @block.sync
            def _(sp):
                sp.wait_ge(zeroed, 1)
                for s in range(NSUP):
                    sp.dma_start(grid_view(m["MEAN"])[:, s * SUP:(s + 1) * SUP, :],
                                 zero[:, :].rearrange("p (t c) -> p t c", c=C)).then_inc(cleared, 16)
                sp.dma_start(m["MEAN"][P * GRID:N, :], zero[0:TAIL, 0:C]).then_inc(cleared, 16)

                def load(i, k):
                    c = 2 * i + k
                    start = start_of(sp, i, k, CH)
                    sp.wait_ge(z, c + 1)
                    sp.dma_start(HC[k][C:P, :], a["ea64T"][:, bass.ds(start, CH)]).then_inc(loaded[k], 16)

                two_by_two(sp, NCH, load)
                sp.wait_ge(cleared, 16 * (NSUP + 1))

            @block.tensor
            def _(pe):
                pe.sem_inc(turned, 2)
                pe.sem_inc(z, 2)

                pe.wait_ge(zeroed, 3)

                def turn(i, k):
                    c = 2 * i + k
                    pe.wait_ge(gathered[k], 16 * CT * (i + 1))
                    pe.wait_ge(hidden, c + 1)
                    for j in range(CT):
                        last = nc.tensor.transpose(banks[k][:, j * P:(j + 1) * P], G[k][:, j, :], m["ident"][:, :])
                    last.then_inc(turned, 1)

                def project(i, k):
                    c = 2 * i + k
                    pe.wait_ge(hidden, c + 3)
                    pe.wait_ge(loaded[k], 16 * i + 16)
                    pe.wait_ge(saved, c + 1)
                    nc.tensor.matmul(banks[2 + k][0:C, :], m["w1a"][:, :], HC[k][:, :], start=True, stop=True).then_inc(z, 1)

                two_by_two(pe, NCH, turn, project)

            @block.scalar
            def _(act):
                act.sem_inc(hidden, 2)
                act.sem_inc(saved, 2)

                def hide(i, k):
                    c = 2 * i + k
                    act.wait_ge(turned, c + 3)
                    act.wait_ge(z, c + 1)
                    nc.scalar.activation(HC[k][0:C, :], banks[k][0:C, :], ACT.Copy).then_inc(hidden, 1)

                def save(i, k):
                    c = 2 * i + k
                    act.wait_ge(z, c + 3)
                    nc.scalar.activation(ZE[:, bass.ds(c * CH, CH)], banks[2 + k][0:C, :], ACT.Identity,
                                         bias=m["b1a"][:, 0:1]).then_inc(saved, 1)

                two_by_two(act, NCH, hide, save)

            @block.vector
            def _(dve):
                nc.vector.memset(zero[:, :], 0.0).then_inc(zeroed, 1)
                for k in range(2):
                    nc.vector.memset(G[k][:, :, C:P], 0.0).then_inc(zeroed, 1)

                def count(i, k):
                    c = 2 * i + k
                    dve.wait_ge(saved, c + 3)
                    nc.vector.bn_stats(m["stats"][0:C, bass.ds(c, 1), :], ZE[:, bass.ds(c * WIN, WIN)])

                two_by_two(dve, NCH, count)


def edge_means(nc, m):
    stage = "em"
    with ExitStack() as ctx:
        def bufs(name, *shape, dt=F32):
            return [ctx.enter_context(nc.sbuf_tensor(f"{stage}_{name}{k}", list(shape), dt)) for k in range(2)]

        IDX = bufs("idx", P, CT, dt=I32)
        CB = bufs("goes_on", C + 1, CH, dt=BF16)
        R = bufs("hidden", C + 1, CH)
        Y = bufs("summed", C + 1, CH)
        RC = bufs("inverse", P, CT)
        OE = bufs("out", P, CT, C)
        loaded, scattered = pair(ctx, nc, stage, "loaded"), pair(ctx, nc, stage, "scattered")
        picked, begun, hidden, summed, mixed, inverse, out = sems(
            ctx, nc, stage, "picked", "begun", "hidden", "summed", "mixed", "inverse", "out")
        banks, AB = m["bank"], m["AB"]
        with nc.Block() as block:

            @block.sync
            def _(sp):
                def load(i, k):
                    c = 2 * i + k
                    start = start_of(sp, i, k, CH)
                    sp.wait_ge(summed, c + 1)
                    sp.dma_start(CB[k][:, :], m["cont_row"][bass.ds(start, CH)].partition_broadcast(C + 1)).then_inc(loaded[k], 16)

                two_by_two(sp, NCH, load)

            @block.scalar
            def _(act):
                def hide(i, k):
                    c = 2 * i + k
                    act.wait_ge(summed, c + 1)
                    nc.scalar.activation(R[k][0:C, :], m["ZE"][:, bass.ds(c * CH, CH)], ACT.Relu, bias=AB[0:C, 1:2],
                                         scale=AB[0:C, 0:1]).then_inc(hidden, 1)

                two_by_two(act, NCH, hide)

            @block.vector
            def _(dve):
                dve.sem_inc(out, 2)
                nc.vector.memset(R[0][C:C + 1, :], 1.0)
                nc.vector.memset(R[1][C:C + 1, :], 1.0).then_inc(summed, 1)
                nc.vector.memset(Y[1][:, :], 0.0).then_inc(summed, 1)

                def add_up(i, k):
                    c = 2 * i + k
                    dve.wait_ge(hidden, c + 1)
                    dve.wait_ge(loaded[k], 16 * i + 16)
                    dve.wait_ge(mixed, c + 1)
                    dve.wait_ge(summed, c + 2)
                    nc.vector.tensor_tensor_scan(Y[k][:, :], CB[k][:, :], R[k][:, :], Y[1 - k][:, CH - 1:CH],
                                                 ALU.mult, ALU.add).then_inc(summed, 1)

                def divide(i, k):
                    c = 2 * i + k
                    rows = banks[k][:, 0:CT * (C + 1)].rearrange("p (t c) -> p t c", c=C + 1)
                    dve.wait_ge(mixed, c + 3)
                    dve.wait_ge(out, c + 1)
                    nc.vector.reciprocal(RC[k][:, :], rows[:, :, C]).then_inc(inverse, 1)
                    dve.wait_ge(inverse, c + 1)
                    if later(i):
                        dve.wait_ge(scattered[k], 16 * CT * i)
                    nc.vector.tensor_tensor(OE[k][:, :, :], rows[:, :, 0:C], RC[k][:, :].unsqueeze(2).to_broadcast([P, CT, C]),
                                            ALU.mult).then_inc(out, 1)

                two_by_two(dve, NCH, add_up, divide, peel=True)

            @block.tensor
            def _(pe):
                pe.sem_inc(mixed, 2)

                def mix(i, k):
                    c = 2 * i + k
                    pe.wait_ge(summed, c + 3)
                    pe.wait_ge(out, c + 1)
                    for j in range(CT):
                        last = nc.tensor.matmul(banks[k][:, j * (C + 1):(j + 1) * (C + 1)], Y[k][:, j * P:(j + 1) * P],
                                                m["w2a"][:, :], start=True, stop=True)
                    last.then_inc(mixed, 1)

                two_by_two(pe, NCH, mix)

            @block.gpsimd
            def _(pool):
                scatter_loop(nc, pool, m, m["MEAN"], IDX, OE, scattered, picked, begun, out)


def node_hidden(nc, m):
    stage = "nh"
    with ExitStack() as ctx:
        X = [ctx.enter_context(nc.sbuf_tensor(f"{stage}_rows{k}", [P, SUP, P], F32)) for k in range(2)]
        EV = [ctx.enter_context(nc.sbuf_tensor(f"{stage}_even{k}", [P, SUB // 2 * P], F32)) for k in range(2)]
        OD = [ctx.enter_context(nc.sbuf_tensor(f"{stage}_odd{k}", [P, SUB // 2 * P], F32)) for k in range(2)]
        loaded = pair(ctx, nc, stage, "loaded")
        turned, even, odd, z, saved, counted = sems(ctx, nc, stage, "turned", "even", "odd", "z", "saved", "counted")
        banks, ZN = m["bank"], m["ZN"]
        NB = SUP // SUB
        USES = 2 * NB
        W = SUB // 2 * P

        with nc.Block() as block:

            @block.sync
            def _(sp):
                def load(i, k, tail=False):
                    start = start_of(sp, i, k, SUP)
                    sp.wait_ge(z, USES * i + k * NB + NB)
                    for n, table in enumerate((m["H2"], m["MEAN"])):
                        c = slice(n * C, (n + 1) * C)
                        if tail:
                            sp.dma_start(X[k][0:TAIL, 0, c], table[P * GRID:N, :]).then_inc(loaded[k], 16)
                        else:
                            sp.dma_start(X[k][:, :, c], grid_view(table)[:, bass.ds(start, SUP), :]).then_inc(loaded[k], 16)

                two_by_two(sp, NSUP, load, tail=True)

            @block.tensor
            def _(pe):
                pe.sem_inc(z, USES)

                def turn(i, k, q, tail):
                    u = k * NB + q
                    r = u % 2
                    if q == 0:
                        pe.wait_ge(loaded[k], 32 * i + 32)
                    pe.wait_ge(even, USES * i + u + 1)
                    pe.wait_ge(odd, USES * i + u + 1)
                    if tail:
                        last = nc.tensor.transpose(banks[2 * r][:, 0:TAIL], X[k][0:TAIL, 0, :], m["ident"][0:TAIL, 0:TAIL])
                    for j in range(0 if tail else SUB):
                        last = nc.tensor.transpose(banks[2 * r + j % 2][:, j // 2 * P:(j // 2 + 1) * P], X[k][:, q * SUB + j, :],
                                                   m["ident"][:, :])
                    last.then_inc(turned, 1)

                def project(i, k, q, tail):
                    u = k * NB + q
                    r = u % 2
                    pe.wait_ge(even, USES * i + u + 3)
                    pe.wait_ge(saved, USES * i + u + 1)
                    w = TAIL if tail else W
                    last = nc.tensor.matmul(banks[4 + r][0:C, 0:w], m["w1b"][:, :], EV[r][:, 0:w], start=True, stop=True)
                    if not tail:
                        pe.wait_ge(odd, USES * i + u + 3)
                        last = nc.tensor.matmul(banks[4 + r][C:P, 0:w], m["w1b"][:, :], OD[r][:, 0:w], start=True, stop=True)
                    last.then_inc(z, 1)

                def step(i, k, tail=False):
                    n = 1 if tail else NB
                    for q in range(n + 1):
                        if q < n:
                            turn(i, k, q, tail)
                        if q:
                            project(i, k, q - 1, tail)

                two_by_two(pe, NSUP, step, tail=True)

            @block.scalar
            def _(act):
                act.sem_inc(even, 2)
                act.sem_inc(saved, 2)

                def copy(i, k, q, tail):
                    u = k * NB + q
                    r = u % 2
                    w = TAIL if tail else W
                    act.wait_ge(turned, USES * i + u + 1)
                    act.wait_ge(z, USES * i + u - 1 + USES)
                    nc.scalar.activation(EV[r][:, 0:w], banks[2 * r][:, 0:w], ACT.Copy).then_inc(even, 1)

                def save(i, k, q, tail):
                    u = k * NB + q
                    r = u % 2
                    act.wait_ge(z, USES * i + u + 1 + USES)
                    p, w = (C, TAIL) if tail else (P, W)
                    nc.scalar.activation(ZN[0:p, bass.ds((USES * i + u) * W, w)], banks[4 + r][0:p, 0:w], ACT.Identity,
                                         bias=m["b1b"][0:p, 0:1]).then_inc(saved, 1)

                def step(i, k, tail=False):
                    n = 1 if tail else NB
                    for q in range(n + 1):
                        if q < n:
                            copy(i, k, q, tail)
                        if q:
                            save(i, k, q - 1, tail)

                two_by_two(act, NSUP, step, tail=True)

            @block.vector
            def _(dve):
                dve.sem_inc(odd, 2)

                def copy(i, k, q, tail):
                    u = k * NB + q
                    r = u % 2
                    if not tail:
                        dve.wait_ge(turned, USES * i + u + 1)
                        dve.wait_ge(z, USES * i + u - 1 + USES)
                        nc.vector.tensor_copy(OD[r][:, :], banks[2 * r + 1][:, 0:W]).then_inc(odd, 1)

                def count(i, k, q, tail):
                    u = k * NB + q
                    dve.wait_ge(saved, USES * i + u + 3)
                    if tail:
                        nc.vector.bn_stats(m["stats"][0:C, 2 * NSUB, :], ZN[0:C, NSUB * W:NSUB * W + TAIL])
                    else:
                        nc.vector.bn_stats(m["stats"][:, bass.ds(USES * i + u, 1), :], ZN[:, bass.ds((USES * i + u) * W, W)])

                def step(i, k, tail=False):
                    n = 1 if tail else NB
                    for q in range(n + 1):
                        if q < n:
                            copy(i, k, q, tail)
                        if q:
                            count(i, k, q - 1, tail)

                two_by_two(dve, NSUP, step, tail=True)


def node_out(nc, m, out_table):
    stage = "no"
    with ExitStack() as ctx:
        X = [ctx.enter_context(nc.sbuf_tensor(f"{stage}_rows{k}", [P, SUP, C], F32)) for k in range(2)]
        Y = [ctx.enter_context(nc.sbuf_tensor(f"{stage}_out{k}", [P, SUP, C], F32)) for k in range(2)]
        HC = [ctx.enter_context(nc.sbuf_tensor(f"{stage}_hidden{k}", [P, SUB // 2 * P], F32)) for k in range(4)]
        loaded, stored = pair(ctx, nc, stage, "loaded"), pair(ctx, nc, stage, "stored")
        hidden, mixed, biased, out = sems(ctx, nc, stage, "hidden", "mixed", "biased", "out")
        banks, AB, ZN = m["bank"], m["AB"], m["ZN"]
        NB = SUP // SUB
        USES = 2 * NB
        W = SUB // 2 * P

        def before(u, ring):
            return u - ring if u >= ring else u % ring + (USES - 1 - u % ring) // ring * ring - USES

        def rows(table, start, tail):
            if tail:
                return table[P * GRID:N, :].rearrange("(p t) c -> p t c", t=1)
            return grid_view(table)[:, bass.ds(start, SUP), :]

        with nc.Block() as block:

            @block.sync
            def _(sp):
                def load(i, k, tail=False):
                    p, t = (TAIL, 1) if tail else (P, SUP)
                    start = start_of(sp, i, k, SUP)
                    sp.wait_ge(out, USES * i + k * NB + NB)
                    sp.dma_start(X[k][0:p, 0:t, :], rows(m["XA"], start, tail)).then_inc(loaded[k], 16)

                two_by_two(sp, NSUP, load, tail=True)

            @block.scalar
            def _(act):
                def step(i, k, tail=False):
                    for q in range(1 if tail else NB):
                        u = k * NB + q
                        act.wait_ge(mixed, USES * i + before(u, 4) + 1 + USES)
                        p, w = (C, TAIL) if tail else (P, W)
                        nc.scalar.activation(HC[u % 4][0:p, 0:w], ZN[0:p, bass.ds((USES * i + u) * W, w)], ACT.Relu,
                                             bias=AB[0:p, 1:2], scale=AB[0:p, 0:1]).then_inc(hidden, 1)

                two_by_two(act, NSUP, step, tail=True)

            @block.tensor
            def _(pe):
                pe.sem_inc(mixed, USES)

                def step(i, k, tail=False):
                    for q in range(1 if tail else NB):
                        u = k * NB + q
                        pe.wait_ge(hidden, USES * i + u + 1)
                        pe.wait_ge(out, USES * i + before(u, 4) + 1 + USES)
                        if tail:
                            last = nc.tensor.matmul(banks[u % 4][0:TAIL, 0:C], HC[u % 4][0:C, 0:TAIL], m["w2b"][0:C, 0:C],
                                                    start=True, stop=True)
                        for j in range(0 if tail else SUB // 2):
                            last = nc.tensor.matmul(banks[u % 4][:, j * P:(j + 1) * P], HC[u % 4][:, j * P:(j + 1) * P],
                                                    m["w2b"][:, :], start=True, stop=True)
                        last.then_inc(mixed, 1)

                two_by_two(pe, NSUP, step, tail=True)

            @block.vector
            def _(dve):
                dve.sem_inc(out, USES)

                def step(i, k, tail=False):
                    if later(i):
                        dve.wait_ge(stored[k], 16 * i)
                    dve.wait_ge(biased, 2 * i + k + 1)
                    for q in range(1 if tail else NB):
                        u = k * NB + q
                        dve.wait_ge(mixed, USES * i + u + 1 + USES)
                        p, t = (TAIL, 1) if tail else (P, SUB)
                        nc.vector.tensor_tensor(
                            Y[k][0:p, q * SUB:q * SUB + t, :], banks[u % 4][0:p, 0:t * C].rearrange("p (t c) -> p t c", c=C),
                            X[k][0:p, q * SUB:q * SUB + t, :], ALU.add).then_inc(out, 1)

                two_by_two(dve, NSUP, step, tail=True, peel=True)

            @block.gpsimd
            def _(pool):
                def bias(i, k, tail=False):
                    p, t = (TAIL, 1) if tail else (P, SUP)
                    pool.wait_ge(loaded[k], 16 * i + 16)
                    nc.gpsimd.tensor_tensor(X[k][0:p, 0:t, :], X[k][0:p, 0:t, :],
                                            m["b2b"][0:p, :].unsqueeze(1).to_broadcast([p, t, C]), ALU.add).then_inc(biased, 1)

                def store(i, k, tail=False):
                    p, t = (TAIL, 1) if tail else (P, SUP)
                    start = start_of(pool, i, k, SUP)
                    pool.wait_ge(out, USES * i + k * NB + (1 if tail else NB) + USES)
                    pool.dma_start(rows(out_table, start, tail), Y[k][0:p, 0:t, :]).then_inc(stored[k], 16)

                two_by_two(pool, NSUP, bias, store, tail=True)
                for k in range(2):
                    pool.wait_ge(stored[k], 16 * (NSUP // 2 + 1))


def kernel(x, src, dst, edge_attr_16, edge_attr_64, L0_gnn_Wl, L0_gnn_Wr, L0_gnn_We, L0_gnn_att, L0_gnn_gat_bias, L0_gnn_gn_weight,
           L0_gnn_gn_bias, L0_gnn_gn_mean_scale, L1_gnn_u, L1_gnn_W1a, L1_gnn_b1a, L1_gnn_g1, L1_gnn_be1, L1_gnn_W2a, L1_gnn_b2a,
           L1_gnn_W1b, L1_gnn_b1b, L1_gnn_g2, L1_gnn_be2, L1_gnn_W2b, L1_gnn_b2b):
    import concourse.bacc as bacc
    from concourse.bass_utils import run_bass_kernel_spmd

    def padded(values, fill, before=0):
        row = np.full(EP, fill, np.int32)
        row[:before] = -1
        some = np.asarray(values)[:EP - before]
        row[before:before + some.size] = some
        return row

    def by_tile(row):
        return np.ascontiguousarray(row.reshape(TILES, P).T)

    def by_row(row):
        return np.ascontiguousarray(row.reshape(RG, RT, P).transpose(1, 0, 2))

    src, dst = np.asarray(src), np.asarray(dst)
    own, behind = padded(dst, FAR), padded(dst[1:], FAR)
    behind[E - 1:] = FAR
    ea16T = np.zeros((DE + 1, EP), np.float32)
    ea16T[0] = 1.0
    ea16T[1:, :E] = np.asarray(edge_attr_16).T
    ea64T = np.zeros((C, EP), np.float32)
    ea64T[:, :E] = np.asarray(edge_attr_64).T
    arrays = {
        "x": x, "src_pt": by_tile(padded(src, 0)), "dstg_pt": by_tile(padded(dst, 0)), "dst_pt": by_tile(own),
        "dnext_pt": by_tile(behind), "dst_rows": by_row(own), "dprev_rows": by_row(padded(dst, FAR, before=1)),
        "dnext_rows": by_row(behind), "ea16T": ea16T, "ea64T": ea64T,
        "Wl": L0_gnn_Wl, "Wr": L0_gnn_Wr, "We": L0_gnn_We, "att": L0_gnn_att, "gat_bias": L0_gnn_gat_bias,
        "gn_weight": L0_gnn_gn_weight, "gn_bias": L0_gnn_gn_bias, "gn_mean_scale": L0_gnn_gn_mean_scale,
        "W1a": L1_gnn_W1a, "W2a": L1_gnn_W2a, "W1b": L1_gnn_W1b, "W2b": L1_gnn_W2b,
    }
    for name, row in (("b1a", L1_gnn_b1a), ("g1", L1_gnn_g1), ("be1", L1_gnn_be1), ("b2a", L1_gnn_b2a), ("b1b", L1_gnn_b1b),
                      ("g2", L1_gnn_g2), ("be2", L1_gnn_be2), ("b2b", L1_gnn_b2b)):
        arrays[name] = np.asarray(row).reshape(1, C)
    nc = bacc.Bacc("TRN2", target_bir_lowering=False, num_devices=1)
    aps, given = {}, {}
    for name, value in arrays.items():
        value = np.ascontiguousarray(value)
        given[f"in_{name}"] = value
        aps[name] = nc.dram_tensor(f"in_{name}", value.shape, mybir.dt.from_np(value.dtype), kind="ExternalInput").ap()
    out = nc.dram_tensor("out", (N, C), F32, kind="ExternalOutput").ap()
    build(nc, aps, out)
    return run_bass_kernel_spmd(nc, [given], core_ids=[0]).results[0]["out"]
```

```python
from contextlib import ExitStack

import numpy as np

import concourse.bass as bass
from concourse import mybir

F32 = mybir.dt.float32
I32 = mybir.dt.int32
BF16 = mybir.dt.bfloat16
ALU = mybir.AluOpType
ACT = mybir.ActivationFunctionType
AX = mybir.AxisListType.X

N, C, H, DE, E = 50000, 64, 4, 16, 25000
NBLOCKS = 2
EPS = 1e-5
SLOPE = 0.2
P = 128
GRID = N // P
TAIL = N - P * GRID
SUP, SUB = 30, 6
NSUP, NSUB = GRID // SUP, GRID // SUB
TILES, CT = 200, 4
CH = CT * P
NCH = TILES // CT
EP = TILES * P
RG = 2
RT = TILES // RG
FAR = 1 << 20
BIG = float(2.0**100)
WIN = E // NCH


def grid_view(table):
    return table[0:P * GRID, :].rearrange("(p t) c -> p t c", p=P)


def start_of(eng, i, k, size):
    return (2 * i + k) * size if isinstance(i, int) else eng.snap((2 * i + k) * size)


def build(nc, a, out):
    with ExitStack() as ctx:
        def sb(name, shape, dt=F32):
            return ctx.enter_context(nc.sbuf_tensor(name, shape, dt))

        def dram(name, shape, dt=F32):
            return nc.dram_tensor(name, shape, dt, kind="Internal").ap()

        m = {}
        m["bank"] = [ctx.enter_context(nc.psum_tensor(f"bank{n}", [P, 512], F32)) for n in range(8)]
        m["T"] = [dram(f"table_x{n}", [N, C]) for n in range(NBLOCKS + 1)]
        m["H2"] = dram("table_h2", [N, C])
        m["XA"] = dram("table_xa", [N, C])
        m["MEAN"] = dram("table_mean", [N, C])
        m["cont_row"] = dram("cont_row", [EP], BF16)

        m["ident"] = sb("ident", [P, P])
        m["gidx"] = sb("gidx", [P, TILES, 2], I32)
        m["sidx"] = sb("sidx", [P, TILES], I32)
        for n in ("cF", "nF", "cB", "nB"):
            m[n] = sb(n, [RT, RG, H, P], BF16)
        for n in ("inF", "nInF", "inB", "nInB"):
            m[n] = sb(n, [RT, RG, P])
        for n in ("wF", "wB", "nWF", "nWB"):
            m[n] = sb(n, [H, TILES])
        m["AB"] = sb("AB", [P, 2])
        m["ABrow"] = sb("ABrow", [P, 2, 2, C])
        m["starts"] = sb("starts", [P, TILES])
        m["stats"] = sb("stats", [P, 2 * NSUB + 1, 6])
        m["small"] = sb("small", [C, 16])

        stage(setup_edges, nc, a, m)
        stage(dense_norm, nc, m, "h0", [a["x"]], None, m["T"][0], stats=True)
        for b in range(NBLOCKS):
            with ExitStack() as w:
                stage(gat_weights, nc, a, m, b, w)
                if b:
                    stage(table_stats, nc, m, b)
                stage(norm_coefficients, nc, m, f"gn{b}", a["gn_weight"][b:b + 1, :], a["gn_bias"][b:b + 1, :],
                                  a["gn_mean_scale"][b:b + 1, :])
                stage(gat_base, nc, m, b)
                m["edges"] = w.enter_context(nc.sbuf_tensor(f"edges{b}", [P, TILES, 2 * C], F32))
                m["alpha"] = w.enter_context(nc.sbuf_tensor(f"alpha{b}", [P, TILES, H], F32))
                stage(gat_logits, nc, a, m, b)
                stage(gat_softmax, nc, m, b)
                stage(gat_values, nc, m, b)
        stage(dense_norm, nc, m, "h2", [a["x"], m["T"][2], m["T"][0]], m["XA"], m["H2"], stats=False)
        with ExitStack() as w:
            stage(node_weights, nc, a, m, w)
            with ExitStack() as hidden:
                m["ZE"] = hidden.enter_context(nc.sbuf_tensor("edge_z", [C, EP], F32))
                stage(edge_hidden, nc, a, m)
                stage(norm_coefficients, nc, m, "bn1", a["g1"], a["be1"], None, chunks=NCH)
                stage(edge_means, nc, m)
            m["ZN"] = w.enter_context(nc.sbuf_tensor("node_z", [P, NSUB * SUB // 2 * P + TAIL], F32))
            stage(node_hidden, nc, m)
            stage(norm_coefficients, nc, m, "bn2", a["g2"], a["be2"], None)
            stage(node_out, nc, m, out)


def stage(function, nc, *args, **kwargs):
    function(nc, *args, **kwargs)
    nc.all_engine_barrier()


def sems(ctx, nc, stage, *names):
    made = [nc.alloc_semaphore(f"{stage}_{n}") for n in names]
    ctx.callback(nc.clear_and_free_semaphores, made)
    return made


def pair(ctx, nc, stage, name):
    return sems(ctx, nc, stage, f"{name}0", f"{name}1")


def in_order(eng, sem):
    n = [0]

    def step(ins):
        n[0] += 1
        ins.then_inc(sem, 1)
        eng.wait_ge(sem, n[0])

    return step


def later(i):
    return not (isinstance(i, int) and i == 0)


def two_by_two(eng, count, *parts, tail=None, peel=False):
    for part in parts if peel else ():
        for k in range(2):
            part(0, k)
    with eng.Fori(int(peel), count // 2) as i:
        for part in parts:
            for k in range(2):
                part(i, k)
    rest = [{}] * (count % 2) + ([{"tail": True}] if tail else [])
    for part in parts:
        for k, kind in enumerate(rest):
            part(count // 2, k, **kind)


def setup_edges(nc, a, m):
    with ExitStack() as ctx:
        loaded, made, stored, dv, pv, tr, tc = sems(
            ctx, nc, "edges", "loaded", "made", "stored", "dve_chain", "pool_chain", "turned", "copied")
        pt = ctx.enter_context(nc.sbuf_tensor("pt", [P, 5, TILES], I32))
        ptf = ctx.enter_context(nc.sbuf_tensor("ptf", [P, 4, TILES], F32))
        rows = ctx.enter_context(nc.sbuf_tensor("rows", [RT, 3, RG, P], I32))
        rowf = ctx.enter_context(nc.sbuf_tensor("rowf", [RT, 3, RG, P], F32))
        cont = ctx.enter_context(nc.sbuf_tensor("cont", [RT, 4, RG, P], F32))
        controw = ctx.enter_context(nc.sbuf_tensor("controw", [RT, RG, P], BF16))
        edgeF = ctx.enter_context(nc.sbuf_tensor("edgeF", [RT, RG, P], F32))
        edgeB = ctx.enter_context(nc.sbuf_tensor("edgeB", [RT, RG, P], F32))
        wcol = ctx.enter_context(nc.sbuf_tensor("wcol", [RT, 2, RG, H], F32))
        ident = m["ident"]
        bank = m["bank"][0]
        with nc.Block() as block:

            @block.sync
            def _(sp):
                for n, name in enumerate(("src_pt", "dstg_pt", "dst_pt", "dnext_pt", "dprev_pt")):
                    sp.dma_start(pt[:, n, :], a[name]).then_inc(loaded, 16)
                for n, name in enumerate(("dst_rows", "dprev_rows", "dnext_rows")):
                    sp.dma_start(rows[:, n, :, :], a[name]).then_inc(loaded, 16)
                sp.wait_ge(made, 1)
                for g in range(RG):
                    sp.dma_start(m["cont_row"].rearrange("(g t p) -> g t p", g=RG, p=P)[g], controw[:, g, :]).then_inc(stored, 16)
                sp.wait_ge(stored, 16 * RG)

            @block.gpsimd
            def _(pool):
                step = in_order(pool, pv)
                step(nc.gpsimd.memset(ident[:, :], 0.0))
                step(nc.gpsimd.affine_select(out=ident[:, :], in_=ident[:, :], compare_op=ALU.not_equal, fill=1.0,
                                             base=0, pattern=[[-1, P]], channel_multiplier=1))

            @block.vector
            def _(dve):
                step = in_order(dve, dv)
                dve.wait_ge(loaded, 16 * 8)
                nc.vector.tensor_copy(m["gidx"][:, :, 0], pt[:, 0, :])
                nc.vector.tensor_copy(m["gidx"][:, :, 1], pt[:, 1, :])
                step(nc.vector.tensor_copy(ptf[:, 0:2, :], pt[:, 2:4, :]))
                step(nc.vector.tensor_copy(ptf[:, 3, :], pt[:, 4, :]))
                step(nc.vector.tensor_tensor(m["starts"][:, :], ptf[:, 0, :], ptf[:, 3, :], ALU.not_equal))
                step(nc.vector.tensor_tensor(ptf[:, 2, :], ptf[:, 0, :], ptf[:, 1, :], ALU.is_equal))
                step(nc.vector.scalar_tensor_tensor(ptf[:, 1, :], ptf[:, 2, :], float(FAR), ptf[:, 0, :], ALU.mult, ALU.add))
                step(nc.vector.tensor_copy(m["sidx"][:, :], ptf[:, 1, :]))
                step(nc.vector.tensor_copy(rowf[:, :, :, :], rows[:, :, :, :]))
                step(nc.vector.tensor_tensor(cont[:, 0], rowf[:, 0], rowf[:, 1], ALU.is_equal))
                step(nc.vector.tensor_tensor(cont[:, 1], rowf[:, 0], rowf[:, 2], ALU.is_equal))
                nc.vector.tensor_copy(controw[:, :, :], cont[:, 0]).then_inc(made, 1)
                step(nc.vector.tensor_copy(cont[:, 2:4], cont[:, 0:2]))
                step(nc.vector.memset(cont[:, 2, :, 0:1], 0.0))
                step(nc.vector.memset(cont[:, 3, :, P - 1:P], 0.0))
                step(nc.vector.memset(edgeF[:, :, :], 0.0))
                step(nc.vector.memset(edgeB[:, :, :], 0.0))
                step(nc.vector.tensor_copy(edgeF[:, :, 0:1], cont[:, 0, :, 0:1]))
                step(nc.vector.tensor_copy(edgeB[:, :, P - 1:P], cont[:, 1, :, P - 1:P]))
                flat = lambda t: t.rearrange("t g p -> t (g p)")
                step(nc.vector.tensor_tensor_scan(flat(m["inF"][:, :, :]), flat(cont[:, 2]), flat(edgeF[:, :, :]),
                                                  0.0, ALU.mult, ALU.add))
                step(nc.vector.tensor_tensor_scan(flat(m["inB"][:, :, :])[:, ::-1], flat(cont[:, 3])[:, ::-1],
                                                  flat(edgeB[:, :, :])[:, ::-1], 0.0, ALU.mult, ALU.add))
                for to, of in (("nInF", m["inF"]), ("nInB", m["inB"])):
                    step(nc.vector.tensor_scalar(m[to][:, :, :], of[:, :, :], -1.0, BIG, ALU.add, ALU.mult))
                for n, (c, neg) in enumerate((("cF", "nF"), ("cB", "nB"))):
                    for h in range(H):
                        step(nc.vector.tensor_copy(m[c][:, :, h, :], cont[:, 2 + n]))
                    step(nc.vector.tensor_scalar(m[neg][:, :, :, :], m[c][:, :, :, :], -1.0, BIG, ALU.add, ALU.mult))
                step(nc.vector.tensor_copy(wcol[:, 0], m["inF"][:, :, P - 1:P].to_broadcast([RT, RG, H])))
                nc.vector.tensor_copy(wcol[:, 1], m["inB"][:, :, 0:1].to_broadcast([RT, RG, H])).then_inc(tr, 1)
                dve.wait_ge(tc, 1)
                step(nc.vector.tensor_copy(m["wF"][:, :], bank[0:H, 0:TILES]))
                step(nc.vector.tensor_copy(m["wB"][:, :], bank[0:H, TILES:2 * TILES]))
                step(nc.vector.tensor_scalar(m["nWF"][:, :], m["wF"][:, :], -1.0, BIG, ALU.add, ALU.mult))
                step(nc.vector.tensor_scalar(m["nWB"][:, :], m["wB"][:, :], -1.0, BIG, ALU.add, ALU.mult))

            @block.tensor
            def _(pe):
                pe.wait_ge(pv, 2)
                pe.wait_ge(tr, 1)
                for n in range(2):
                    for g in range(RG):
                        at = n * TILES + g * RT
                        last = nc.tensor.transpose(bank[0:H, at:at + RT], wcol[:, n, g, :], ident[0:RT, 0:RT])
                last.then_inc(tc, 1)


def dense_norm(nc, m, stage, sources, sum_table, table, stats):
    with ExitStack() as ctx:
        def bufs(name, *shape):
            return [ctx.enter_context(nc.sbuf_tensor(f"{stage}_{name}{k}", [P, *shape], F32)) for k in range(2)]

        n_in = len(sources)
        X, CEN, SQ, HN, OUT = [bufs(n, SUP, C) for n in ("sum", "centred", "squares", "scaled", "out")]
        MORE = [bufs(f"more{q}", SUP, C) for q in range(1, n_in)]
        R = bufs("rows", 4, SUP)
        added, meaned, centred, squared, varied, rooted, inverted, scaled, normed, turned, counted, begun = sems(
            ctx, nc, stage, "added", "meaned", "centred", "squared", "varied", "rooted", "inverted", "scaled", "normed", "turned", "counted", "begun")
        loaded, stored, sum_stored = [pair(ctx, nc, stage, n) for n in ("loaded", "stored", "sum_stored")]
        banks = m["bank"]
        NB = SUP // SUB
        USES = 2 * NB

        def shape(tail):
            return (TAIL, 1) if tail else (P, SUP)

        def of(table, start, tail):
            if tail:
                return table[P * GRID:N, :].rearrange("(p t) c -> p t c", t=1)
            return grid_view(table)[:, bass.ds(start, SUP), :]

        with nc.Block() as block:

            @block.sync
            def _(sp):
                def load(i, k, tail=False):
                    p, t = shape(tail)
                    start = start_of(sp, i, k, SUP)
                    sp.wait_ge(centred, 2 * i + k + 1)
                    if sum_table is not None and later(i):
                        sp.sem_inc(begun, 1)
                        sp.wait_ge(sum_stored[k], 16 * i)
                    for q, source in enumerate(sources):
                        to = X[k] if q == 0 else MORE[q - 1][k]
                        sp.dma_start(to[0:p, 0:t, :], of(source, start, tail)).then_inc(loaded[k], 16)

                two_by_two(sp, NSUP, load, tail=True, peel=True)
                for k in range(2):
                    sp.wait_ge(stored[k], 16 * (NSUP // 2 + 1))
                    if sum_table is not None:
                        sp.wait_ge(sum_stored[k], 16 * (NSUP // 2 + 1))

            @block.vector
            def _(dve):
                dve.sem_inc(counted, USES)

                def mean(i, k, tail=False):
                    p, t = shape(tail)
                    s = 2 * i + k
                    x, r = X[k][0:p, 0:t, :], R[k]
                    dve.wait_ge(loaded[k], 16 * n_in * (i + 1))
                    for q in range(1, n_in):
                        nc.vector.tensor_tensor(x, x, MORE[q - 1][k][0:p, 0:t, :], ALU.add).then_inc(added, 1)
                        dve.wait_ge(added, (n_in - 1) * s + q)
                    dve.wait_ge(scaled, s + 1)
                    nc.vector.tensor_reduce(r[0:p, 0, 0:t], x, AX, ALU.add).then_inc(meaned, 1)
                    dve.wait_ge(meaned, 2 * s + 1)
                    nc.vector.tensor_scalar(r[0:p, 1, 0:t], r[0:p, 0, 0:t], -1.0 / C, None, ALU.mult).then_inc(meaned, 1)

                def variance(i, k, tail=False):
                    p, t = shape(tail)
                    s = 2 * i + k
                    r = R[k]
                    dve.wait_ge(squared, s + 1)
                    nc.vector.tensor_reduce(r[0:p, 2, 0:t], SQ[k][0:p, 0:t, :], AX, ALU.add).then_inc(varied, 1)
                    dve.wait_ge(varied, 2 * s + 1)
                    nc.vector.tensor_scalar(r[0:p, 2, 0:t], r[0:p, 2, 0:t], 1.0 / C, EPS, ALU.mult, ALU.add).then_inc(varied, 1)

                def invert(i, k, tail=False):
                    p, t = shape(tail)
                    s = 2 * i + k
                    dve.wait_ge(rooted, s + 1)
                    nc.vector.reciprocal(R[k][0:p, 3, 0:t], R[k][0:p, 3, 0:t]).then_inc(inverted, 1)

                def count(i, k, tail=False):
                    for q in range(1 if tail else NB):
                        u = k * NB + q
                        dve.wait_ge(turned, USES * i + u + 1)
                        if tail:
                            nc.vector.bn_stats(m["stats"][0:C, 2 * NSUB, :], banks[u % 8][0:C, 0:TAIL]).then_inc(counted, 1)
                        else:
                            nc.vector.bn_stats(m["stats"][:, bass.ds((2 * i + k) * NB + q, 1), :],
                                               banks[u % 8][:, 0:SUB // 2 * P]).then_inc(counted, 1)

                two_by_two(dve, NSUP, mean, variance, invert, *([count] if stats else []), tail=True)

            @block.gpsimd
            def _(pool):
                pool.sem_inc(centred, 2)
                pool.sem_inc(scaled, 2)

                def centre(i, k, tail=False):
                    p, t = shape(tail)
                    s = 2 * i + k
                    pool.wait_ge(meaned, 2 * s + 2)
                    pool.wait_ge(scaled, s + 1)
                    nc.gpsimd.tensor_tensor(CEN[k][0:p, 0:t, :], X[k][0:p, 0:t, :],
                                            R[k][0:p, 1, 0:t].unsqueeze(2).to_broadcast([p, t, C]), ALU.add).then_inc(centred, 1)

                def scale(i, k, tail=False):
                    p, t = shape(tail)
                    s = 2 * i + k
                    pool.wait_ge(centred, s + 3)
                    pool.wait_ge(inverted, s + 1)
                    pool.wait_ge(normed, s + 1)
                    nc.gpsimd.tensor_tensor(HN[k][0:p, 0:t, :], CEN[k][0:p, 0:t, :],
                                            R[k][0:p, 3, 0:t].unsqueeze(2).to_broadcast([p, t, C]), ALU.mult).then_inc(scaled, 1)

                two_by_two(pool, NSUP, centre, scale, tail=True)

            @block.scalar
            def _(act):
                act.sem_inc(normed, 2)

                def square(i, k, tail=False):
                    p, t = shape(tail)
                    s = 2 * i + k
                    start = start_of(act, i, k, SUP)
                    act.wait_ge(centred, s + 3)
                    nc.scalar.activation(SQ[k][0:p, 0:t, :], CEN[k][0:p, 0:t, :], ACT.Square).then_inc(squared, 1)
                    if sum_table is not None:
                        act.dma_start(of(sum_table, start, tail), X[k][0:p, 0:t, :]).then_inc(sum_stored[k], 16)

                def root(i, k, tail=False):
                    p, t = shape(tail)
                    s = 2 * i + k
                    act.wait_ge(varied, 2 * s + 2)
                    nc.scalar.activation(R[k][0:p, 3, 0:t], R[k][0:p, 2, 0:t], ACT.Sqrt).then_inc(rooted, 1)

                def rectify(i, k, tail=False):
                    p, t = shape(tail)
                    s = 2 * i + k
                    start = start_of(act, i, k, SUP)
                    act.wait_ge(scaled, s + 3)
                    if later(i):
                        act.wait_ge(stored[k], 16 * i)
                    if stats:
                        act.wait_ge(counted, USES * i + NB * (k + 1))
                    nc.scalar.activation(OUT[k][0:p, 0:t, :], HN[k][0:p, 0:t, :], ACT.Relu).then_inc(normed, 1)
                    act.wait_ge(normed, s + 3)
                    act.dma_start(of(table, start, tail), OUT[k][0:p, 0:t, :]).then_inc(stored[k], 16)

                two_by_two(act, NSUP, square, root, rectify, tail=True, peel=True)

            @block.tensor
            def _(pe):
                def turn(i, k, tail=False):
                    pe.wait_ge(normed, 2 * i + k + 3)
                    for q in range(1 if tail else NB):
                        u = k * NB + q
                        before = u - 8 if u >= 8 else u + 8 - USES if u + 8 < USES else u - USES
                        pe.wait_ge(counted, USES * i + before + 1 + USES)
                        if tail:
                            last = nc.tensor.transpose(banks[u % 8][0:C, 0:TAIL], OUT[k][0:TAIL, 0, :], m["ident"][0:TAIL, 0:TAIL])
                        for j in range(0 if tail else SUB // 2):
                            two = OUT[k][:, q * SUB + 2 * j:q * SUB + 2 * j + 2, :].rearrange("p t c -> p (t c)")
                            last = nc.tensor.transpose(banks[u % 8][:, j * P:(j + 1) * P], two, m["ident"][:, :])
                        last.then_inc(turned, 1)

                if stats:
                    two_by_two(pe, NSUP, turn, tail=True)


def table_stats(nc, m, b):
    stage = f"ts{b}"
    table = m["T"][b]
    with ExitStack() as ctx:
        X = [ctx.enter_context(nc.sbuf_tensor(f"{stage}_rows{k}", [P, SUP, C], F32)) for k in range(2)]
        loaded = pair(ctx, nc, stage, "loaded")
        turned, counted = sems(ctx, nc, stage, "turned", "counted")
        banks = m["bank"]
        NB = SUP // SUB
        USES = 2 * NB
        with nc.Block() as block:

            @block.sync
            def _(sp):
                def load(i, k, tail=False):
                    start = start_of(sp, i, k, SUP)
                    sp.wait_ge(counted, USES * i + k * NB + NB)
                    if tail:
                        sp.dma_start(X[k][0:TAIL, 0, :], table[P * GRID:N, :]).then_inc(loaded[k], 16)
                    else:
                        sp.dma_start(X[k][:, :, :], grid_view(table)[:, bass.ds(start, SUP), :]).then_inc(loaded[k], 16)

                two_by_two(sp, NSUP, load, tail=True)

            @block.tensor
            def _(pe):
                def turn(i, k, tail=False):
                    pe.wait_ge(loaded[k], 16 * i + 16)
                    for q in range(1 if tail else NB):
                        u = k * NB + q
                        before = u - 8 if u >= 8 else u + 8 - USES if u + 8 < USES else u - USES
                        pe.wait_ge(counted, USES * i + before + 1 + USES)
                        if tail:
                            last = nc.tensor.transpose(banks[u % 8][0:C, 0:TAIL], X[k][0:TAIL, 0, :], m["ident"][0:TAIL, 0:TAIL])
                        for j in range(0 if tail else SUB // 2):
                            two = X[k][:, q * SUB + 2 * j:q * SUB + 2 * j + 2, :].rearrange("p t c -> p (t c)")
                            last = nc.tensor.transpose(banks[u % 8][:, j * P:(j + 1) * P], two, m["ident"][:, :])
                        last.then_inc(turned, 1)

                two_by_two(pe, NSUP, turn, tail=True)

            @block.vector
            def _(dve):
                dve.sem_inc(counted, USES)

                def count(i, k, tail=False):
                    for q in range(1 if tail else NB):
                        u = k * NB + q
                        dve.wait_ge(turned, USES * i + u + 1)
                        if tail:
                            nc.vector.bn_stats(m["stats"][0:C, 2 * NSUB, :], banks[u % 8][0:C, 0:TAIL]).then_inc(counted, 1)
                        else:
                            nc.vector.bn_stats(m["stats"][:, bass.ds((2 * i + k) * NB + q, 1), :],
                                               banks[u % 8][:, 0:SUB // 2 * P]).then_inc(counted, 1)

                two_by_two(dve, NSUP, count, tail=True)


def norm_coefficients(nc, m, stage, weight, bias, mean_scale, chunks=None):
    with ExitStack() as ctx:
        moved, loaded, varied, rooted, made, spread, dv = sems(
            ctx, nc, stage, "moved", "loaded", "varied", "rooted", "made", "spread", "dve_chain")
        v = m["small"]
        stats, AB = m["stats"], m["AB"]
        wide = ctx.enter_context(nc.sbuf_tensor(f"{stage}_wide", [C, 2, P], F32))
        widened, rowed = sems(ctx, nc, stage, "widened", "rowed")
        with nc.Block() as block:

            @block.sync
            def _(sp):
                sp.dma_start(v[:, 2:3], weight.rearrange("a c -> c a")).then_inc(loaded, 16)
                sp.dma_start(v[:, 3:4], bias.rearrange("a c -> c a")).then_inc(loaded, 16)
                if mean_scale is not None:
                    sp.dma_start(v[:, 4:5], mean_scale.rearrange("a c -> c a")).then_inc(loaded, 16)
                if chunks is None:
                    sp.dma_start(stats[0:C, NSUB:2 * NSUB, :], stats[C:P, 0:NSUB, :]).then_inc(moved, 16)
                sp.wait_ge(made, 1)
                sp.dma_start(AB[C:P, :], AB[0:C, :]).then_inc(spread, 16)
                sp.wait_ge(spread, 16)

            @block.tensor
            def _(pe):
                if mean_scale is not None:
                    pe.wait_ge(widened, 1)
                    for n in range(2):
                        for k in range(2):
                            last = nc.tensor.matmul(m["bank"][0][:, (2 * n + k) * C:(2 * n + k + 1) * C], wide[:, n, :],
                                                    m["ident"][0:C, 0:C], start=True, stop=True)
                    last.then_inc(rowed, 1)

            @block.scalar
            def _(act):
                act.wait_ge(varied, 1)
                nc.scalar.activation(v[:, 7:8], v[:, 6:7], ACT.Sqrt).then_inc(rooted, 1)

            @block.vector
            def _(dve):
                step = in_order(dve, dv)
                if chunks is None:
                    dve.wait_ge(moved, 16)
                step(nc.vector.bn_aggr(v[:, 0:2], stats[0:C, 0:chunks or 2 * NSUB + 1, :].rearrange("c n s -> c (n s)")))
                dve.wait_ge(loaded, 16 * (2 if mean_scale is None else 3))
                mean, var, w, b, scaled, t = (v[:, n:n + 1] for n in (0, 1, 2, 3, 5, 6))
                if mean_scale is None:
                    step(nc.vector.tensor_copy(scaled, mean))
                else:
                    step(nc.vector.tensor_tensor(scaled, mean, v[:, 4:5], ALU.mult))
                    step(nc.vector.tensor_tensor(t, mean, scaled, ALU.subtract))
                    step(nc.vector.tensor_tensor(t, t, t, ALU.mult))
                    step(nc.vector.tensor_tensor(var, var, t, ALU.add))
                nc.vector.tensor_scalar(t, var, EPS, None, ALU.add).then_inc(varied, 1)
                dve.wait_ge(rooted, 1)
                step(nc.vector.reciprocal(t, v[:, 7:8]))
                step(nc.vector.tensor_tensor(AB[0:C, 0:1], t, w, ALU.mult))
                step(nc.vector.tensor_tensor(t, scaled, AB[0:C, 0:1], ALU.mult))
                nc.vector.tensor_tensor(AB[0:C, 1:2], b, t, ALU.subtract).then_inc(made, 1)
                if mean_scale is not None:
                    dve.wait_ge(made, 1)
                    nc.vector.tensor_copy(wide[:, :, :], AB[0:C, :].unsqueeze(2).to_broadcast([C, 2, P])).then_inc(widened, 1)
                    dve.wait_ge(rowed, 1)
                    nc.vector.tensor_copy(m["ABrow"][:, :, :, :].rearrange("p n k c -> p (n k c)"), m["bank"][0][:, 0:4 * C])


def gat_weights(nc, a, m, b, keep):
    stage = f"gw{b}"
    with ExitStack() as ctx:
        def kept(name, shape):
            m[name] = keep.enter_context(nc.sbuf_tensor(f"{stage}_{name}", shape, F32))
            return m[name]

        def tmp(name, shape):
            return ctx.enter_context(nc.sbuf_tensor(f"{stage}_{name}", shape, F32))

        wself = kept("wself", [P, H * C])
        wedge = kept("wedge", [C + DE, H * C])
        att = kept("att", [P, 2, H])
        eem = kept("eem", [P, 2])
        wout = kept("wout", [P, 2, C])
        wmean = kept("wmean", [P, P])
        biasb = kept("biasb", [P, C])
        wl2 = tmp("wl2", [P, H * C])
        eseg = tmp("eseg", [P, E // 8])
        esum = tmp("esum", [P, 1])
        wes = tmp("wes", [P, H * C])
        zeroed, loaded, dv, ready, summed = sems(ctx, nc, stage, "zeroed", "loaded", "dve_chain", "ready", "summed")
        Wl, Wr, We, attd = (a[n] for n in ("Wl", "Wr", "We", "att"))
        bank = m["bank"][0]
        with nc.Block() as block:

            @block.gpsimd
            def _(pool):
                for t in (wself[:, :], att[:, :, :], wmean[:, :]):
                    nc.gpsimd.memset(t, 0.0).then_inc(zeroed, 1)

            @block.sync
            def _(sp):
                sp.wait_ge(zeroed, 3)
                n = 0
                for to, of in ((wself[C:P, :], Wr[b]), (wedge[0:C, :], Wl[b]), (wedge[C:C + DE, :], We[b]), (wl2[0:C, :], Wl[b]),
                               (wl2[C:P, :], Wl[b]), (biasb[:, :], a["gat_bias"][b, :].partition_broadcast(P))):
                    sp.dma_start(to, of).then_inc(loaded, 16)
                    n += 1
                for h in range(H):
                    at = (h % 2) * C
                    sp.dma_start(att[at:at + C, h // 2, h:h + 1], attd[b, h:h + 1, :].rearrange("a c -> c a")).then_inc(loaded, 16)
                    sp.dma_start(wout[at:at + C, h // 2, :], Wl[b, :, h * C:(h + 1) * C]).then_inc(loaded, 16)
                    n += 2
                for s in range(8):
                    sp.dma_start(eseg[s * DE:(s + 1) * DE, :], a["ea16T"][:, s * (E // 8):(s + 1) * (E // 8)]).then_inc(loaded, 16)
                    sp.dma_start(wes[s * DE:(s + 1) * DE, :], We[b]).then_inc(loaded, 16)
                    n += 2
                assert n == 30

            @block.vector
            def _(dve):
                step = in_order(dve, dv)
                dve.wait_ge(loaded, 16 * 30)
                step(nc.vector.tensor_reduce(esum[:, :], eseg[:, :], AX, ALU.add))
                nc.vector.tensor_scalar(esum[:, :], esum[:, :], 1.0 / E, None, ALU.mult).then_inc(ready, 1)
                step(nc.vector.tensor_tensor(wself[C:P, :], wself[C:P, :], wl2[C:P, :], ALU.add))
                for at in (0, C):
                    r = slice(at, at + C)
                    to = wmean[r, at:at + C]
                    step(nc.vector.tensor_tensor(to, wl2[r, 0:C], wl2[r, C:2 * C], ALU.add))
                    for h in range(2, H):
                        step(nc.vector.tensor_tensor(to, to, wl2[r, h * C:(h + 1) * C], ALU.add))
                    step(nc.vector.tensor_scalar(to, to, 1.0 / H, None, ALU.mult))
                step(nc.vector.tensor_scalar(wout[:, :, :], wout[:, :, :], 1.0 / H, None, ALU.mult))
                dve.wait_ge(summed, 1)
                step(nc.vector.tensor_copy(eem[:, :], bank[:, 0:2]))

            @block.tensor
            def _(pe):
                pe.wait_ge(ready, 1)
                for f in range(2):
                    last = nc.tensor.matmul(bank[:, f:f + 1], wes[:, f * P:(f + 1) * P], esum[:, :], start=True, stop=True)
                last.then_inc(summed, 1)


def gat_base(nc, m, b):
    stage = f"gb{b}"
    source, table = m["T"][b], m["T"][b + 1]
    with ExitStack() as ctx:
        X = [ctx.enter_context(nc.sbuf_tensor(f"{stage}_rows{k}", [P, SUP, C], F32)) for k in range(2)]
        Y = [ctx.enter_context(nc.sbuf_tensor(f"{stage}_next{k}", [P, SUP, C], F32)) for k in range(2)]
        HC = [ctx.enter_context(nc.sbuf_tensor(f"{stage}_hidden{k}", [P, SUB // 2 * P], F32)) for k in range(4)]
        loaded, stored = pair(ctx, nc, stage, "loaded"), pair(ctx, nc, stage, "stored")
        turned, hidden, mixed, out = sems(ctx, nc, stage, "turned", "hidden", "mixed", "out")
        banks, AB = m["bank"], m["AB"]
        NB = SUP // SUB
        USES = 2 * NB
        W = SUB // 2 * P

        def before(u, ring):
            return u - ring if u >= ring else u % ring + (USES - 1 - u % ring) // ring * ring - USES

        with nc.Block() as block:

            @block.sync
            def _(sp):
                def load(i, k, tail=False):
                    start = start_of(sp, i, k, SUP)
                    sp.wait_ge(hidden, USES * i + k * NB + NB)
                    if tail:
                        sp.dma_start(X[k][0:TAIL, 0, :], source[P * GRID:N, :]).then_inc(loaded[k], 16)
                    else:
                        sp.dma_start(X[k][:, :, :], grid_view(source)[:, bass.ds(start, SUP), :]).then_inc(loaded[k], 16)

                two_by_two(sp, NSUP, load, tail=True)

            @block.tensor
            def _(pe):
                pe.sem_inc(mixed, USES)

                def turn(i, k, q, tail):
                    u = k * NB + q
                    if q == 0:
                        pe.wait_ge(loaded[k], 16 * i + 16)
                    pe.wait_ge(hidden, USES * i + before(u, 4) + 1 + USES)
                    if tail:
                        last = nc.tensor.transpose(banks[u % 4][0:C, 0:TAIL], X[k][0:TAIL, 0, :], m["ident"][0:TAIL, 0:TAIL])
                    for j in range(0 if tail else SUB // 2):
                        two = X[k][:, q * SUB + 2 * j:q * SUB + 2 * j + 2, :].rearrange("p t c -> p (t c)")
                        last = nc.tensor.transpose(banks[u % 4][:, j * P:(j + 1) * P], two, m["ident"][:, :])
                    last.then_inc(turned, 1)

                def mix(i, k, q, tail):
                    u = k * NB + q
                    pe.wait_ge(hidden, USES * i + u + 1 + USES)
                    pe.wait_ge(out, USES * i + before(u, 4) + 1 + USES)
                    if tail:
                        last = nc.tensor.matmul(banks[4 + u % 4][0:TAIL, 0:C], HC[u % 4][0:C, 0:TAIL], m["wmean"][0:C, 0:C],
                                                start=True, stop=True)
                    for j in range(0 if tail else SUB // 2):
                        last = nc.tensor.matmul(banks[4 + u % 4][:, j * P:(j + 1) * P], HC[u % 4][:, j * P:(j + 1) * P],
                                                m["wmean"][:, :], start=True, stop=True)
                    last.then_inc(mixed, 1)

                def step(i, k, tail=False):
                    n = 1 if tail else NB
                    for q in range(n + 2):
                        if q < n:
                            turn(i, k, q, tail)
                        if q >= 2:
                            mix(i, k, q - 2, tail)

                two_by_two(pe, NSUP, step, tail=True)

            @block.scalar
            def _(act):
                act.sem_inc(hidden, USES)

                def step(i, k, tail=False):
                    for q in range(1 if tail else NB):
                        u = k * NB + q
                        act.wait_ge(turned, USES * i + u + 1)
                        act.wait_ge(mixed, USES * i + before(u, 4) + 1 + USES)
                        p, w = (C, TAIL) if tail else (P, W)
                        nc.scalar.activation(HC[u % 4][0:p, 0:w], banks[u % 4][0:p, 0:w], ACT.Relu, bias=AB[0:p, 1:2],
                                             scale=AB[0:p, 0:1]).then_inc(hidden, 1)

                two_by_two(act, NSUP, step, tail=True)

            @block.vector
            def _(dve):
                dve.sem_inc(out, USES)

                def step(i, k, tail=False):
                    if later(i):
                        dve.wait_ge(stored[k], 16 * i)
                    for q in range(1 if tail else NB):
                        u = k * NB + q
                        dve.wait_ge(mixed, USES * i + u + 1 + USES)
                        p, t = (TAIL, 1) if tail else (P, SUB)
                        nc.vector.tensor_tensor(
                            Y[k][0:p, q * SUB:q * SUB + t, :], banks[4 + u % 4][0:p, 0:t * C].rearrange("p (t c) -> p t c", c=C),
                            m["biasb"][0:p, :].unsqueeze(1).to_broadcast([p, t, C]), ALU.add).then_inc(out, 1)

                two_by_two(dve, NSUP, step, tail=True, peel=True)

            @block.gpsimd
            def _(pool):
                def store(i, k, tail=False):
                    n = 1 if tail else NB
                    start = start_of(pool, i, k, SUP)
                    pool.wait_ge(out, USES * i + k * NB + n + USES)
                    if tail:
                        pool.dma_start(table[P * GRID:N, :], Y[k][0:TAIL, 0, :]).then_inc(stored[k], 16)
                    else:
                        pool.dma_start(grid_view(table)[:, bass.ds(start, SUP), :], Y[k][:, :, :]).then_inc(stored[k], 16)

                two_by_two(pool, NSUP, store, tail=True)
                for k in range(2):
                    pool.wait_ge(stored[k], 16 * (NSUP // 2 + 1))


def gat_logits(nc, a, m, b):
    stage = f"gl{b}"
    table = m["T"][b]
    with ExitStack() as ctx:
        def bufs(name, *shape, dt=F32):
            return [ctx.enter_context(nc.sbuf_tensor(f"{stage}_{name}{k}", list(shape), dt)) for k in range(2)]

        IDX = bufs("idx", P, CT, 2, dt=I32)
        G = bufs("gathered", P, CT, 2 * C)
        HR = bufs("rows", P, CT, 2 * C)
        HC = bufs("channels", P, CH)
        DA = bufs("difference", C + DE, CH)
        ZS = bufs("z_self", P, 2, CH)
        ZE = bufs("z_edge", P, 2, CH)
        gathered, loaded = pair(ctx, nc, stage, "gathered"), pair(ctx, nc, stage, "loaded")
        picked, begun, scaled, shifted, normed, differed, saved, parted, turned, hidden, stacked = sems(
            ctx, nc, stage, "picked", "begun", "scaled", "shifted", "normed", "differed", "saved", "parted", "turned", "hidden", "stacked")
        zs, ze, cs, ce, ls, le, apart, logit, kept = sems(
            ctx, nc, stage, "z_self", "z_edge", "copied_self", "copied_edge", "leaky_self", "leaky_edge", "apart", "logits", "kept")
        banks = m["bank"]
        with nc.Block() as block:

            @block.gpsimd
            def _(pool):
                def gather(i, k):
                    c = 2 * i + k
                    pool.wait_ge(scaled, c + 1)
                    nc.gpsimd.tensor_copy(IDX[k][:, :, :], m["gidx"][:, bass.ds(c * CT, CT), :]).then_inc(picked, 1)
                    pool.wait_ge(picked, c + 1)
                    pool.sem_inc(begun, 1)
                    for j in range(CT):
                        for side in range(2):
                            pool.indirect_dma_start(G[k][:, j, side * C:(side + 1) * C], None, table[:, :],
                                                    bass.IndirectOffsetOnAxis(ap=IDX[k][:, j, side:side + 1], axis=0)
                                                    ).then_inc(gathered[k], 16)

                two_by_two(pool, NCH, gather)

            @block.sync
            def _(sp):
                def load(i, k):
                    start = start_of(sp, i, k, CH)
                    sp.wait_ge(ze, 4 * i + 2 * k + 2)
                    sp.dma_start(DA[k][C:C + DE, :], a["ea16T"][:, bass.ds(start, CH)]).then_inc(loaded[k], 16)

                two_by_two(sp, NCH, load)

            @block.vector
            def _(dve):
                dve.sem_inc(scaled, 2)
                dve.sem_inc(le, 4)
                dve.sem_inc(apart, 4)
                dve.sem_inc(kept, 2)
                dve.sem_inc(parted, 2)
                ab = [m["ABrow"][:, n].rearrange("p k c -> p (k c)").unsqueeze(1).to_broadcast([P, CT, 2 * C]) for n in range(2)]

                def norm(i, k):
                    c = 2 * i + k
                    dve.wait_ge(gathered[k], 16 * 2 * CT * (i + 1))
                    dve.wait_ge(turned, c + 1)
                    dve.wait_ge(saved, c + 1)
                    dve.wait_ge(parted, c + 1)
                    nc.vector.tensor_tensor(HR[k][:, :, :], G[k][:, :, :], ab[0], ALU.mult).then_inc(scaled, 1)
                    dve.wait_ge(scaled, c + 3)
                    nc.vector.tensor_tensor(HR[k][:, :, :], HR[k][:, :, :], ab[1], ALU.add).then_inc(shifted, 1)

                def differ(i, k):
                    c = 2 * i + k
                    dve.wait_ge(normed, c + 1)
                    nc.vector.tensor_tensor(HR[k][:, :, 0:C], HR[k][:, :, 0:C], HR[k][:, :, C:2 * C], ALU.subtract).then_inc(differed, 1)
                    nc.vector.tensor_tensor(m["edges"][:, bass.ds(c * CT, CT), C:2 * C], HR[k][:, :, C:2 * C],
                                            m["starts"][:, bass.ds(c * CT, CT)].unsqueeze(2).to_broadcast([P, CT, C]),
                                            ALU.mult).then_inc(parted, 1)

                def leaky_self(i, k):
                    c = 2 * i + k
                    for f in range(2):
                        dve.wait_ge(cs, 2 * c + f + 1)
                        z = ZS[k][:, f, :]
                        nc.vector.scalar_tensor_tensor(z, z, SLOPE, z, ALU.mult, ALU.max).then_inc(ls, 1)

                def leaky_edge(i, k):
                    c = 2 * i + k
                    for f in range(2):
                        dve.wait_ge(ce, 2 * c + f + 1)
                        z = ZE[k][:, f, :]
                        nc.vector.scalar_tensor_tensor(z, z, SLOPE, z, ALU.mult, ALU.max).then_inc(le, 1)
                        dve.wait_ge(le, 2 * c + f + 5)
                        dve.wait_ge(ls, 2 * c + f + 1)
                        nc.vector.tensor_tensor(z, z, ZS[k][:, f, :], ALU.subtract).then_inc(apart, 1)

                def keep(i, k):
                    c = 2 * i + k
                    dve.wait_ge(logit, c + 3)
                    nc.vector.tensor_copy(m["alpha"][:, bass.ds(c * CT, CT), :],
                                          banks[6 + k][:, 0:CT * H].rearrange("p (t h) -> p t h", h=H)).then_inc(kept, 1)

                def step(i, ahead=True, behind=True):
                    for k in range(2):
                        if ahead:
                            norm(i + 1, k)
                        leaky_self(i, k)
                    for k in range(2):
                        if ahead:
                            differ(i + 1, k)
                    for k in range(2):
                        leaky_edge(i, k)
                        if behind:
                            keep(i - 1, k)

                for k in range(2):
                    norm(0, k)
                for k in range(2):
                    differ(0, k)
                step(0, behind=False)
                with dve.Fori(1, NCH // 2 - 1) as i:
                    step(i)
                step(NCH // 2 - 1, ahead=False)
                for k in range(2):
                    keep(NCH // 2 - 1, k)

            @block.scalar
            def _(act):
                act.sem_inc(hidden, 2)
                act.sem_inc(stacked, 2)
                act.sem_inc(saved, 2)

                def norm(i, k):
                    c = 2 * i + k
                    act.wait_ge(shifted, c + 1)
                    nc.scalar.activation(HR[k][:, :, :], HR[k][:, :, :], ACT.Relu).then_inc(normed, 1)

                def save(i, k):
                    c = 2 * i + k
                    act.wait_ge(differed, c + 1)
                    nc.scalar.activation(m["edges"][:, bass.ds(c * CT, CT), 0:C], HR[k][:, :, 0:C], ACT.Copy).then_inc(saved, 1)

                def hide(i, k):
                    c = 2 * i + k
                    act.wait_ge(turned, c + 3)
                    act.wait_ge(ze, 2 * c + 2)
                    nc.scalar.activation(HC[k][:, :], banks[k][:, :], ACT.Copy).then_inc(hidden, 1)
                    nc.scalar.activation(DA[k][0:C, :], banks[k][0:C, :], ACT.Copy).then_inc(stacked, 1)

                def copy_self(i, k):
                    c = 2 * i + k
                    for f in range(2):
                        act.wait_ge(zs, 2 * c + f + 1)
                        act.wait_ge(apart, 2 * c + f + 1)
                        nc.scalar.activation(ZS[k][:, f, :], banks[2 + 2 * k + f][:, :], ACT.Identity,
                                             bias=m["eem"][:, f:f + 1]).then_inc(cs, 1)

                def copy_edge(i, k):
                    c = 2 * i + k
                    for f in range(2):
                        act.wait_ge(ze, 2 * c + f + 5)
                        act.wait_ge(logit, c + 1)
                        nc.scalar.activation(ZE[k][:, f, :], banks[2 + 2 * k + f][:, :], ACT.Copy).then_inc(ce, 1)

                def step(i, ahead=True):
                    for k in range(2):
                        if ahead:
                            norm(i + 1, k)
                        copy_self(i, k)
                    for k in range(2):
                        if ahead:
                            save(i + 1, k)
                    for k in range(2):
                        copy_edge(i, k)
                        if ahead:
                            hide(i + 1, k)

                for k in range(2):
                    norm(0, k)
                for k in range(2):
                    save(0, k)
                for k in range(2):
                    hide(0, k)
                with act.Fori(0, NCH // 2 - 1) as i:
                    step(i)
                step(NCH // 2 - 1, ahead=False)

            @block.tensor
            def _(pe):
                pe.sem_inc(turned, 2)
                pe.sem_inc(logit, 2)
                pe.sem_inc(ze, 4)

                def turn(i, k):
                    c = 2 * i + k
                    pe.wait_ge(differed, c + 1)
                    pe.wait_ge(stacked, c + 1)
                    for j in range(CT):
                        last = nc.tensor.transpose(banks[k][:, j * P:(j + 1) * P], HR[k][:, j, :], m["ident"][:, :])
                    last.then_inc(turned, 1)

                def project_self(i, k):
                    c = 2 * i + k
                    pe.wait_ge(hidden, c + 3)
                    for f in range(2):
                        w = slice(f * P, (f + 1) * P)
                        if later(i):
                            pe.wait_ge(ce, 2 * c + f - 3)
                        nc.tensor.matmul(banks[2 + 2 * k + f][:, :], m["wself"][:, w], HC[k][:, :], start=True, stop=False,
                                         skip_group_check=True).then_inc(zs, 1)

                def project_edge(i, k):
                    c = 2 * i + k
                    pe.wait_ge(stacked, c + 3)
                    pe.wait_ge(loaded[k], 16 * i + 16)
                    for f in range(2):
                        w = slice(f * P, (f + 1) * P)
                        pe.wait_ge(cs, 2 * c + f + 1)
                        nc.tensor.matmul(banks[2 + 2 * k + f][:, :], m["wedge"][:, w], DA[k][:, :], start=False, stop=True,
                                         skip_group_check=True).then_inc(ze, 1)

                def logits(i, k):
                    c = 2 * i + k
                    pe.wait_ge(apart, 2 * c + 6)
                    pe.wait_ge(kept, c + 1)
                    for j in range(CT):
                        for f in range(2):
                            last = nc.tensor.matmul(banks[6 + k][:, j * H:(j + 1) * H], ZE[k][:, f, j * P:(j + 1) * P],
                                                    m["att"][:, f, :], start=f == 0, stop=f == 1)
                    last.then_inc(logit, 1)

                def step(i, ahead=True, behind=True):
                    for k in range(2):
                        project_self(i, k)
                    for k in range(2):
                        if behind:
                            logits(i - 1, k)
                        project_edge(i, k)
                    for k in range(2):
                        if ahead:
                            turn(i + 1, k)

                for k in range(2):
                    turn(0, k)
                step(0, behind=False)
                with pe.Fori(1, NCH // 2 - 1) as i:
                    step(i)
                step(NCH // 2 - 1, ahead=False)
                for k in range(2):
                    logits(NCH // 2 - 1, k)


def gat_softmax(nc, m, b):
    stage = f"sm{b}"
    with ExitStack() as ctx:
        def rows(name):
            return ctx.enter_context(nc.sbuf_tensor(f"{stage}_{name}", [RT, RG, H, P], F32))

        L, S, U, F, B, T, X = [rows(n) for n in ("edge", "self", "both", "forward", "backward", "whole", "carried")]
        SF = ctx.enter_context(nc.sbuf_tensor(f"{stage}_tiles_forward", [H, TILES + 1], F32))
        SB = ctx.enter_context(nc.sbuf_tensor(f"{stage}_tiles_backward", [H, TILES + 1], F32))
        turned, copied, ends, carries, shifted, powers, done, back, dv = sems(
            ctx, nc, stage, "turned", "copied", "ends", "carries", "shifted", "powers", "done", "back", "dve_chain")
        banks, ident, alpha = m["bank"], m["ident"], m["alpha"]
        flat = lambda t: t[:, :, :, :].rearrange("t g h p -> t (g h p)")
        with nc.Block() as block:

            @block.tensor
            def _(pe):
                for g in range(RG):
                    for h in range(H):
                        last = nc.tensor.transpose(banks[g][0:RT, h * P:(h + 1) * P], alpha[:, g * RT:(g + 1) * RT, h], ident[:, :])
                last.then_inc(turned, 1)
                for n in range(2):
                    pe.wait_ge(ends, 2 * n + 1)
                    for g in range(RG):
                        nc.tensor.transpose(banks[4][0:H, g * RT:(g + 1) * RT], F[:, g, :, P - 1], ident[0:RT, 0:RT])
                        last = nc.tensor.transpose(banks[5][0:H, g * RT:(g + 1) * RT], B[:, g, :, 0], ident[0:RT, 0:RT])
                    last.then_inc(carries, 1)
                    pe.wait_ge(ends, 2 * n + 2)
                    for g in range(RG):
                        nc.tensor.transpose(banks[6][0:RT, g * H:(g + 1) * H], SF[:, g * RT:(g + 1) * RT], ident[0:H, 0:H])
                        last = nc.tensor.transpose(banks[7][0:RT, g * H:(g + 1) * H], SB[:, g * RT + 1:(g + 1) * RT + 1], ident[0:H, 0:H])
                    last.then_inc(carries, 1)
                pe.wait_ge(done, 1)
                for g in range(RG):
                    for h in range(H):
                        last = nc.tensor.transpose(banks[2 + g][:, h * RT:(h + 1) * RT], L[:, g, h, :], ident[0:RT, 0:RT])
                last.then_inc(back, 1)

            @block.scalar
            def _(act):
                act.wait_ge(turned, 1)
                for g in range(RG):
                    nc.scalar.activation(L[:, g, :, :], banks[g][0:RT, :].rearrange("t (h p) -> t h p", p=P),
                                         ACT.Copy).then_inc(copied, 1)
                act.wait_ge(shifted, 1)
                nc.scalar.activation(flat(S), flat(T), ACT.Exp, scale=-1.0).then_inc(powers, 1)
                act.wait_ge(shifted, 2)
                nc.scalar.activation(flat(L), flat(L), ACT.Exp).then_inc(powers, 1)
                act.wait_ge(back, 1)
                for g in range(RG):
                    nc.scalar.activation(alpha[:, g * RT:(g + 1) * RT, :].rearrange("p t h -> p h t"),
                                         banks[2 + g][:, 0:H * RT].rearrange("p (h t) -> p h t", h=H), ACT.Copy)

            @block.vector
            def _(dve):
                step = in_order(dve, dv)

                def over_destination(n, x, forward, backward, tiles_forward, tiles_backward, inside, op0, op1, mask0, mask1):
                    step(nc.vector.tensor_tensor_scan(flat(F), flat(forward), flat(x), 0.0, op0, op1))
                    nc.vector.tensor_tensor_scan(flat(B)[:, ::-1], flat(backward)[:, ::-1], flat(x)[:, ::-1],
                                                 0.0, op0, op1).then_inc(ends, 1)
                    dve.wait_ge(ends, 2 * n + 1)
                    step(nc.vector.tensor_tensor(flat(T), flat(F), flat(B), op1))
                    if inside:
                        step(nc.vector.tensor_tensor(flat(T), flat(T), flat(x), ALU.subtract))
                    dve.wait_ge(carries, 2 * n + 1)
                    step(nc.vector.tensor_tensor_scan(SF[:, 1:TILES + 1], tiles_forward[:, :], banks[4][0:H, 0:TILES], 0.0, op0, op1))
                    nc.vector.tensor_tensor_scan(SB[:, 0:TILES][:, ::-1], tiles_backward[:, :][:, ::-1],
                                                 banks[5][0:H, 0:TILES][:, ::-1], 0.0, op0, op1).then_inc(ends, 1)
                    dve.wait_ge(carries, 2 * n + 2)
                    for bank, mask in ((banks[6], mask0), (banks[7], mask1)):
                        for g in range(RG):
                            step(nc.vector.tensor_tensor(
                                X[:, g], mask[:, g, :].unsqueeze(1).to_broadcast([RT, H, P]),
                                bank[0:RT, g * H:(g + 1) * H].unsqueeze(2).to_broadcast([RT, H, P]), op0))
                        step(nc.vector.tensor_tensor(flat(T), flat(T), flat(X), op1))

                step(nc.vector.memset(SF[:, 0:1], 0.0))
                step(nc.vector.memset(SB[:, TILES:TILES + 1], 0.0))
                dve.wait_ge(copied, 2)
                step(nc.vector.tensor_scalar(flat(U), flat(L), 0.0, None, ALU.max))
                over_destination(0, U, m["nF"], m["nB"], m["nWF"], m["nWB"], False, ALU.add, ALU.max, m["nInF"], m["nInB"])
                dve.sem_inc(shifted, 1)
                nc.vector.tensor_tensor(flat(L), flat(L), flat(T), ALU.subtract).then_inc(shifted, 1)
                dve.wait_ge(powers, 2)
                over_destination(1, L, m["cF"], m["cB"], m["wF"], m["wB"], True, ALU.mult, ALU.add, m["inF"], m["inB"])
                step(nc.vector.tensor_tensor(flat(T), flat(T), flat(S), ALU.add))
                step(nc.vector.reciprocal(flat(T), flat(T)))
                nc.vector.tensor_tensor(flat(L), flat(L), flat(T), ALU.mult).then_inc(done, 1)


def gat_values(nc, m, b):
    stage = f"gv{b}"
    table = m["T"][b + 1]
    with ExitStack() as ctx:
        def bufs(name, *shape, dt=F32):
            return [ctx.enter_context(nc.sbuf_tensor(f"{stage}_{name}{k}", list(shape), dt)) for k in range(2)]

        IDX = bufs("idx", P, CT, dt=I32)
        CB = bufs("goes_on", P, CH, dt=BF16)
        W = bufs("weighted", P, CT, H, C)
        Y = bufs("summed", P, 2, CH)
        OE = bufs("out", P, CT, C)
        loaded, scattered = pair(ctx, nc, stage, "loaded"), pair(ctx, nc, stage, "scattered")
        picked, begun, weighted, started, turned, summed, mixed, out = sems(
            ctx, nc, stage, "picked", "begun", "weighted", "started", "turned", "summed", "mixed", "out")
        banks = m["bank"]
        with nc.Block() as block:

            @block.sync
            def _(sp):
                def load(i, k):
                    c = 2 * i + k
                    start = start_of(sp, i, k, CH)
                    sp.wait_ge(summed, 2 * c + 2)
                    sp.dma_start(CB[k][:, :], m["cont_row"][bass.ds(start, CH)].partition_broadcast(P)).then_inc(loaded[k], 16)

                two_by_two(sp, NCH, load)

            @block.tensor
            def _(pe):
                pe.sem_inc(turned, 2)
                pe.sem_inc(mixed, 2)

                def turn(i, k):
                    c = 2 * i + k
                    pe.wait_ge(started, c + 1)
                    pe.wait_ge(summed, 2 * c + 2)
                    for j in range(CT):
                        for f in range(2):
                            last = nc.tensor.transpose(banks[2 * k + f][:, j * P:(j + 1) * P],
                                                       W[k][:, j, 2 * f:2 * f + 2, :].rearrange("p h c -> p (h c)"), m["ident"][:, :])
                    last.then_inc(turned, 1)

                def mix(i, k):
                    c = 2 * i + k
                    pe.wait_ge(summed, 2 * c + 6)
                    pe.wait_ge(out, c + 1)
                    for j in range(CT):
                        for f in range(2):
                            last = nc.tensor.matmul(banks[4 + k][:, j * C:(j + 1) * C], Y[k][:, f, j * P:(j + 1) * P],
                                                    m["wout"][:, f, :], start=f == 0, stop=f == 1)
                    last.then_inc(mixed, 1)

                for k in range(2):
                    turn(0, k)
                with pe.Fori(0, NCH // 2 - 1) as i:
                    mix(i, 0)
                    turn(i + 1, 0)
                    mix(i, 1)
                    turn(i + 1, 1)
                for k in range(2):
                    mix(NCH // 2 - 1, k)

            @block.vector
            def _(dve):
                dve.sem_inc(summed, 4 - 1)
                dve.sem_inc(out, 2)
                nc.vector.memset(Y[1][:, :, :], 0.0).then_inc(summed, 1)

                def weigh(i, k):
                    c = 2 * i + k
                    dve.wait_ge(turned, c + 1)
                    for f in range(2):
                        e = m["edges"][:, bass.ds(c * CT + 2 * f, 2), 0:C].unsqueeze(2).to_broadcast([P, 2, H, C])
                        w = m["alpha"][:, bass.ds(c * CT + 2 * f, 2), :].unsqueeze(3).to_broadcast([P, 2, H, C])
                        nc.vector.tensor_tensor(W[k][:, 2 * f:2 * f + 2], e, w, ALU.mult).then_inc(weighted, 1)
                    dve.wait_ge(weighted, 2 * c + 2)
                    for h in range(0, H, 4):
                        e = m["edges"][:, bass.ds(c * CT, CT), C:2 * C].unsqueeze(2).to_broadcast([P, CT, H, C])
                        nc.vector.tensor_tensor(W[k][:, :, :, :], W[k][:, :, :, :], e, ALU.add).then_inc(started, 1)

                def add_up(i, k):
                    c = 2 * i + k
                    dve.wait_ge(turned, c + 3)
                    dve.wait_ge(loaded[k], 16 * i + 16)
                    dve.wait_ge(mixed, c + 1)
                    dve.wait_ge(summed, 2 * c + 4)
                    for f in range(2):
                        nc.vector.tensor_tensor_scan(Y[k][:, f, :], CB[k][:, :], banks[2 * k + f][:, :], Y[1 - k][:, f, CH - 1:CH],
                                                     ALU.mult, ALU.add).then_inc(summed, 1)

                def put_out(i, k):
                    c = 2 * i + k
                    dve.wait_ge(mixed, c + 3)
                    if later(i):
                        dve.wait_ge(scattered[k], 16 * CT * i)
                    nc.vector.tensor_tensor(OE[k][:, :, :], banks[4 + k][:, 0:CT * C].rearrange("p (t c) -> p t c", c=C),
                                            m["biasb"][:, :].unsqueeze(1).to_broadcast([P, CT, C]), ALU.add).then_inc(out, 1)

                def step(i, ahead=True):
                    for k in range(2):
                        add_up(i, k)
                        if ahead:
                            weigh(i + 1, k)
                    for k in range(2):
                        put_out(i, k)

                for k in range(2):
                    weigh(0, k)
                step(0)
                with dve.Fori(1, NCH // 2 - 1) as i:
                    step(i)
                step(NCH // 2 - 1, ahead=False)

            @block.gpsimd
            def _(pool):
                scatter_loop(nc, pool, m, table, IDX, OE, scattered, picked, begun, out)


def scatter_loop(nc, pool, m, table, IDX, OE, scattered, picked, begun, out):
    def scatter(i, k):
        c = 2 * i + k
        if later(i):
            pool.wait_ge(scattered[k], 16 * CT * i)
        nc.gpsimd.tensor_copy(IDX[k][:, :], m["sidx"][:, bass.ds(c * CT, CT)]).then_inc(picked, 1)
        pool.wait_ge(picked, c + 1)
        pool.wait_ge(out, c + 3)
        pool.sem_inc(begun, 1)
        for j in range(CT):
            pool.indirect_dma_start(table[:, :], bass.IndirectOffsetOnAxis(ap=IDX[k][:, j:j + 1], axis=0), OE[k][:, j, :], None,
                                    bounds_check=N - 1, oob_is_err=False).then_inc(scattered[k], 16)

    two_by_two(pool, NCH, scatter, peel=True)
    for k in range(2):
        pool.wait_ge(scattered[k], 16 * CT * (NCH // 2))


def node_weights(nc, a, m, keep):
    with ExitStack() as ctx:
        def kept(name, shape):
            m[name] = keep.enter_context(nc.sbuf_tensor(f"nw_{name}", shape, F32))
            return m[name]

        w1a, w1b = kept("w1a", [P, C]), kept("w1b", [P, C])
        w2a = kept("w2a", [C + 1, C + 1])
        w2b = kept("w2b", [P, P])
        b1a, b1b = kept("b1a", [C, 1]), kept("b1b", [P, 1])
        b2b = kept("b2b", [P, C])
        zeroed, loaded = sems(ctx, nc, "nw", "zeroed", "loaded")
        with nc.Block() as block:

            @block.vector
            def _(dve):
                nc.vector.memset(w2a[:, :], 0.0).then_inc(zeroed, 1)
                nc.vector.memset(w2b[:, :], 0.0).then_inc(zeroed, 1)
                dve.wait_ge(zeroed, 2)
                nc.vector.memset(w2a[C:C + 1, C:C + 1], 1.0).then_inc(zeroed, 1)

            @block.sync
            def _(sp):
                sp.wait_ge(zeroed, 3)
                loads = ((w1a[:, :], a["W1a"]), (w1b[:, :], a["W1b"]), (w2a[0:C, 0:C], a["W2a"]), (w2a[C:C + 1, 0:C], a["b2a"]),
                         (w2b[0:C, 0:C], a["W2b"]), (w2b[C:P, C:P], a["W2b"]), (b1a[:, :], a["b1a"].rearrange("a c -> c a")),
                         (b1b[0:C, :], a["b1b"].rearrange("a c -> c a")), (b1b[C:P, :], a["b1b"].rearrange("a c -> c a")),
                         (b2b[:, :], a["b2b"][0, :].partition_broadcast(P)))
                for to, of in loads:
                    sp.dma_start(to, of).then_inc(loaded, 16)
                sp.wait_ge(loaded, 16 * len(loads))


def edge_hidden(nc, a, m):
    stage = "eh"
    with ExitStack() as ctx:
        def bufs(name, *shape, dt=F32):
            return [ctx.enter_context(nc.sbuf_tensor(f"{stage}_{name}{k}", list(shape), dt)) for k in range(2)]

        G = bufs("gathered", P, CT, P)
        IDX = bufs("idx", P, CT, dt=I32)
        HC = bufs("hidden", P, CH)
        zero = ctx.enter_context(nc.sbuf_tensor(f"{stage}_zero", [P, SUP * C], F32))
        gathered, loaded = pair(ctx, nc, stage, "gathered"), pair(ctx, nc, stage, "loaded")
        picked, begun, turned, hidden, z, saved, zeroed, cleared = sems(
            ctx, nc, stage, "picked", "begun", "turned", "hidden", "z", "saved", "zeroed", "cleared")
        banks, ZE = m["bank"], m["ZE"]
        with nc.Block() as block:

            @block.gpsimd
            def _(pool):
                def gather(i, k):
                    c = 2 * i + k
                    pool.wait_ge(turned, c + 1)
                    nc.gpsimd.tensor_copy(IDX[k][:, :], m["gidx"][:, bass.ds(c * CT, CT), 0]).then_inc(picked, 1)
                    pool.wait_ge(picked, c + 1)
                    pool.sem_inc(begun, 1)
                    for j in range(CT):
                        pool.indirect_dma_start(G[k][:, j, 0:C], None, m["H2"][:, :],
                                                bass.IndirectOffsetOnAxis(ap=IDX[k][:, j:j + 1], axis=0)).then_inc(gathered[k], 16)

                two_by_two(pool, NCH, gather)

            @block.sync
            def _(sp):
                sp.wait_ge(zeroed, 1)
                for s in range(NSUP):
                    sp.dma_start(grid_view(m["MEAN"])[:, s * SUP:(s + 1) * SUP, :],
                                 zero[:, :].rearrange("p (t c) -> p t c", c=C)).then_inc(cleared, 16)
                sp.dma_start(m["MEAN"][P * GRID:N, :], zero[0:TAIL, 0:C]).then_inc(cleared, 16)

                def load(i, k):
                    c = 2 * i + k
                    start = start_of(sp, i, k, CH)
                    sp.wait_ge(z, c + 1)
                    sp.dma_start(HC[k][C:P, :], a["ea64T"][:, bass.ds(start, CH)]).then_inc(loaded[k], 16)

                two_by_two(sp, NCH, load)
                sp.wait_ge(cleared, 16 * (NSUP + 1))

            @block.tensor
            def _(pe):
                pe.sem_inc(turned, 2)
                pe.sem_inc(z, 2)

                pe.wait_ge(zeroed, 3)

                def turn(i, k):
                    c = 2 * i + k
                    pe.wait_ge(gathered[k], 16 * CT * (i + 1))
                    pe.wait_ge(hidden, c + 1)
                    for j in range(CT):
                        last = nc.tensor.transpose(banks[k][:, j * P:(j + 1) * P], G[k][:, j, :], m["ident"][:, :])
                    last.then_inc(turned, 1)

                def project(i, k):
                    c = 2 * i + k
                    pe.wait_ge(hidden, c + 3)
                    pe.wait_ge(loaded[k], 16 * i + 16)
                    pe.wait_ge(saved, c + 1)
                    nc.tensor.matmul(banks[2 + k][0:C, :], m["w1a"][:, :], HC[k][:, :], start=True, stop=True).then_inc(z, 1)

                two_by_two(pe, NCH, turn, project)

            @block.scalar
            def _(act):
                act.sem_inc(hidden, 2)
                act.sem_inc(saved, 2)

                def hide(i, k):
                    c = 2 * i + k
                    act.wait_ge(turned, c + 3)
                    act.wait_ge(z, c + 1)
                    nc.scalar.activation(HC[k][0:C, :], banks[k][0:C, :], ACT.Copy).then_inc(hidden, 1)

                def save(i, k):
                    c = 2 * i + k
                    act.wait_ge(z, c + 3)
                    nc.scalar.activation(ZE[:, bass.ds(c * CH, CH)], banks[2 + k][0:C, :], ACT.Identity,
                                         bias=m["b1a"][:, 0:1]).then_inc(saved, 1)

                two_by_two(act, NCH, hide, save)

            @block.vector
            def _(dve):
                nc.vector.memset(zero[:, :], 0.0).then_inc(zeroed, 1)
                for k in range(2):
                    nc.vector.memset(G[k][:, :, C:P], 0.0).then_inc(zeroed, 1)

                def count(i, k):
                    c = 2 * i + k
                    dve.wait_ge(saved, c + 3)
                    nc.vector.bn_stats(m["stats"][0:C, bass.ds(c, 1), :], ZE[:, bass.ds(c * WIN, WIN)])

                two_by_two(dve, NCH, count)


def edge_means(nc, m):
    stage = "em"
    with ExitStack() as ctx:
        def bufs(name, *shape, dt=F32):
            return [ctx.enter_context(nc.sbuf_tensor(f"{stage}_{name}{k}", list(shape), dt)) for k in range(2)]

        IDX = bufs("idx", P, CT, dt=I32)
        CB = bufs("goes_on", C + 1, CH, dt=BF16)
        R = bufs("hidden", C + 1, CH)
        Y = bufs("summed", C + 1, CH)
        RC = bufs("inverse", P, CT)
        OE = bufs("out", P, CT, C)
        loaded, scattered = pair(ctx, nc, stage, "loaded"), pair(ctx, nc, stage, "scattered")
        picked, begun, hidden, summed, mixed, inverse, out = sems(
            ctx, nc, stage, "picked", "begun", "hidden", "summed", "mixed", "inverse", "out")
        banks, AB = m["bank"], m["AB"]
        with nc.Block() as block:

            @block.sync
            def _(sp):
                def load(i, k):
                    c = 2 * i + k
                    start = start_of(sp, i, k, CH)
                    sp.wait_ge(summed, c + 1)
                    sp.dma_start(CB[k][:, :], m["cont_row"][bass.ds(start, CH)].partition_broadcast(C + 1)).then_inc(loaded[k], 16)

                two_by_two(sp, NCH, load)

            @block.scalar
            def _(act):
                def hide(i, k):
                    c = 2 * i + k
                    act.wait_ge(summed, c + 1)
                    nc.scalar.activation(R[k][0:C, :], m["ZE"][:, bass.ds(c * CH, CH)], ACT.Relu, bias=AB[0:C, 1:2],
                                         scale=AB[0:C, 0:1]).then_inc(hidden, 1)

                two_by_two(act, NCH, hide)

            @block.vector
            def _(dve):
                dve.sem_inc(out, 2)
                nc.vector.memset(R[0][C:C + 1, :], 1.0)
                nc.vector.memset(R[1][C:C + 1, :], 1.0).then_inc(summed, 1)
                nc.vector.memset(Y[1][:, :], 0.0).then_inc(summed, 1)

                def add_up(i, k):
                    c = 2 * i + k
                    dve.wait_ge(hidden, c + 1)
                    dve.wait_ge(loaded[k], 16 * i + 16)
                    dve.wait_ge(mixed, c + 1)
                    dve.wait_ge(summed, c + 2)
                    nc.vector.tensor_tensor_scan(Y[k][:, :], CB[k][:, :], R[k][:, :], Y[1 - k][:, CH - 1:CH],
                                                 ALU.mult, ALU.add).then_inc(summed, 1)

                def divide(i, k):
                    c = 2 * i + k
                    rows = banks[k][:, 0:CT * (C + 1)].rearrange("p (t c) -> p t c", c=C + 1)
                    dve.wait_ge(mixed, c + 3)
                    dve.wait_ge(out, c + 1)
                    nc.vector.reciprocal(RC[k][:, :], rows[:, :, C]).then_inc(inverse, 1)
                    dve.wait_ge(inverse, c + 1)
                    if later(i):
                        dve.wait_ge(scattered[k], 16 * CT * i)
                    nc.vector.tensor_tensor(OE[k][:, :, :], rows[:, :, 0:C], RC[k][:, :].unsqueeze(2).to_broadcast([P, CT, C]),
                                            ALU.mult).then_inc(out, 1)

                two_by_two(dve, NCH, add_up, divide, peel=True)

            @block.tensor
            def _(pe):
                pe.sem_inc(mixed, 2)

                def mix(i, k):
                    c = 2 * i + k
                    pe.wait_ge(summed, c + 3)
                    pe.wait_ge(out, c + 1)
                    for j in range(CT):
                        last = nc.tensor.matmul(banks[k][:, j * (C + 1):(j + 1) * (C + 1)], Y[k][:, j * P:(j + 1) * P],
                                                m["w2a"][:, :], start=True, stop=True)
                    last.then_inc(mixed, 1)

                two_by_two(pe, NCH, mix)

            @block.gpsimd
            def _(pool):
                scatter_loop(nc, pool, m, m["MEAN"], IDX, OE, scattered, picked, begun, out)


def node_hidden(nc, m):
    stage = "nh"
    with ExitStack() as ctx:
        X = [ctx.enter_context(nc.sbuf_tensor(f"{stage}_rows{k}", [P, SUP, P], F32)) for k in range(2)]
        EV = [ctx.enter_context(nc.sbuf_tensor(f"{stage}_even{k}", [P, SUB // 2 * P], F32)) for k in range(2)]
        OD = [ctx.enter_context(nc.sbuf_tensor(f"{stage}_odd{k}", [P, SUB // 2 * P], F32)) for k in range(2)]
        loaded = pair(ctx, nc, stage, "loaded")
        turned, even, odd, z, saved, counted = sems(ctx, nc, stage, "turned", "even", "odd", "z", "saved", "counted")
        banks, ZN = m["bank"], m["ZN"]
        NB = SUP // SUB
        USES = 2 * NB
        W = SUB // 2 * P

        with nc.Block() as block:

            @block.sync
            def _(sp):
                def load(i, k, tail=False):
                    start = start_of(sp, i, k, SUP)
                    sp.wait_ge(z, USES * i + k * NB + NB)
                    for n, table in enumerate((m["H2"], m["MEAN"])):
                        c = slice(n * C, (n + 1) * C)
                        if tail:
                            sp.dma_start(X[k][0:TAIL, 0, c], table[P * GRID:N, :]).then_inc(loaded[k], 16)
                        else:
                            sp.dma_start(X[k][:, :, c], grid_view(table)[:, bass.ds(start, SUP), :]).then_inc(loaded[k], 16)

                two_by_two(sp, NSUP, load, tail=True)

            @block.tensor
            def _(pe):
                pe.sem_inc(z, USES)

                def turn(i, k, q, tail):
                    u = k * NB + q
                    r = u % 2
                    if q == 0:
                        pe.wait_ge(loaded[k], 32 * i + 32)
                    pe.wait_ge(even, USES * i + u + 1)
                    pe.wait_ge(odd, USES * i + u + 1)
                    if tail:
                        last = nc.tensor.transpose(banks[2 * r][:, 0:TAIL], X[k][0:TAIL, 0, :], m["ident"][0:TAIL, 0:TAIL])
                    for j in range(0 if tail else SUB):
                        last = nc.tensor.transpose(banks[2 * r + j % 2][:, j // 2 * P:(j // 2 + 1) * P], X[k][:, q * SUB + j, :],
                                                   m["ident"][:, :])
                    last.then_inc(turned, 1)

                def project(i, k, q, tail):
                    u = k * NB + q
                    r = u % 2
                    pe.wait_ge(even, USES * i + u + 3)
                    pe.wait_ge(saved, USES * i + u + 1)
                    w = TAIL if tail else W
                    last = nc.tensor.matmul(banks[4 + r][0:C, 0:w], m["w1b"][:, :], EV[r][:, 0:w], start=True, stop=True)
                    if not tail:
                        pe.wait_ge(odd, USES * i + u + 3)
                        last = nc.tensor.matmul(banks[4 + r][C:P, 0:w], m["w1b"][:, :], OD[r][:, 0:w], start=True, stop=True)
                    last.then_inc(z, 1)

                def step(i, k, tail=False):
                    n = 1 if tail else NB
                    for q in range(n + 1):
                        if q < n:
                            turn(i, k, q, tail)
                        if q:
                            project(i, k, q - 1, tail)

                two_by_two(pe, NSUP, step, tail=True)

            @block.scalar
            def _(act):
                act.sem_inc(even, 2)
                act.sem_inc(saved, 2)

                def copy(i, k, q, tail):
                    u = k * NB + q
                    r = u % 2
                    w = TAIL if tail else W
                    act.wait_ge(turned, USES * i + u + 1)
                    act.wait_ge(z, USES * i + u - 1 + USES)
                    nc.scalar.activation(EV[r][:, 0:w], banks[2 * r][:, 0:w], ACT.Copy).then_inc(even, 1)

                def save(i, k, q, tail):
                    u = k * NB + q
                    r = u % 2
                    act.wait_ge(z, USES * i + u + 1 + USES)
                    p, w = (C, TAIL) if tail else (P, W)
                    nc.scalar.activation(ZN[0:p, bass.ds((USES * i + u) * W, w)], banks[4 + r][0:p, 0:w], ACT.Identity,
                                         bias=m["b1b"][0:p, 0:1]).then_inc(saved, 1)

                def step(i, k, tail=False):
                    n = 1 if tail else NB
                    for q in range(n + 1):
                        if q < n:
                            copy(i, k, q, tail)
                        if q:
                            save(i, k, q - 1, tail)

                two_by_two(act, NSUP, step, tail=True)

            @block.vector
            def _(dve):
                dve.sem_inc(odd, 2)

                def copy(i, k, q, tail):
                    u = k * NB + q
                    r = u % 2
                    if not tail:
                        dve.wait_ge(turned, USES * i + u + 1)
                        dve.wait_ge(z, USES * i + u - 1 + USES)
                        nc.vector.tensor_copy(OD[r][:, :], banks[2 * r + 1][:, 0:W]).then_inc(odd, 1)

                def count(i, k, q, tail):
                    u = k * NB + q
                    dve.wait_ge(saved, USES * i + u + 3)
                    if tail:
                        nc.vector.bn_stats(m["stats"][0:C, 2 * NSUB, :], ZN[0:C, NSUB * W:NSUB * W + TAIL])
                    else:
                        nc.vector.bn_stats(m["stats"][:, bass.ds(USES * i + u, 1), :], ZN[:, bass.ds((USES * i + u) * W, W)])

                def step(i, k, tail=False):
                    n = 1 if tail else NB
                    for q in range(n + 1):
                        if q < n:
                            copy(i, k, q, tail)
                        if q:
                            count(i, k, q - 1, tail)

                two_by_two(dve, NSUP, step, tail=True)


def node_out(nc, m, out_table):
    stage = "no"
    with ExitStack() as ctx:
        X = [ctx.enter_context(nc.sbuf_tensor(f"{stage}_rows{k}", [P, SUP, C], F32)) for k in range(2)]
        Y = [ctx.enter_context(nc.sbuf_tensor(f"{stage}_out{k}", [P, SUP, C], F32)) for k in range(2)]
        HC = [ctx.enter_context(nc.sbuf_tensor(f"{stage}_hidden{k}", [P, SUB // 2 * P], F32)) for k in range(4)]
        loaded, stored = pair(ctx, nc, stage, "loaded"), pair(ctx, nc, stage, "stored")
        hidden, mixed, biased, out = sems(ctx, nc, stage, "hidden", "mixed", "biased", "out")
        banks, AB, ZN = m["bank"], m["AB"], m["ZN"]
        NB = SUP // SUB
        USES = 2 * NB
        W = SUB // 2 * P

        def before(u, ring):
            return u - ring if u >= ring else u % ring + (USES - 1 - u % ring) // ring * ring - USES

        def rows(table, start, tail):
            if tail:
                return table[P * GRID:N, :].rearrange("(p t) c -> p t c", t=1)
            return grid_view(table)[:, bass.ds(start, SUP), :]

        with nc.Block() as block:

            @block.sync
            def _(sp):
                def load(i, k, tail=False):
                    p, t = (TAIL, 1) if tail else (P, SUP)
                    start = start_of(sp, i, k, SUP)
                    sp.wait_ge(out, USES * i + k * NB + NB)
                    sp.dma_start(X[k][0:p, 0:t, :], rows(m["XA"], start, tail)).then_inc(loaded[k], 16)

                two_by_two(sp, NSUP, load, tail=True)

            @block.scalar
            def _(act):
                def step(i, k, tail=False):
                    for q in range(1 if tail else NB):
                        u = k * NB + q
                        act.wait_ge(mixed, USES * i + before(u, 4) + 1 + USES)
                        p, w = (C, TAIL) if tail else (P, W)
                        nc.scalar.activation(HC[u % 4][0:p, 0:w], ZN[0:p, bass.ds((USES * i + u) * W, w)], ACT.Relu,
                                             bias=AB[0:p, 1:2], scale=AB[0:p, 0:1]).then_inc(hidden, 1)

                two_by_two(act, NSUP, step, tail=True)

            @block.tensor
            def _(pe):
                pe.sem_inc(mixed, USES)

                def step(i, k, tail=False):
                    for q in range(1 if tail else NB):
                        u = k * NB + q
                        pe.wait_ge(hidden, USES * i + u + 1)
                        pe.wait_ge(out, USES * i + before(u, 4) + 1 + USES)
                        if tail:
                            last = nc.tensor.matmul(banks[u % 4][0:TAIL, 0:C], HC[u % 4][0:C, 0:TAIL], m["w2b"][0:C, 0:C],
                                                    start=True, stop=True)
                        for j in range(0 if tail else SUB // 2):
                            last = nc.tensor.matmul(banks[u % 4][:, j * P:(j + 1) * P], HC[u % 4][:, j * P:(j + 1) * P],
                                                    m["w2b"][:, :], start=True, stop=True)
                        last.then_inc(mixed, 1)

                two_by_two(pe, NSUP, step, tail=True)

            @block.vector
            def _(dve):
                dve.sem_inc(out, USES)

                def step(i, k, tail=False):
                    if later(i):
                        dve.wait_ge(stored[k], 16 * i)
                    dve.wait_ge(biased, 2 * i + k + 1)
                    for q in range(1 if tail else NB):
                        u = k * NB + q
                        dve.wait_ge(mixed, USES * i + u + 1 + USES)
                        p, t = (TAIL, 1) if tail else (P, SUB)
                        nc.vector.tensor_tensor(
                            Y[k][0:p, q * SUB:q * SUB + t, :], banks[u % 4][0:p, 0:t * C].rearrange("p (t c) -> p t c", c=C),
                            X[k][0:p, q * SUB:q * SUB + t, :], ALU.add).then_inc(out, 1)

                two_by_two(dve, NSUP, step, tail=True, peel=True)

            @block.gpsimd
            def _(pool):
                def bias(i, k, tail=False):
                    p, t = (TAIL, 1) if tail else (P, SUP)
                    pool.wait_ge(loaded[k], 16 * i + 16)
                    nc.gpsimd.tensor_tensor(X[k][0:p, 0:t, :], X[k][0:p, 0:t, :],
                                            m["b2b"][0:p, :].unsqueeze(1).to_broadcast([p, t, C]), ALU.add).then_inc(biased, 1)

                def store(i, k, tail=False):
                    p, t = (TAIL, 1) if tail else (P, SUP)
                    start = start_of(pool, i, k, SUP)
                    pool.wait_ge(out, USES * i + k * NB + (1 if tail else NB) + USES)
                    pool.dma_start(rows(out_table, start, tail), Y[k][0:p, 0:t, :]).then_inc(stored[k], 16)

                two_by_two(pool, NSUP, bias, store, tail=True)
                for k in range(2):
                    pool.wait_ge(stored[k], 16 * (NSUP // 2 + 1))


def kernel(x, src, dst, edge_attr_16, edge_attr_64, L0_gnn_Wl, L0_gnn_Wr, L0_gnn_We, L0_gnn_att, L0_gnn_gat_bias, L0_gnn_gn_weight,
           L0_gnn_gn_bias, L0_gnn_gn_mean_scale, L1_gnn_u, L1_gnn_W1a, L1_gnn_b1a, L1_gnn_g1, L1_gnn_be1, L1_gnn_W2a, L1_gnn_b2a,
           L1_gnn_W1b, L1_gnn_b1b, L1_gnn_g2, L1_gnn_be2, L1_gnn_W2b, L1_gnn_b2b):
    import concourse.bacc as bacc
    from concourse.bass_utils import run_bass_kernel_spmd

    def padded(values, fill, before=0):
        row = np.full(EP, fill, np.int32)
        row[:before] = -1
        some = np.asarray(values)[:EP - before]
        row[before:before + some.size] = some
        return row

    def by_tile(row):
        return np.ascontiguousarray(row.reshape(TILES, P).T)

    def by_row(row):
        return np.ascontiguousarray(row.reshape(RG, RT, P).transpose(1, 0, 2))

    src, dst = np.asarray(src), np.asarray(dst)
    own, behind = padded(dst, FAR), padded(dst[1:], FAR)
    behind[E - 1:] = FAR
    ea16T = np.zeros((DE, EP), np.float32)
    ea16T[:, :E] = np.asarray(edge_attr_16).T
    ea64T = np.zeros((C, EP), np.float32)
    ea64T[:, :E] = np.asarray(edge_attr_64).T
    arrays = {
        "x": x, "src_pt": by_tile(padded(src, 0)), "dstg_pt": by_tile(padded(dst, 0)), "dst_pt": by_tile(own),
        "dnext_pt": by_tile(behind), "dprev_pt": by_tile(padded(dst, FAR, before=1)), "dst_rows": by_row(own), "dprev_rows": by_row(padded(dst, FAR, before=1)),
        "dnext_rows": by_row(behind), "ea16T": ea16T, "ea64T": ea64T,
        "Wl": L0_gnn_Wl, "Wr": L0_gnn_Wr, "We": L0_gnn_We, "att": L0_gnn_att, "gat_bias": L0_gnn_gat_bias,
        "gn_weight": L0_gnn_gn_weight, "gn_bias": L0_gnn_gn_bias, "gn_mean_scale": L0_gnn_gn_mean_scale,
        "W1a": L1_gnn_W1a, "W2a": L1_gnn_W2a, "W1b": L1_gnn_W1b, "W2b": L1_gnn_W2b,
    }
    for name, row in (("b1a", L1_gnn_b1a), ("g1", L1_gnn_g1), ("be1", L1_gnn_be1), ("b2a", L1_gnn_b2a), ("b1b", L1_gnn_b1b),
                      ("g2", L1_gnn_g2), ("be2", L1_gnn_be2), ("b2b", L1_gnn_b2b)):
        arrays[name] = np.asarray(row).reshape(1, C)
    nc = bacc.Bacc("TRN2", target_bir_lowering=False, num_devices=1)
    aps, given = {}, {}
    for name, value in arrays.items():
        value = np.ascontiguousarray(value)
        given[f"in_{name}"] = value
        aps[name] = nc.dram_tensor(f"in_{name}", value.shape, mybir.dt.from_np(value.dtype), kind="ExternalInput").ap()
    out = nc.dram_tensor("out", (N, C), F32, kind="ExternalOutput").ap()
    build(nc, aps, out)
    return run_bass_kernel_spmd(nc, [given], core_ids=[0]).results[0]["out"]
```

```python
from contextlib import ExitStack, contextmanager

import numpy as np

import concourse.bass as bass
from concourse import mybir

F32 = mybir.dt.float32
I32 = mybir.dt.int32
BF16 = mybir.dt.bfloat16
ALU = mybir.AluOpType
ACT = mybir.ActivationFunctionType
AX = mybir.AxisListType.X

N, C, H, DE, E = 50000, 64, 4, 16, 25000
NBLOCKS = 2
EPS = 1e-5
SLOPE = 0.2
P = 128
GRID = N // P
TAIL = N - P * GRID
SUP, SUB = 30, 6
NSUP, NSUB = GRID // SUP, GRID // SUB
TILES, CT = 200, 4
CH = CT * P
NCH = TILES // CT
EP = TILES * P
RG = 2
RT = TILES // RG
FAR = 1 << 20
BIG = float(2.0**100)
WIN = E // NCH


def grid_view(table):
    return table[0:P * GRID, :].rearrange("(p t) c -> p t c", p=P)


def start_of(eng, i, k, size):
    return (2 * i + k) * size if isinstance(i, int) else eng.snap((2 * i + k) * size)


def build(nc, a, out):
    with ExitStack() as ctx:
        def sb(name, shape, dt=F32):
            return ctx.enter_context(nc.sbuf_tensor(name, shape, dt))

        def dram(name, shape, dt=F32):
            return nc.dram_tensor(name, shape, dt, kind="Internal").ap()

        m = {}
        m["bank"] = [ctx.enter_context(nc.psum_tensor(f"bank{n}", [P, 512], F32)) for n in range(8)]
        m["T"] = [dram(f"table_x{n}", [N, C]) for n in range(NBLOCKS + 1)]
        m["H2"] = dram("table_h2", [N, C])
        m["XA"] = dram("table_xa", [N, C])
        m["MEAN"] = dram("table_mean", [N, C])
        m["logits_row"] = dram("logits_row", [H, EP])
        m["cont_row"] = dram("cont_row", [EP], BF16)

        m["ident"] = sb("ident", [P, P])
        m["gidx"] = sb("gidx", [P, TILES, 2], I32)
        m["sidx"] = sb("sidx", [P, TILES], I32)
        for n in ("cF", "nF", "cB", "nB"):
            m[n] = sb(n, [RT, RG, H, P], BF16)
        for n in ("inF", "nInF", "inB", "nInB"):
            m[n] = sb(n, [RT, RG, P])
        for n in ("wF", "wB", "nWF", "nWB"):
            m[n] = sb(n, [H, TILES])
        m["AB"] = sb("AB", [P, 2])
        m["ABrow"] = sb("ABrow", [P, 2, 2, C])
        m["starts"] = sb("starts", [P, TILES])
        m["stats"] = sb("stats", [P, 2 * NSUB + 1, 6])
        m["small"] = sb("small", [C, 16])

        weights = []
        for b in range(NBLOCKS):
            weights.append({
                "wself": sb(f"wself{b}", [P, H * C]),
                "wedge": sb(f"wedge{b}", [C + DE, H * C]),
                "att": sb(f"att{b}", [P, 2, H]),
                "eem": sb(f"eem{b}", [P, 2]),
                "wout": sb(f"wout{b}", [P, 2, C]),
                "wmean": sb(f"wmean{b}", [P, P]),
                "biasb": sb(f"biasb{b}", [P, C]),
            })
        m["w1a"] = sb("w1a", [P, C])
        m["w1h"], m["w1m"] = sb("w1h", [P, P]), sb("w1m", [P, P])
        m["w2a"] = sb("w2a", [C + 1, C + 1])
        m["w2b"] = sb("w2b", [P, P])
        m["b1a"], m["b1b"], m["b2b"] = sb("b1a", [C, 1]), sb("b1b", [P, 1]), sb("b2b", [P, C])

        scratch = ExitStack()
        for name, shape, dt in (
                ("pt", [P, 3, TILES], I32), ("rows", [RT, 3, RG, P], I32), ("attributes", [P, E // 8], F32),
                ("wl2", [P, NBLOCKS, H * C], F32), ("wes", [P, NBLOCKS, H * C], F32)):
            m[name] = scratch.enter_context(nc.sbuf_tensor(name, shape, dt))
        with programs(nc) as (block, held):
            zeroed, loaded = sems(held, nc, "setup", "zeroed", "loaded")
            clear_setup(nc, block, m, weights, zeroed)
            others = setup_loads(a, m, weights)
            dense_norm(nc, block, held, m, "h0", [a["x"]], None, m["T"][0], stats=True, others=(others, zeroed, loaded))
        for b in range(NBLOCKS):
            m.update(weights[b])
            with ExitStack() as w, programs(nc) as (block, held):
                m["edges"] = w.enter_context(nc.sbuf_tensor(f"edges{b}", [P, TILES, 2 * C], F32))
                m["alpha"] = w.enter_context(nc.sbuf_tensor(f"alpha{b}", [P, TILES, H], F32))
                gather_edges(nc, block, held, m, b, w, clear=b == NBLOCKS - 1)
                if b == 0:
                    with ExitStack() as parts:
                        setup_edges(nc, block, held, m, parts)
                        gat_weights(nc, block, held, m, weights, parts)
                    meet(nc, held, "setup", block.tensor, block.scalar, block.vector)
                if b:
                    table_stats(nc, block, held, m, b)
                    meet(nc, held, f"stats{b}", block.tensor, block.scalar, block.vector)
                norm_coefficients(nc, block, held, m, f"gn{b}", a["gn_weight"][b:b + 1, :], a["gn_bias"][b:b + 1, :],
                                  a["gn_mean_scale"][b:b + 1, :])
                meet(nc, held, f"norm{b}", block.tensor, block.scalar, block.vector)
                gat_base(nc, block, held, m, b)
                meet(nc, held, f"base{b}", block.tensor, block.scalar, block.vector)
                gat_logits(nc, block, held, a, m, b)
                meet(nc, held, f"logits{b}", block.tensor, block.scalar, block.vector)
                gat_softmax(nc, block, held, m, b)
                meet(nc, held, f"softmax{b}", block.sync, block.tensor, block.scalar, block.vector, block.gpsimd)
                gat_values(nc, block, held, m, b)
            if b == 0:
                scratch.close()
        with programs(nc) as (block, held):
            dense_norm(nc, block, held, m, "h2", [a["x"], m["T"][2], m["T"][0]], m["XA"], m["H2"], stats=False)
        with ExitStack() as hidden, programs(nc) as (block, held):
            m["ZE"] = hidden.enter_context(nc.sbuf_tensor("edge_z", [C, EP], F32))
            edge_hidden(nc, block, held, a, m)
            meet(nc, held, "edges", block.sync, block.tensor, block.scalar, block.vector, block.gpsimd)
            norm_coefficients(nc, block, held, m, "bn1", a["g1"], a["be1"], None, chunks=NCH)
            meet(nc, held, "norm_edges", block.sync, block.tensor, block.scalar, block.vector, block.gpsimd)
            edge_means(nc, block, held, m)
        with ExitStack() as w, programs(nc) as (block, held):
            m["ZN"] = w.enter_context(nc.sbuf_tensor("node_z", [P, NSUB * SUB // 2 * P + TAIL], F32))
            node_hidden(nc, block, held, m)
            meet(nc, held, "nodes", block.sync, block.tensor, block.scalar, block.vector)
            norm_coefficients(nc, block, held, m, "bn2", a["g2"], a["be2"], None)
            meet(nc, held, "norm_nodes", block.sync, block.tensor, block.scalar, block.vector)
            node_out(nc, block, held, m, out)


@contextmanager
def programs(nc):
    with ExitStack() as held:
        with nc.Block() as block:
            yield block, held
    nc.all_engine_barrier()


def meet(nc, held, name, *engines):
    met, = sems(held, nc, name, "met")
    for engine in engines:

        @engine
        def _(eng):
            eng.drain()
            eng.sem_inc(met, 1)
            eng.wait_ge(met, len(engines))


def sems(held, nc, stage, *names):
    made = [nc.alloc_semaphore(f"{stage}_{n}") for n in names]
    held.callback(nc.clear_and_free_semaphores, made)
    return made


def pair(held, nc, stage, name):
    return sems(held, nc, stage, f"{name}0", f"{name}1")


def in_order(eng, sem):
    n = [0]

    def step(ins):
        n[0] += 1
        ins.then_inc(sem, 1)
        eng.wait_ge(sem, n[0])

    return step


def later(i):
    return not (isinstance(i, int) and i == 0)


def two_by_two(eng, count, *parts, tail=None, peel=False):
    for part in parts if peel else ():
        for k in range(2):
            part(0, k)
    with eng.Fori(int(peel), count // 2) as i:
        for part in parts:
            for k in range(2):
                part(i, k)
    rest = [{}] * (count % 2) + ([{"tail": True}] if tail else [])
    for part in parts:
        for k, kind in enumerate(rest):
            part(count // 2, k, **kind)


def staggered(eng, count, *parts, peel=False):
    least, most = min(ahead for _, ahead in parts), max(ahead for _, ahead in parts)
    first = ((2 if peel else 0) - least + 1) // 2
    last = (count - 3 - most) // 2 + 1

    def slot(i, k):
        for part, ahead in parts:
            pairs, q = divmod(k + ahead, 2)
            if not isinstance(i, int):
                part(i + pairs if pairs else i, q)
            elif 0 <= 2 * (i + pairs) + q < count - 1:
                part(i + pairs, q)
            elif 2 * (i + pairs) + q == count - 1:
                part(i + pairs, q, tail=True)

    def pair_of_slots(i):
        for k in range(2):
            slot(i, k)

    for i in range(-most // 2, first):
        pair_of_slots(i)
    with eng.Fori(first, last) as i:
        pair_of_slots(i)
    for i in range(last, (count - least + 1) // 2):
        pair_of_slots(i)


def clear_setup(nc, block, m, weights, zeroed):
    ident = m["ident"]

    @block.gpsimd
    def _(pool):
        nc.gpsimd.memset(ident[:, :], 0.0).then_inc(zeroed, 1)
        for w in weights:
            for t in (w["wself"][:, :], w["att"][:, :, :], w["wmean"][:, :]):
                nc.gpsimd.memset(t, 0.0).then_inc(zeroed, 1)
        for n in ("w2a", "w2b", "w1h", "w1m"):
            nc.gpsimd.memset(m[n][:, :], 0.0).then_inc(zeroed, 1)
        pool.wait_ge(zeroed, 5 + 3 * NBLOCKS)
        nc.gpsimd.memset(m["w2a"][C:C + 1, C:C + 1], 1.0).then_inc(zeroed, 1)
        pool.wait_ge(zeroed, 6 + 3 * NBLOCKS)
        nc.gpsimd.affine_select(out=ident[:, :], in_=ident[:, :], compare_op=ALU.not_equal, fill=1.0,
                                base=0, pattern=[[-1, P]], channel_multiplier=1).then_inc(zeroed, 1)
        pool.wait_ge(zeroed, 7 + 3 * NBLOCKS)

    @block.tensor
    def _(pe):
        pe.wait_ge(zeroed, 7 + 3 * NBLOCKS)


def setup_loads(a, m, weights):
    loads = [(m["gidx"][:, :, :], a["gidx"]), (m["pt"][:, :, :], a["dst_pt"]), (m["rows"][:, :, :, :], a["dst_rows"])]
    for b, w in enumerate(weights):
        loads += [(w["wself"][C:P, :], a["Wr"][b]), (w["wedge"][0:C, :], a["Wl"][b]), (w["wedge"][C:C + DE, :], a["We"][b]),
                  (w["biasb"][:, :], a["gat_bias"][b, :].partition_broadcast(P))]
        for r in range(2):
            at = slice(r * C, (r + 1) * C)
            loads += [(m["wl2"][at, b, :], a["Wl"][b]),
                      (w["wout"][at, :, :], a["Wl"][b].rearrange("c (f r k) -> r c f k", r=2, k=C)[r])]
        for h in range(H):
            at = (h % 2) * C
            loads.append((w["att"][at:at + C, h // 2, h:h + 1], a["att"][b, h:h + 1, :].rearrange("a c -> c a")))
    for s in range(8):
        at = slice(s * DE, (s + 1) * DE)
        loads += [(m["attributes"][at, :], a["ea16T"][:, s * (E // 8):(s + 1) * (E // 8)]),
                  (m["wes"][at, :, :], a["We"].rearrange("b d n -> d b n"))]
    loads += [(m["w1a"][:, :], a["W1a"]), (m["w1h"][0:C, 0:C], a["W1b"][0:C, :]), (m["w1h"][C:P, C:P], a["W1b"][0:C, :]),
              (m["w1m"][0:C, 0:C], a["W1b"][C:P, :]), (m["w1m"][C:P, C:P], a["W1b"][C:P, :]),
              (m["w2a"][0:C, 0:C], a["W2a"]), (m["w2a"][C:C + 1, 0:C], a["b2a"]),
              (m["w2b"][0:C, 0:C], a["W2b"]), (m["w2b"][C:P, C:P], a["W2b"]), (m["b1a"][:, :], a["b1a"].rearrange("a c -> c a")),
              (m["b1b"][0:C, :], a["b1b"].rearrange("a c -> c a")), (m["b1b"][C:P, :], a["b1b"].rearrange("a c -> c a")),
              (m["b2b"][:, :], a["b2b"][0, :].partition_broadcast(P))]
    return loads


def setup_edges(nc, block, held, m, ctx):
    made, stored, dv, tr, tc = sems(held, nc, "edges", "made", "stored", "dve_chain", "turned", "copied")
    pt, rows = m["pt"], m["rows"]
    ptf = ctx.enter_context(nc.sbuf_tensor("ptf", [P, 4, TILES], F32))
    rowf = ctx.enter_context(nc.sbuf_tensor("rowf", [RT, 3, RG, P], F32))
    cont = ctx.enter_context(nc.sbuf_tensor("cont", [RT, 4, RG, P], F32))
    controw = ctx.enter_context(nc.sbuf_tensor("controw", [RT, RG, P], BF16))
    edgeF = ctx.enter_context(nc.sbuf_tensor("edgeF", [RT, RG, P], F32))
    edgeB = ctx.enter_context(nc.sbuf_tensor("edgeB", [RT, RG, P], F32))
    wcol = ctx.enter_context(nc.sbuf_tensor("wcol", [RT, 2, RG, H], F32))
    ident = m["ident"]
    bank = m["bank"][0]

    @block.scalar
    def _(act):
        act.wait_ge(made, 1)
        for g in range(RG):
            act.dma_start(m["cont_row"].rearrange("(g t p) -> g t p", g=RG, p=P)[g], controw[:, g, :]).then_inc(stored, 16)
        act.wait_ge(stored, 16 * RG)

    @block.vector
    def _(dve):
        step = in_order(dve, dv)
        step(nc.vector.tensor_copy(ptf[:, 0:2, :], pt[:, 0:2, :]))
        step(nc.vector.tensor_copy(ptf[:, 3, :], pt[:, 2, :]))
        step(nc.vector.tensor_tensor(m["starts"][:, :], ptf[:, 0, :], ptf[:, 3, :], ALU.not_equal))
        step(nc.vector.tensor_tensor(ptf[:, 2, :], ptf[:, 0, :], ptf[:, 1, :], ALU.is_equal))
        step(nc.vector.scalar_tensor_tensor(ptf[:, 1, :], ptf[:, 2, :], float(FAR), ptf[:, 0, :], ALU.mult, ALU.add))
        step(nc.vector.tensor_copy(m["sidx"][:, :], ptf[:, 1, :]))
        step(nc.vector.tensor_copy(rowf[:, :, :, :], rows[:, :, :, :]))
        step(nc.vector.tensor_tensor(cont[:, 0], rowf[:, 0], rowf[:, 2], ALU.is_equal))
        step(nc.vector.tensor_tensor(cont[:, 1], rowf[:, 0], rowf[:, 1], ALU.is_equal))
        nc.vector.tensor_copy(controw[:, :, :], cont[:, 0]).then_inc(made, 1)
        step(nc.vector.tensor_copy(cont[:, 2:4], cont[:, 0:2]))
        step(nc.vector.memset(cont[:, 2, :, 0:1], 0.0))
        step(nc.vector.memset(cont[:, 3, :, P - 1:P], 0.0))
        step(nc.vector.memset(edgeF[:, :, :], 0.0))
        step(nc.vector.memset(edgeB[:, :, :], 0.0))
        step(nc.vector.tensor_copy(edgeF[:, :, 0:1], cont[:, 0, :, 0:1]))
        step(nc.vector.tensor_copy(edgeB[:, :, P - 1:P], cont[:, 1, :, P - 1:P]))
        flat = lambda t: t.rearrange("t g p -> t (g p)")
        step(nc.vector.tensor_tensor_scan(flat(m["inF"][:, :, :]), flat(cont[:, 2]), flat(edgeF[:, :, :]),
                                          0.0, ALU.mult, ALU.add))
        step(nc.vector.tensor_tensor_scan(flat(m["inB"][:, :, :])[:, ::-1], flat(cont[:, 3])[:, ::-1],
                                          flat(edgeB[:, :, :])[:, ::-1], 0.0, ALU.mult, ALU.add))
        for to, of in (("nInF", m["inF"]), ("nInB", m["inB"])):
            step(nc.vector.tensor_scalar(m[to][:, :, :], of[:, :, :], -1.0, BIG, ALU.add, ALU.mult))
        for n, (c, neg) in enumerate((("cF", "nF"), ("cB", "nB"))):
            for h in range(H):
                step(nc.vector.tensor_copy(m[c][:, :, h, :], cont[:, 2 + n]))
            step(nc.vector.tensor_scalar(m[neg][:, :, :, :], m[c][:, :, :, :], -1.0, BIG, ALU.add, ALU.mult))
        step(nc.vector.tensor_copy(wcol[:, 0], m["inF"][:, :, P - 1:P].to_broadcast([RT, RG, H])))
        nc.vector.tensor_copy(wcol[:, 1], m["inB"][:, :, 0:1].to_broadcast([RT, RG, H])).then_inc(tr, 1)
        dve.wait_ge(tc, 1)
        step(nc.vector.tensor_copy(m["wF"][:, :], bank[0:H, 0:TILES]))
        step(nc.vector.tensor_copy(m["wB"][:, :], bank[0:H, TILES:2 * TILES]))
        step(nc.vector.tensor_scalar(m["nWF"][:, :], m["wF"][:, :], -1.0, BIG, ALU.add, ALU.mult))
        step(nc.vector.tensor_scalar(m["nWB"][:, :], m["wB"][:, :], -1.0, BIG, ALU.add, ALU.mult))

    @block.tensor
    def _(pe):
        pe.wait_ge(tr, 1)
        for n in range(2):
            for g in range(RG):
                at = n * TILES + g * RT
                last = nc.tensor.transpose(bank[0:H, at:at + RT], wcol[:, n, g, :], ident[0:RT, 0:RT])
        last.then_inc(tc, 1)


def dense_norm(nc, block, held, m, stage, sources, sum_table, table, stats, others=None):
    with ExitStack() as ctx:
        def bufs(name, *shape):
            return [ctx.enter_context(nc.sbuf_tensor(f"{stage}_{name}{k}", [P, *shape], F32)) for k in range(2)]

        n_in = len(sources)
        X, CEN, SQ, HN, OUT = [bufs(n, SUP, C) for n in ("sum", "centred", "squares", "scaled", "out")]
        MORE = [bufs(f"more{q}", SUP, C) for q in range(1, n_in)]
        R = bufs("rows", 4, SUP)
        added, meaned, centred, squared, varied, rooted, inverted, scaled, normed, turned, counted, begun = sems(
            held, nc, stage, "added", "meaned", "centred", "squared", "varied", "rooted", "inverted", "scaled", "normed", "turned",
            "counted", "begun")
        loaded, stored, sum_stored = [pair(held, nc, stage, n) for n in ("loaded", "stored", "sum_stored")]
        banks = m["bank"]
        NB = SUP // SUB
        USES = 2 * NB

        def shape(tail):
            return (TAIL, 1) if tail else (P, SUP)

        def of(table, start, tail):
            if tail:
                return table[P * GRID:N, :].rearrange("(p t) c -> p t c", t=1)
            return grid_view(table)[:, bass.ds(start, SUP), :]


        def load(sp, i, k, tail=False):
            p, t = shape(tail)
            start = start_of(sp, i, k, SUP)
            sp.wait_ge(centred, 2 * i + k + 1)
            if sum_table is not None and later(i):
                sp.sem_inc(begun, 1)
                sp.wait_ge(sum_stored[k], 16 * i)
            for q, source in enumerate(sources):
                to = X[k] if q == 0 else MORE[q - 1][k]
                sp.dma_start(to[0:p, 0:t, :], of(source, start, tail)).then_inc(loaded[k], 16)

        @block.sync
        def _(sp):
            for k in range(2):
                load(sp, 0, k)
            if others:
                loads, zeroed, other_loaded = others
                sp.wait_ge(zeroed, 6 + 3 * NBLOCKS)
                few = -(-len(loads) // (NSUP - 2))
                for s in range(2, NSUP):
                    for to, of in loads[(s - 2) * few:(s - 1) * few]:
                        sp.dma_start(to, of).then_inc(other_loaded, 16)
                    load(sp, s // 2, s % 2)
                sp.wait_ge(other_loaded, 16 * len(loads))
            else:
                with sp.Fori(1, NSUP // 2) as i:
                    for k in range(2):
                        load(sp, i, k)
                load(sp, NSUP // 2, 0)
            load(sp, NSUP // 2, 1, tail=True)
            for k in range(2):
                sp.wait_ge(stored[k], 16 * (NSUP // 2 + 1))
                if sum_table is not None:
                    sp.wait_ge(sum_stored[k], 16 * (NSUP // 2 + 1))

        @block.vector
        def _(dve):
            dve.sem_inc(counted, USES)

            def mean(i, k, tail=False):
                p, t = shape(tail)
                s = 2 * i + k
                x, r = X[k][0:p, 0:t, :], R[k]
                dve.wait_ge(loaded[k], 16 * n_in * (i + 1))
                for q in range(1, n_in):
                    nc.vector.tensor_tensor(x, x, MORE[q - 1][k][0:p, 0:t, :], ALU.add).then_inc(added, 1)
                    dve.wait_ge(added, (n_in - 1) * s + q)
                dve.wait_ge(centred, s + 1)
                nc.vector.tensor_reduce(r[0:p, 0, 0:t], x, AX, ALU.add).then_inc(meaned, 1)
                dve.wait_ge(meaned, 2 * s + 1)
                nc.vector.tensor_scalar(r[0:p, 1, 0:t], r[0:p, 0, 0:t], -1.0 / C, None, ALU.mult).then_inc(meaned, 1)

            def variance(i, k, tail=False):
                p, t = shape(tail)
                s = 2 * i + k
                r = R[k]
                dve.wait_ge(squared, s + 1)
                nc.vector.tensor_reduce(r[0:p, 2, 0:t], SQ[k][0:p, 0:t, :], AX, ALU.add).then_inc(varied, 1)
                dve.wait_ge(varied, 2 * s + 1)
                nc.vector.tensor_scalar(r[0:p, 2, 0:t], r[0:p, 2, 0:t], 1.0 / C, EPS, ALU.mult, ALU.add).then_inc(varied, 1)

            def invert(i, k, tail=False):
                p, t = shape(tail)
                s = 2 * i + k
                dve.wait_ge(rooted, s + 1)
                nc.vector.reciprocal(R[k][0:p, 3, 0:t], R[k][0:p, 3, 0:t]).then_inc(inverted, 1)

            def count(i, k, tail=False):
                for q in range(1 if tail else NB):
                    u = k * NB + q
                    dve.wait_ge(turned, USES * i + u + 1)
                    if tail:
                        nc.vector.bn_stats(m["stats"][0:C, 2 * NSUB, :], banks[u % 8][0:C, 0:TAIL]).then_inc(counted, 1)
                    else:
                        nc.vector.bn_stats(m["stats"][:, bass.ds((2 * i + k) * NB + q, 1), :],
                                           banks[u % 8][:, 0:SUB // 2 * P]).then_inc(counted, 1)

            staggered(dve, NSUP + 1, (mean, 2), (variance, 1), (invert, 1), *([(count, -1)] if stats else []))

        @block.gpsimd
        def _(pool):
            pool.sem_inc(centred, 2)
            pool.sem_inc(scaled, 2)

            def centre(i, k, tail=False):
                p, t = shape(tail)
                s = 2 * i + k
                pool.wait_ge(meaned, 2 * s + 2)
                pool.wait_ge(scaled, s + 1)
                nc.gpsimd.tensor_tensor(CEN[k][0:p, 0:t, :], X[k][0:p, 0:t, :],
                                        R[k][0:p, 1, 0:t].unsqueeze(2).to_broadcast([p, t, C]), ALU.add).then_inc(centred, 1)

            def scale(i, k, tail=False):
                p, t = shape(tail)
                s = 2 * i + k
                pool.wait_ge(centred, s + 3)
                pool.wait_ge(inverted, s + 1)
                pool.wait_ge(normed, s + 1)
                nc.gpsimd.tensor_tensor(HN[k][0:p, 0:t, :], CEN[k][0:p, 0:t, :],
                                        R[k][0:p, 3, 0:t].unsqueeze(2).to_broadcast([p, t, C]), ALU.mult).then_inc(scaled, 1)

            staggered(pool, NSUP + 1, (scale, 0), (centre, 2))

        @block.scalar
        def _(act):
            act.sem_inc(normed, 2)

            def square(i, k, tail=False):
                p, t = shape(tail)
                s = 2 * i + k
                start = start_of(act, i, k, SUP)
                act.wait_ge(centred, s + 3)
                nc.scalar.activation(SQ[k][0:p, 0:t, :], CEN[k][0:p, 0:t, :], ACT.Square).then_inc(squared, 1)
                if sum_table is not None:
                    act.dma_start(of(sum_table, start, tail), X[k][0:p, 0:t, :]).then_inc(sum_stored[k], 16)

            def root(i, k, tail=False):
                p, t = shape(tail)
                s = 2 * i + k
                act.wait_ge(varied, 2 * s + 2)
                nc.scalar.activation(R[k][0:p, 3, 0:t], R[k][0:p, 2, 0:t], ACT.Sqrt).then_inc(rooted, 1)

            def rectify(i, k, tail=False):
                p, t = shape(tail)
                s = 2 * i + k
                start = start_of(act, i, k, SUP)
                act.wait_ge(scaled, s + 3)
                if later(i):
                    act.wait_ge(stored[k], 16 * i)
                if stats:
                    act.wait_ge(counted, USES * i + NB * (k + 1))
                nc.scalar.activation(OUT[k][0:p, 0:t, :], HN[k][0:p, 0:t, :], ACT.Relu).then_inc(normed, 1)
                act.wait_ge(normed, s + 3)
                act.dma_start(of(table, start, tail), OUT[k][0:p, 0:t, :]).then_inc(stored[k], 16)

            staggered(act, NSUP + 1, (square, 1), (rectify, -1), (root, 1), peel=True)

        @block.tensor
        def _(pe):
            def turn(i, k, tail=False):
                pe.wait_ge(normed, 2 * i + k + 3)
                for q in range(1 if tail else NB):
                    u = k * NB + q
                    before = u - 8 if u >= 8 else u + 8 - USES if u + 8 < USES else u - USES
                    pe.wait_ge(counted, USES * i + before + 1 + USES)
                    if tail:
                        last = nc.tensor.transpose(banks[u % 8][0:C, 0:TAIL], OUT[k][0:TAIL, 0, :], m["ident"][0:TAIL, 0:TAIL])
                    for j in range(0 if tail else SUB // 2):
                        two = OUT[k][:, q * SUB + 2 * j:q * SUB + 2 * j + 2, :].rearrange("p t c -> p (t c)")
                        last = nc.tensor.transpose(banks[u % 8][:, j * P:(j + 1) * P], two, m["ident"][:, :])
                    last.then_inc(turned, 1)

            if stats:
                two_by_two(pe, NSUP, turn, tail=True)


def table_stats(nc, block, held, m, b):
    stage = f"ts{b}"
    table = m["T"][b]
    with ExitStack() as ctx:
        X = [ctx.enter_context(nc.sbuf_tensor(f"{stage}_rows{k}", [P, SUP, C], F32)) for k in range(2)]
        loaded = pair(held, nc, stage, "loaded")
        turned, counted = sems(held, nc, stage, "turned", "counted")
        banks = m["bank"]
        NB = SUP // SUB
        USES = 2 * NB

        @block.scalar
        def _(act):
            def load(i, k, tail=False):
                start = start_of(act, i, k, SUP)
                act.wait_ge(counted, USES * i + k * NB + NB)
                if tail:
                    act.dma_start(X[k][0:TAIL, 0, :], table[P * GRID:N, :]).then_inc(loaded[k], 16)
                else:
                    act.dma_start(X[k][:, :, :], grid_view(table)[:, bass.ds(start, SUP), :]).then_inc(loaded[k], 16)

            two_by_two(act, NSUP, load, tail=True)

        @block.tensor
        def _(pe):
            def turn(i, k, tail=False):
                pe.wait_ge(loaded[k], 16 * i + 16)
                for q in range(1 if tail else NB):
                    u = k * NB + q
                    before = u - 8 if u >= 8 else u + 8 - USES if u + 8 < USES else u - USES
                    pe.wait_ge(counted, USES * i + before + 1 + USES)
                    if tail:
                        last = nc.tensor.transpose(banks[u % 8][0:C, 0:TAIL], X[k][0:TAIL, 0, :], m["ident"][0:TAIL, 0:TAIL])
                    for j in range(0 if tail else SUB // 2):
                        two = X[k][:, q * SUB + 2 * j:q * SUB + 2 * j + 2, :].rearrange("p t c -> p (t c)")
                        last = nc.tensor.transpose(banks[u % 8][:, j * P:(j + 1) * P], two, m["ident"][:, :])
                    last.then_inc(turned, 1)

            two_by_two(pe, NSUP, turn, tail=True)

        @block.vector
        def _(dve):
            dve.sem_inc(counted, USES)

            def count(i, k, tail=False):
                for q in range(1 if tail else NB):
                    u = k * NB + q
                    dve.wait_ge(turned, USES * i + u + 1)
                    if tail:
                        nc.vector.bn_stats(m["stats"][0:C, 2 * NSUB, :], banks[u % 8][0:C, 0:TAIL]).then_inc(counted, 1)
                    else:
                        nc.vector.bn_stats(m["stats"][:, bass.ds((2 * i + k) * NB + q, 1), :],
                                           banks[u % 8][:, 0:SUB // 2 * P]).then_inc(counted, 1)

            two_by_two(dve, NSUP, count, tail=True)


def norm_coefficients(nc, block, held, m, stage, weight, bias, mean_scale, chunks=None):
    with ExitStack() as ctx:
        moved, loaded, varied, rooted, made, spread, dv = sems(
            held, nc, stage, "moved", "loaded", "varied", "rooted", "made", "spread", "dve_chain")
        v = m["small"]
        stats, AB = m["stats"], m["AB"]
        wide = ctx.enter_context(nc.sbuf_tensor(f"{stage}_wide", [C, 2, P], F32))
        widened, rowed = sems(held, nc, stage, "widened", "rowed")

        @block.tensor
        def _(pe):
            if mean_scale is not None:
                pe.wait_ge(widened, 1)
                for n in range(2):
                    for k in range(2):
                        last = nc.tensor.matmul(m["bank"][0][:, (2 * n + k) * C:(2 * n + k + 1) * C], wide[:, n, :],
                                                m["ident"][0:C, 0:C], start=True, stop=True)
                last.then_inc(rowed, 1)

        @block.scalar
        def _(act):
            act.dma_start(v[:, 2:3], weight.rearrange("a c -> c a")).then_inc(loaded, 16)
            act.dma_start(v[:, 3:4], bias.rearrange("a c -> c a")).then_inc(loaded, 16)
            if mean_scale is not None:
                act.dma_start(v[:, 4:5], mean_scale.rearrange("a c -> c a")).then_inc(loaded, 16)
            if chunks is None:
                act.dma_start(stats[0:C, NSUB:2 * NSUB, :], stats[C:P, 0:NSUB, :]).then_inc(moved, 16)
            act.wait_ge(varied, 1)
            nc.scalar.activation(v[:, 7:8], v[:, 6:7], ACT.Sqrt).then_inc(rooted, 1)
            act.wait_ge(made, 1)
            act.dma_start(AB[C:P, :], AB[0:C, :]).then_inc(spread, 16)
            act.wait_ge(spread, 16)

        @block.vector
        def _(dve):
            step = in_order(dve, dv)
            if chunks is None:
                dve.wait_ge(moved, 16)
            step(nc.vector.bn_aggr(v[:, 0:2], stats[0:C, 0:chunks or 2 * NSUB + 1, :].rearrange("c n s -> c (n s)")))
            dve.wait_ge(loaded, 16 * (2 if mean_scale is None else 3))
            mean, var, w, b, scaled, t = (v[:, n:n + 1] for n in (0, 1, 2, 3, 5, 6))
            if mean_scale is None:
                step(nc.vector.tensor_copy(scaled, mean))
            else:
                step(nc.vector.tensor_tensor(scaled, mean, v[:, 4:5], ALU.mult))
                step(nc.vector.tensor_tensor(t, mean, scaled, ALU.subtract))
                step(nc.vector.tensor_tensor(t, t, t, ALU.mult))
                step(nc.vector.tensor_tensor(var, var, t, ALU.add))
            nc.vector.tensor_scalar(t, var, EPS, None, ALU.add).then_inc(varied, 1)
            dve.wait_ge(rooted, 1)
            step(nc.vector.reciprocal(t, v[:, 7:8]))
            step(nc.vector.tensor_tensor(AB[0:C, 0:1], t, w, ALU.mult))
            step(nc.vector.tensor_tensor(t, scaled, AB[0:C, 0:1], ALU.mult))
            nc.vector.tensor_tensor(AB[0:C, 1:2], b, t, ALU.subtract).then_inc(made, 1)
            if mean_scale is not None:
                dve.wait_ge(made, 1)
                nc.vector.tensor_copy(wide[:, :, :], AB[0:C, :].unsqueeze(2).to_broadcast([C, 2, P])).then_inc(widened, 1)
                dve.wait_ge(rowed, 1)
                nc.vector.tensor_copy(m["ABrow"][:, :, :, :].rearrange("p n k c -> p (n k c)"), m["bank"][0][:, 0:4 * C])


def gat_weights(nc, block, held, m, weights, ctx):
    esum = ctx.enter_context(nc.sbuf_tensor("attributes_mean", [P, 1], F32))
    dv, ready, summed = sems(held, nc, "weights", "dve_chain", "ready", "summed")
    bank, wl2, wes = m["bank"][1], m["wl2"], m["wes"]

    @block.vector
    def _(dve):
        step = in_order(dve, dv)
        step(nc.vector.tensor_reduce(esum[:, :], m["attributes"][:, :], AX, ALU.add))
        nc.vector.tensor_scalar(esum[:, :], esum[:, :], 1.0 / E, None, ALU.mult).then_inc(ready, 1)
        for b, w in enumerate(weights):
            wself, wmean, wout = w["wself"], w["wmean"], w["wout"]
            step(nc.vector.tensor_tensor(wself[C:P, :], wself[C:P, :], wl2[C:P, b, :], ALU.add))
            for at in (0, C):
                r = slice(at, at + C)
                to = wmean[r, at:at + C]
                step(nc.vector.tensor_tensor(to, wl2[r, b, 0:C], wl2[r, b, C:2 * C], ALU.add))
                for h in range(2, H):
                    step(nc.vector.tensor_tensor(to, to, wl2[r, b, h * C:(h + 1) * C], ALU.add))
                step(nc.vector.tensor_scalar(to, to, 1.0 / H, None, ALU.mult))
            step(nc.vector.tensor_scalar(wout[:, :, :], wout[:, :, :], 1.0 / H, None, ALU.mult))
        dve.wait_ge(summed, 1)
        for b, w in enumerate(weights):
            step(nc.vector.tensor_copy(w["eem"][:, :], bank[:, 2 * b:2 * b + 2]))

    @block.tensor
    def _(pe):
        pe.wait_ge(ready, 1)
        for b in range(NBLOCKS):
            for f in range(2):
                last = nc.tensor.matmul(bank[:, 2 * b + f:2 * b + f + 1], wes[:, b, f * P:(f + 1) * P], esum[:, :],
                                        start=True, stop=True)
        last.then_inc(summed, 1)


def gat_base(nc, block, held, m, b):
    stage = f"gb{b}"
    source, table = m["T"][b], m["T"][b + 1]
    with ExitStack() as ctx:
        X = [ctx.enter_context(nc.sbuf_tensor(f"{stage}_rows{k}", [P, SUP, C], F32)) for k in range(2)]
        Y = [ctx.enter_context(nc.sbuf_tensor(f"{stage}_next{k}", [P, SUP, C], F32)) for k in range(2)]
        HC = [ctx.enter_context(nc.sbuf_tensor(f"{stage}_hidden{k}", [P, SUB // 2 * P], F32)) for k in range(4)]
        loaded, stored = pair(held, nc, stage, "loaded"), pair(held, nc, stage, "stored")
        turned, hidden, mixed, out = sems(held, nc, stage, "turned", "hidden", "mixed", "out")
        banks, AB = m["bank"], m["AB"]
        NB = SUP // SUB
        USES = 2 * NB
        W = SUB // 2 * P

        def before(u, ring):
            return u - ring if u >= ring else u % ring + (USES - 1 - u % ring) // ring * ring - USES


        @block.tensor
        def _(pe):
            pe.sem_inc(mixed, USES)

            def turn(i, k, q, tail):
                u = k * NB + q
                if q == 0:
                    pe.wait_ge(loaded[k], 16 * i + 16)
                pe.wait_ge(hidden, USES * i + before(u, 4) + 1 + USES)
                if tail:
                    last = nc.tensor.transpose(banks[u % 4][0:C, 0:TAIL], X[k][0:TAIL, 0, :], m["ident"][0:TAIL, 0:TAIL])
                for j in range(0 if tail else SUB // 2):
                    two = X[k][:, q * SUB + 2 * j:q * SUB + 2 * j + 2, :].rearrange("p t c -> p (t c)")
                    last = nc.tensor.transpose(banks[u % 4][:, j * P:(j + 1) * P], two, m["ident"][:, :])
                last.then_inc(turned, 1)

            def mix(i, k, q, tail):
                u = k * NB + q
                pe.wait_ge(hidden, USES * i + u + 1 + USES)
                pe.wait_ge(out, USES * i + before(u, 4) + 1 + USES)
                if tail:
                    last = nc.tensor.matmul(banks[4 + u % 4][0:TAIL, 0:C], HC[u % 4][0:C, 0:TAIL], m["wmean"][0:C, 0:C],
                                            start=True, stop=True)
                for j in range(0 if tail else SUB // 2):
                    last = nc.tensor.matmul(banks[4 + u % 4][:, j * P:(j + 1) * P], HC[u % 4][:, j * P:(j + 1) * P],
                                            m["wmean"][:, :], start=True, stop=True)
                last.then_inc(mixed, 1)

            def step(i, k, tail=False):
                n = 1 if tail else NB
                for q in range(n + 2):
                    if q < n:
                        turn(i, k, q, tail)
                    if q >= 2:
                        mix(i, k, q - 2, tail)

            two_by_two(pe, NSUP, step, tail=True)

        @block.scalar
        def _(act):
            act.sem_inc(hidden, USES)

            def step(i, k, tail=False):
                for q in range(1 if tail else NB):
                    u = k * NB + q
                    act.wait_ge(turned, USES * i + u + 1)
                    act.wait_ge(mixed, USES * i + before(u, 4) + 1 + USES)
                    p, w = (C, TAIL) if tail else (P, W)
                    nc.scalar.activation(HC[u % 4][0:p, 0:w], banks[u % 4][0:p, 0:w], ACT.Relu, bias=AB[0:p, 1:2],
                                         scale=AB[0:p, 0:1]).then_inc(hidden, 1)

            def store(i, k, tail=False):
                n = 1 if tail else NB
                start = start_of(act, i, k, SUP)
                act.wait_ge(out, USES * i + k * NB + n + USES)
                if tail:
                    act.dma_start(table[P * GRID:N, :], Y[k][0:TAIL, 0, :]).then_inc(stored[k], 16)
                else:
                    act.dma_start(grid_view(table)[:, bass.ds(start, SUP), :], Y[k][:, :, :]).then_inc(stored[k], 16)

            def load(i, k, tail=False):
                start = start_of(act, i, k, SUP)
                act.wait_ge(hidden, USES * i + k * NB + NB)
                if tail:
                    act.dma_start(X[k][0:TAIL, 0, :], source[P * GRID:N, :]).then_inc(loaded[k], 16)
                else:
                    act.dma_start(X[k][:, :, :], grid_view(source)[:, bass.ds(start, SUP), :]).then_inc(loaded[k], 16)

            def pair_of_steps(i, last=False):
                for k in range(2):
                    step(i, k)
                    load(i + 1, k, tail=last and k == 1)
                for k in range(2):
                    store(i, k)

            for k in range(2):
                load(0, k)
            with act.Fori(0, NSUP // 2 - 1) as i:
                pair_of_steps(i)
            pair_of_steps(NSUP // 2 - 1, last=True)
            for k in range(2):
                step(NSUP // 2, k, tail=k == 1)
            for k in range(2):
                store(NSUP // 2, k, tail=k == 1)
            for k in range(2):
                act.wait_ge(stored[k], 16 * (NSUP // 2 + 1))

        @block.vector
        def _(dve):
            dve.sem_inc(out, USES)

            def step(i, k, tail=False):
                if later(i):
                    dve.wait_ge(stored[k], 16 * i)
                for q in range(1 if tail else NB):
                    u = k * NB + q
                    dve.wait_ge(mixed, USES * i + u + 1 + USES)
                    p, t = (TAIL, 1) if tail else (P, SUB)
                    nc.vector.tensor_tensor(
                        Y[k][0:p, q * SUB:q * SUB + t, :], banks[4 + u % 4][0:p, 0:t * C].rearrange("p (t c) -> p t c", c=C),
                        m["biasb"][0:p, :].unsqueeze(1).to_broadcast([p, t, C]), ALU.add).then_inc(out, 1)

            two_by_two(dve, NSUP, step, tail=True, peel=True)


def gather_edges(nc, block, held, m, b, ctx, clear):
    stage = f"ge{b}"
    table = m["T"][b]
    IDX = [ctx.enter_context(nc.sbuf_tensor(f"{stage}_idx{k}", [P, CT, 2], I32)) for k in range(2)]
    G = [ctx.enter_context(nc.sbuf_tensor(f"{stage}_gathered{k}", [P, CT, 2 * C], F32)) for k in range(2)]
    gathered = pair(held, nc, stage, "gathered")
    picked, begun = sems(held, nc, stage, "picked", "begun")
    m["landed"] = landed = pair(held, nc, stage, "landed")
    if clear:
        COLS = -(-GRID // (NCH // 2 + 1))
        zero = ctx.enter_context(nc.sbuf_tensor("zero_rows", [P, COLS, C], F32))
        zeroed, cleared = sems(held, nc, "clear", "zeroed", "cleared")

        @block.vector
        def _(dve):
            nc.vector.memset(zero[:, :, :], 0.0).then_inc(zeroed, 1)

    @block.gpsimd
    def _(pool):
        def gather(i, k):
            c = 2 * i + k
            if later(i):
                pool.wait_ge(landed[k], 16 * i)
            nc.gpsimd.tensor_copy(IDX[k][:, :, :], m["gidx"][:, bass.ds(c * CT, CT), :]).then_inc(picked, 1)
            pool.wait_ge(picked, c + 1)
            pool.sem_inc(begun, 1)
            for j in range(CT):
                for side in range(2):
                    pool.indirect_dma_start(G[k][:, j, side * C:(side + 1) * C], None, table[:, :],
                                            bass.IndirectOffsetOnAxis(ap=IDX[k][:, j, side:side + 1], axis=0)
                                            ).then_inc(gathered[k], 16)

        two_by_two(pool, NCH, gather, peel=True)

    @block.sync
    def _(sp):
        def land(i, k):
            start = start_of(sp, i, k, CT)
            sp.wait_ge(gathered[k], 16 * 2 * CT * (i + 1))
            sp.dma_start(m["edges"][:, bass.ds(start, CT), :], G[k][:, :, :]).then_inc(landed[k], 16)

        if clear:
            sp.wait_ge(zeroed, 1)
        with sp.Fori(0, NCH // 2) as i:
            for k in range(2):
                land(i, k)
            if clear:
                sp.dma_start(grid_view(m["MEAN"])[:, bass.ds(i * COLS, COLS), :], zero[:, :, :]).then_inc(cleared, 16)
        if clear:
            rest = NCH // 2 * COLS
            sp.dma_start(grid_view(m["MEAN"])[:, rest:GRID, :], zero[:, 0:GRID - rest, :]).then_inc(cleared, 16)
            sp.dma_start(m["MEAN"][P * GRID:N, :], zero[0:TAIL, 0, :]).then_inc(cleared, 16)
            sp.wait_ge(cleared, 16 * (NCH // 2 + 2))


def gat_logits(nc, block, held, a, m, b):
    stage = f"gl{b}"
    with ExitStack() as ctx:
        def bufs(name, *shape, dt=F32):
            return [ctx.enter_context(nc.sbuf_tensor(f"{stage}_{name}{k}", list(shape), dt)) for k in range(2)]

        HR = bufs("rows", P, CT, 2 * C)
        HC = bufs("channels", P, CH)
        DA = bufs("difference", C + DE, CH)
        ZS = bufs("z_self", P, 2, CH)
        ZE = bufs("z_edge", P, 2, CH)
        LR = bufs("logits_row", H, CH)
        loaded, stored = pair(held, nc, stage, "loaded"), pair(held, nc, stage, "stored")
        scaled, shifted, normed, differed, saved, parted, turned, hidden, stacked = sems(
            held, nc, stage, "scaled", "shifted", "normed", "differed", "saved", "parted", "turned", "hidden", "stacked")
        zs, ze, cs, ce, ls, le, apart, logit, kept = sems(
            held, nc, stage, "z_self", "z_edge", "copied_self", "copied_edge", "leaky_self", "leaky_edge", "apart", "logits", "kept")
        banks = m["bank"]

        @block.vector
        def _(dve):
            dve.sem_inc(le, 4)
            dve.sem_inc(apart, 4)
            dve.sem_inc(parted, 2)
            ab = [m["ABrow"][:, n].rearrange("p k c -> p (k c)").unsqueeze(1).to_broadcast([P, CT, 2 * C]) for n in range(2)]

            def norm(i, k):
                c = 2 * i + k
                dve.wait_ge(m["landed"][k], 16 * (i + 1))
                dve.wait_ge(turned, c + 1)
                dve.wait_ge(saved, c + 1)
                dve.wait_ge(parted, c + 1)
                nc.vector.tensor_tensor(HR[k][:, :, :], m["edges"][:, bass.ds(c * CT, CT), :], ab[0], ALU.mult).then_inc(scaled, 1)
                dve.wait_ge(scaled, c + 1)
                nc.vector.tensor_tensor(HR[k][:, :, :], HR[k][:, :, :], ab[1], ALU.add).then_inc(shifted, 1)

            def differ(i, k):
                c = 2 * i + k
                dve.wait_ge(normed, c + 1)
                nc.vector.tensor_tensor(HR[k][:, :, 0:C], HR[k][:, :, 0:C], HR[k][:, :, C:2 * C], ALU.subtract).then_inc(differed, 1)
                nc.vector.tensor_tensor(m["edges"][:, bass.ds(c * CT, CT), C:2 * C], HR[k][:, :, C:2 * C],
                                        m["starts"][:, bass.ds(c * CT, CT)].unsqueeze(2).to_broadcast([P, CT, C]),
                                        ALU.mult).then_inc(parted, 1)

            def leaky_self(i, k):
                c = 2 * i + k
                for f in range(2):
                    dve.wait_ge(cs, 2 * c + f + 1)
                    z = ZS[k][:, f, :]
                    nc.vector.scalar_tensor_tensor(z, z, SLOPE, z, ALU.mult, ALU.max).then_inc(ls, 1)

            def leaky_edge(i, k):
                c = 2 * i + k
                for f in range(2):
                    dve.wait_ge(ce, 2 * c + f + 1)
                    z = ZE[k][:, f, :]
                    nc.vector.scalar_tensor_tensor(z, z, SLOPE, z, ALU.mult, ALU.max).then_inc(le, 1)
                    dve.wait_ge(le, 2 * c + f + 5)
                    dve.wait_ge(ls, 2 * c + f + 1)
                    nc.vector.tensor_tensor(z, z, ZS[k][:, f, :], ALU.subtract).then_inc(apart, 1)

            def step(i, norms=True, parts=True):
                if parts:
                    for k in range(2):
                        differ(i + 1, k)
                for k in range(2):
                    leaky_self(i, k)
                if norms:
                    for k in range(2):
                        norm(i + 2, k)
                for k in range(2):
                    leaky_edge(i, k)

            for part, i in ((norm, 0), (differ, 0), (norm, 1)):
                for k in range(2):
                    part(i, k)
            with dve.Fori(0, NCH // 2 - 2) as i:
                step(i)
            step(NCH // 2 - 2, norms=False)
            step(NCH // 2 - 1, norms=False, parts=False)

        @block.scalar
        def _(act):
            act.sem_inc(hidden, 2)
            act.sem_inc(stacked, 2)
            act.sem_inc(saved, 2)
            act.sem_inc(kept, 2)

            def norm(i, k):
                c = 2 * i + k
                act.wait_ge(shifted, c + 1)
                nc.scalar.activation(HR[k][:, :, :], HR[k][:, :, :], ACT.Relu).then_inc(normed, 1)

            def save(i, k):
                c = 2 * i + k
                act.wait_ge(differed, c + 1)
                nc.scalar.activation(m["edges"][:, bass.ds(c * CT, CT), 0:C], HR[k][:, :, 0:C], ACT.Copy).then_inc(saved, 1)

            def hide(i, k):
                c = 2 * i + k
                act.wait_ge(turned, c + 3)
                act.wait_ge(zs, 2 * c + 2)
                nc.scalar.activation(HC[k][:, :], banks[k][:, :], ACT.Copy).then_inc(hidden, 1)

            def stack(i, k):
                c = 2 * i + k
                start = start_of(act, i, k, CH)
                act.wait_ge(ze, 2 * c + 2)
                act.dma_start(DA[k][C:C + DE, :], a["ea16T"][:, bass.ds(start, CH)]).then_inc(loaded[k], 16)
                nc.scalar.activation(DA[k][0:C, :], banks[k][0:C, :], ACT.Copy).then_inc(stacked, 1)

            def copy_self(i, k):
                c = 2 * i + k
                for f in range(2):
                    act.wait_ge(zs, 2 * c + f + 5)
                    act.wait_ge(apart, 2 * c + f + 1)
                    nc.scalar.activation(ZS[k][:, f, :], banks[2 + 2 * k + f][:, :], ACT.Identity,
                                         bias=m["eem"][:, f:f + 1]).then_inc(cs, 1)

            def copy_edge(i, k):
                c = 2 * i + k
                for f in range(2):
                    act.wait_ge(ze, 2 * c + f + 5)
                    act.wait_ge(logit, c + 1)
                    nc.scalar.activation(ZE[k][:, f, :], banks[2 + 2 * k + f][:, :], ACT.Copy).then_inc(ce, 1)

            def keep(i, k):
                c = 2 * i + k
                start = start_of(act, i, k, CH)
                act.wait_ge(logit, c + 3)
                if later(i):
                    act.wait_ge(stored[k], 16 * i)
                nc.scalar.activation(LR[k][:, :], banks[6 + k][0:H, :], ACT.Copy).then_inc(kept, 1)
                act.wait_ge(kept, c + 3)
                act.dma_start(m["logits_row"][:, bass.ds(start, CH)], LR[k][:, :]).then_inc(stored[k], 16)

            def step(i, norms=True, parts=True, logits=True):
                for k in range(2):
                    copy_self(i, k)
                if parts:
                    for part in (save, hide):
                        for k in range(2):
                            part(i + 1, k)
                for k in range(2):
                    copy_edge(i, k)
                    if norms:
                        norm(i + 2, k)
                    if parts:
                        stack(i + 1, k)
                    if logits:
                        keep(i - 1, k)

            for part, i in ((norm, 0), (save, 0), (hide, 0), (stack, 0), (norm, 1)):
                for k in range(2):
                    part(i, k)
            step(0, logits=False)
            step(1)
            with act.Fori(2, NCH // 2 - 2) as i:
                step(i)
            step(NCH // 2 - 2, norms=False)
            step(NCH // 2 - 1, norms=False, parts=False)
            for k in range(2):
                keep(NCH // 2 - 1, k)
            for k in range(2):
                act.wait_ge(stored[k], 16 * (NCH // 2))

        @block.tensor
        def _(pe):
            pe.sem_inc(turned, 2)
            pe.sem_inc(logit, 2)
            pe.sem_inc(ze, 4)
            pe.sem_inc(zs, 4)

            def turn(i, k):
                c = 2 * i + k
                pe.wait_ge(differed, c + 1)
                pe.wait_ge(stacked, c + 1)
                pe.wait_ge(hidden, c + 1)
                for j in range(CT):
                    last = nc.tensor.transpose(banks[k][:, j * P:(j + 1) * P], HR[k][:, j, :], m["ident"][:, :])
                last.then_inc(turned, 1)

            def project_self(i, k):
                c = 2 * i + k
                pe.wait_ge(hidden, c + 3)
                for f in range(2):
                    w = slice(f * P, (f + 1) * P)
                    if later(i):
                        pe.wait_ge(ce, 2 * c + f - 3)
                    nc.tensor.matmul(banks[2 + 2 * k + f][:, :], m["wself"][:, w], HC[k][:, :], start=True, stop=False,
                                     skip_group_check=True).then_inc(zs, 1)

            def project_edge(i, k):
                c = 2 * i + k
                pe.wait_ge(stacked, c + 3)
                pe.wait_ge(loaded[k], 16 * i + 16)
                for f in range(2):
                    w = slice(f * P, (f + 1) * P)
                    pe.wait_ge(cs, 2 * c + f + 1)
                    nc.tensor.matmul(banks[2 + 2 * k + f][:, :], m["wedge"][:, w], DA[k][:, :], start=False, stop=True,
                                     skip_group_check=True).then_inc(ze, 1)

            def logits(i, k):
                c = 2 * i + k
                pe.wait_ge(apart, 2 * c + 6)
                pe.wait_ge(kept, c + 1)
                for f in range(2):
                    last = nc.tensor.matmul(banks[6 + k][0:H, :], m["att"][:, f, :], ZE[k][:, f, :], start=f == 0, stop=f == 1)
                last.then_inc(logit, 1)

            def step(i, ahead=True, behind=True):
                for k in range(2):
                    project_self(i, k)
                for k in range(2):
                    if behind:
                        logits(i - 1, k)
                for k in range(2):
                    if ahead:
                        turn(i + 1, k)
                for k in range(2):
                    project_edge(i, k)

            for k in range(2):
                turn(0, k)
            step(0, behind=False)
            with pe.Fori(1, NCH // 2 - 1) as i:
                step(i)
            step(NCH // 2 - 1, ahead=False)
            for k in range(2):
                logits(NCH // 2 - 1, k)


def gat_softmax(nc, block, held, m, b):
    stage = f"sm{b}"
    with ExitStack() as ctx:
        def rows(name):
            return ctx.enter_context(nc.sbuf_tensor(f"{stage}_{name}", [RT, RG, H, P], F32))

        L, S, U, F, B, T, X = [rows(n) for n in ("edge", "self", "both", "forward", "backward", "whole", "carried")]
        SF = ctx.enter_context(nc.sbuf_tensor(f"{stage}_tiles_forward", [H, TILES + 1], F32))
        SB = ctx.enter_context(nc.sbuf_tensor(f"{stage}_tiles_backward", [H, TILES + 1], F32))
        loaded, ends, carries, shifted, powers, done, back, dv = sems(
            held, nc, stage, "loaded", "ends", "carries", "shifted", "powers", "done", "back", "dve_chain")
        banks, ident, alpha = m["bank"], m["ident"], m["alpha"]
        flat = lambda t: t[:, :, :, :].rearrange("t g h p -> t (g h p)")

        @block.tensor
        def _(pe):
            for n in range(2):
                pe.wait_ge(ends, 2 * n + 1)
                for g in range(RG):
                    nc.tensor.transpose(banks[4][0:H, g * RT:(g + 1) * RT], F[:, g, :, P - 1], ident[0:RT, 0:RT])
                    last = nc.tensor.transpose(banks[5][0:H, g * RT:(g + 1) * RT], B[:, g, :, 0], ident[0:RT, 0:RT])
                last.then_inc(carries, 1)
                pe.wait_ge(ends, 2 * n + 2)
                for g in range(RG):
                    nc.tensor.transpose(banks[6][0:RT, g * H:(g + 1) * H], SF[:, g * RT:(g + 1) * RT], ident[0:H, 0:H])
                    last = nc.tensor.transpose(banks[7][0:RT, g * H:(g + 1) * H], SB[:, g * RT + 1:(g + 1) * RT + 1], ident[0:H, 0:H])
                last.then_inc(carries, 1)
            pe.wait_ge(done, 1)
            for g in range(RG):
                for h in range(H):
                    last = nc.tensor.transpose(banks[2 + g][:, h * RT:(h + 1) * RT], L[:, g, h, :], ident[0:RT, 0:RT])
            last.then_inc(back, 1)

        @block.scalar
        def _(act):
            for g in range(RG):
                act.dma_start(L[:, g, :, :], m["logits_row"][:, g * RT * P:(g + 1) * RT * P].rearrange("h (t p) -> t h p", p=P)
                              ).then_inc(loaded, 16)
            act.wait_ge(shifted, 1)
            nc.scalar.activation(flat(S), flat(T), ACT.Exp, scale=-1.0).then_inc(powers, 1)
            act.wait_ge(shifted, 2)
            nc.scalar.activation(flat(L), flat(L), ACT.Exp).then_inc(powers, 1)
            act.wait_ge(back, 1)
            for g in range(RG):
                nc.scalar.activation(alpha[:, g * RT:(g + 1) * RT, :].rearrange("p t h -> p h t"),
                                     banks[2 + g][:, 0:H * RT].rearrange("p (h t) -> p h t", h=H), ACT.Copy)

        @block.vector
        def _(dve):
            step = in_order(dve, dv)

            def over_destination(n, x, forward, backward, tiles_forward, tiles_backward, inside, op0, op1, mask0, mask1):
                step(nc.vector.tensor_tensor_scan(flat(F), flat(forward), flat(x), 0.0, op0, op1))
                nc.vector.tensor_tensor_scan(flat(B)[:, ::-1], flat(backward)[:, ::-1], flat(x)[:, ::-1],
                                             0.0, op0, op1).then_inc(ends, 1)
                dve.wait_ge(ends, 2 * n + 1)
                step(nc.vector.tensor_tensor(flat(T), flat(F), flat(B), op1))
                if inside:
                    step(nc.vector.tensor_tensor(flat(T), flat(T), flat(x), ALU.subtract))
                dve.wait_ge(carries, 2 * n + 1)
                step(nc.vector.tensor_tensor_scan(SF[:, 1:TILES + 1], tiles_forward[:, :], banks[4][0:H, 0:TILES], 0.0, op0, op1))
                nc.vector.tensor_tensor_scan(SB[:, 0:TILES][:, ::-1], tiles_backward[:, :][:, ::-1],
                                             banks[5][0:H, 0:TILES][:, ::-1], 0.0, op0, op1).then_inc(ends, 1)
                dve.wait_ge(carries, 2 * n + 2)
                for bank, mask in ((banks[6], mask0), (banks[7], mask1)):
                    for g in range(RG):
                        step(nc.vector.tensor_tensor(
                            X[:, g], mask[:, g, :].unsqueeze(1).to_broadcast([RT, H, P]),
                            bank[0:RT, g * H:(g + 1) * H].unsqueeze(2).to_broadcast([RT, H, P]), op0))
                    step(nc.vector.tensor_tensor(flat(T), flat(T), flat(X), op1))

            step(nc.vector.memset(SF[:, 0:1], 0.0))
            step(nc.vector.memset(SB[:, TILES:TILES + 1], 0.0))
            dve.wait_ge(loaded, 16 * RG)
            step(nc.vector.tensor_scalar(flat(U), flat(L), 0.0, None, ALU.max))
            over_destination(0, U, m["nF"], m["nB"], m["nWF"], m["nWB"], False, ALU.add, ALU.max, m["nInF"], m["nInB"])
            dve.sem_inc(shifted, 1)
            nc.vector.tensor_tensor(flat(L), flat(L), flat(T), ALU.subtract).then_inc(shifted, 1)
            dve.wait_ge(powers, 2)
            over_destination(1, L, m["cF"], m["cB"], m["wF"], m["wB"], True, ALU.mult, ALU.add, m["inF"], m["inB"])
            step(nc.vector.tensor_tensor(flat(T), flat(T), flat(S), ALU.add))
            step(nc.vector.reciprocal(flat(T), flat(T)))
            nc.vector.tensor_tensor(flat(L), flat(L), flat(T), ALU.mult).then_inc(done, 1)


def gat_values(nc, block, held, m, b):
    stage = f"gv{b}"
    table = m["T"][b + 1]
    with ExitStack() as ctx:
        def bufs(name, *shape, dt=F32):
            return [ctx.enter_context(nc.sbuf_tensor(f"{stage}_{name}{k}", list(shape), dt)) for k in range(2)]

        IDX = bufs("idx", P, CT, dt=I32)
        CB = bufs("goes_on", P, CH, dt=BF16)
        W = bufs("weighted", P, CT, H, C)
        Y = bufs("summed", P, 2, CH)
        OE = bufs("out", P, CT, C)
        loaded, scattered = pair(held, nc, stage, "loaded"), pair(held, nc, stage, "scattered")
        picked, begun, weighted, started, turned, summed, mixed, out = sems(
            held, nc, stage, "picked", "begun", "weighted", "started", "turned", "summed", "mixed", "out")
        banks = m["bank"]

        @block.sync
        def _(sp):
            def load(i, k):
                c = 2 * i + k
                start = start_of(sp, i, k, CH)
                sp.wait_ge(summed, 2 * c + 2)
                sp.dma_start(CB[k][:, :], m["cont_row"][bass.ds(start, CH)].partition_broadcast(P)).then_inc(loaded[k], 16)

            two_by_two(sp, NCH, load)

        @block.tensor
        def _(pe):
            pe.sem_inc(turned, 2)
            pe.sem_inc(mixed, 2)

            def turn(i, k):
                c = 2 * i + k
                pe.wait_ge(started, c + 1)
                pe.wait_ge(summed, 2 * c + 2)
                for j in range(CT):
                    for f in range(2):
                        last = nc.tensor.transpose(banks[2 * k + f][:, j * P:(j + 1) * P],
                                                   W[k][:, j, 2 * f:2 * f + 2, :].rearrange("p h c -> p (h c)"), m["ident"][:, :])
                last.then_inc(turned, 1)

            def mix(i, k):
                c = 2 * i + k
                pe.wait_ge(summed, 2 * c + 6)
                pe.wait_ge(out, c + 1)
                for j in range(CT):
                    for f in range(2):
                        last = nc.tensor.matmul(banks[4 + k][:, j * C:(j + 1) * C], Y[k][:, f, j * P:(j + 1) * P],
                                                m["wout"][:, f, :], start=f == 0, stop=f == 1)
                last.then_inc(mixed, 1)

            for k in range(2):
                turn(0, k)
            with pe.Fori(0, NCH // 2 - 1) as i:
                mix(i, 0)
                turn(i + 1, 0)
                mix(i, 1)
                turn(i + 1, 1)
            for k in range(2):
                mix(NCH // 2 - 1, k)

        @block.vector
        def _(dve):
            dve.sem_inc(summed, 4 - 1)
            dve.sem_inc(out, 2)
            nc.vector.memset(Y[1][:, :, :], 0.0).then_inc(summed, 1)

            def weigh(i, k):
                c = 2 * i + k
                dve.wait_ge(turned, c + 1)
                for f in range(2):
                    e = m["edges"][:, bass.ds(c * CT + 2 * f, 2), 0:C].unsqueeze(2).to_broadcast([P, 2, H, C])
                    w = m["alpha"][:, bass.ds(c * CT + 2 * f, 2), :].unsqueeze(3).to_broadcast([P, 2, H, C])
                    nc.vector.tensor_tensor(W[k][:, 2 * f:2 * f + 2], e, w, ALU.mult).then_inc(weighted, 1)
                dve.wait_ge(weighted, 2 * c + 2)
                e = m["edges"][:, bass.ds(c * CT, CT), C:2 * C].unsqueeze(2).to_broadcast([P, CT, H, C])
                nc.vector.tensor_tensor(W[k][:, :, :, :], W[k][:, :, :, :], e, ALU.add).then_inc(started, 1)

            def add_up(i, k):
                c = 2 * i + k
                dve.wait_ge(turned, c + 3)
                dve.wait_ge(loaded[k], 16 * i + 16)
                dve.wait_ge(mixed, c + 1)
                dve.wait_ge(summed, 2 * c + 4)
                for f in range(2):
                    nc.vector.tensor_tensor_scan(Y[k][:, f, :], CB[k][:, :], banks[2 * k + f][:, :], Y[1 - k][:, f, CH - 1:CH],
                                                 ALU.mult, ALU.add).then_inc(summed, 1)

            def put_out(i, k):
                c = 2 * i + k
                dve.wait_ge(mixed, c + 3)
                if later(i):
                    dve.wait_ge(scattered[k], 16 * CT * i)
                nc.vector.tensor_tensor(OE[k][:, :, :], banks[4 + k][:, 0:CT * C].rearrange("p (t c) -> p t c", c=C),
                                        m["biasb"][:, :].unsqueeze(1).to_broadcast([P, CT, C]), ALU.add).then_inc(out, 1)

            def step(i, ahead=True, behind=True):
                add_up(i, 0)
                if behind:
                    put_out(i - 1, 1)
                if ahead:
                    weigh(i + 1, 0)
                add_up(i, 1)
                put_out(i, 0)
                if ahead:
                    weigh(i + 1, 1)

            for k in range(2):
                weigh(0, k)
            step(0, behind=False)
            step(1)
            with dve.Fori(2, NCH // 2 - 1) as i:
                step(i)
            step(NCH // 2 - 1, ahead=False)
            put_out(NCH // 2 - 1, 1)

        @block.gpsimd
        def _(pool):
            scatter_loop(nc, pool, m, table, IDX, OE, scattered, picked, begun, out)


def scatter_loop(nc, pool, m, table, IDX, OE, scattered, picked, begun, out):
    def scatter(i, k):
        c = 2 * i + k
        if later(i):
            pool.wait_ge(scattered[k], 16 * CT * i)
        nc.gpsimd.tensor_copy(IDX[k][:, :], m["sidx"][:, bass.ds(c * CT, CT)]).then_inc(picked, 1)
        pool.wait_ge(picked, c + 1)
        pool.wait_ge(out, c + 3)
        pool.sem_inc(begun, 1)
        for j in range(CT):
            pool.indirect_dma_start(table[:, :], bass.IndirectOffsetOnAxis(ap=IDX[k][:, j:j + 1], axis=0), OE[k][:, j, :], None,
                                    bounds_check=N - 1, oob_is_err=False).then_inc(scattered[k], 16)

    two_by_two(pool, NCH, scatter, peel=True)
    for k in range(2):
        pool.wait_ge(scattered[k], 16 * CT * (NCH // 2))


def edge_hidden(nc, block, held, a, m):
    stage = "eh"
    with ExitStack() as ctx:
        def bufs(name, *shape, dt=F32):
            return [ctx.enter_context(nc.sbuf_tensor(f"{stage}_{name}{k}", list(shape), dt)) for k in range(2)]

        G = bufs("gathered", P, CT, P)
        IDX = bufs("idx", P, CT, dt=I32)
        HC = bufs("hidden", P, CH)
        gathered, loaded = pair(held, nc, stage, "gathered"), pair(held, nc, stage, "loaded")
        picked, begun, turned, hidden, z, saved, zeroed = sems(
            held, nc, stage, "picked", "begun", "turned", "hidden", "z", "saved", "zeroed")
        banks, ZE = m["bank"], m["ZE"]

        @block.gpsimd
        def _(pool):
            def gather(i, k):
                c = 2 * i + k
                pool.wait_ge(turned, c + 1)
                nc.gpsimd.tensor_copy(IDX[k][:, :], m["gidx"][:, bass.ds(c * CT, CT), 0]).then_inc(picked, 1)
                pool.wait_ge(picked, c + 1)
                pool.sem_inc(begun, 1)
                for j in range(CT):
                    pool.indirect_dma_start(G[k][:, j, 0:C], None, m["H2"][:, :],
                                            bass.IndirectOffsetOnAxis(ap=IDX[k][:, j:j + 1], axis=0)).then_inc(gathered[k], 16)

            two_by_two(pool, NCH, gather)

        @block.sync
        def _(sp):
            def load(i, k):
                c = 2 * i + k
                start = start_of(sp, i, k, CH)
                sp.wait_ge(z, c + 1)
                sp.dma_start(HC[k][C:P, :], a["ea64T"][:, bass.ds(start, CH)]).then_inc(loaded[k], 16)

            two_by_two(sp, NCH, load)

        @block.tensor
        def _(pe):
            pe.sem_inc(turned, 2)
            pe.sem_inc(z, 2)

            pe.wait_ge(zeroed, 2)

            def turn(i, k):
                c = 2 * i + k
                pe.wait_ge(gathered[k], 16 * CT * (i + 1))
                pe.wait_ge(hidden, c + 1)
                for j in range(CT):
                    last = nc.tensor.transpose(banks[k][:, j * P:(j + 1) * P], G[k][:, j, :], m["ident"][:, :])
                last.then_inc(turned, 1)

            def project(i, k):
                c = 2 * i + k
                pe.wait_ge(hidden, c + 3)
                pe.wait_ge(loaded[k], 16 * i + 16)
                pe.wait_ge(saved, c + 1)
                nc.tensor.matmul(banks[2 + k][0:C, :], m["w1a"][:, :], HC[k][:, :], start=True, stop=True).then_inc(z, 1)

            two_by_two(pe, NCH, turn, project)

        @block.scalar
        def _(act):
            act.sem_inc(hidden, 2)
            act.sem_inc(saved, 2)

            def hide(i, k):
                c = 2 * i + k
                act.wait_ge(turned, c + 3)
                act.wait_ge(z, c + 1)
                nc.scalar.activation(HC[k][0:C, :], banks[k][0:C, :], ACT.Copy).then_inc(hidden, 1)

            def save(i, k):
                c = 2 * i + k
                act.wait_ge(z, c + 3)
                nc.scalar.activation(ZE[:, bass.ds(c * CH, CH)], banks[2 + k][0:C, :], ACT.Identity,
                                     bias=m["b1a"][:, 0:1]).then_inc(saved, 1)

            two_by_two(act, NCH, hide, save)

        @block.vector
        def _(dve):
            for k in range(2):
                nc.vector.memset(G[k][:, :, C:P], 0.0).then_inc(zeroed, 1)

            def count(i, k):
                c = 2 * i + k
                dve.wait_ge(saved, c + 3)
                nc.vector.bn_stats(m["stats"][0:C, bass.ds(c, 1), :], ZE[:, bass.ds(c * WIN, WIN)])

            two_by_two(dve, NCH, count)


def edge_means(nc, block, held, m):
    stage = "em"
    with ExitStack() as ctx:
        def bufs(name, *shape, dt=F32):
            return [ctx.enter_context(nc.sbuf_tensor(f"{stage}_{name}{k}", list(shape), dt)) for k in range(2)]

        IDX = bufs("idx", P, CT, dt=I32)
        CB = bufs("goes_on", C + 1, CH, dt=BF16)
        R = bufs("hidden", C + 1, CH)
        Y = bufs("summed", C + 1, CH)
        RC = bufs("inverse", P, CT)
        OE = bufs("out", P, CT, C)
        loaded, scattered = pair(held, nc, stage, "loaded"), pair(held, nc, stage, "scattered")
        picked, begun, hidden, summed, mixed, inverse, out = sems(
            held, nc, stage, "picked", "begun", "hidden", "summed", "mixed", "inverse", "out")
        banks, AB = m["bank"], m["AB"]

        @block.sync
        def _(sp):
            def load(i, k):
                c = 2 * i + k
                start = start_of(sp, i, k, CH)
                sp.wait_ge(summed, c + 1)
                sp.dma_start(CB[k][:, :], m["cont_row"][bass.ds(start, CH)].partition_broadcast(C + 1)).then_inc(loaded[k], 16)

            two_by_two(sp, NCH, load)

        @block.scalar
        def _(act):
            def hide(i, k):
                c = 2 * i + k
                act.wait_ge(summed, c + 1)
                nc.scalar.activation(R[k][0:C, :], m["ZE"][:, bass.ds(c * CH, CH)], ACT.Relu, bias=AB[0:C, 1:2],
                                     scale=AB[0:C, 0:1]).then_inc(hidden, 1)

            two_by_two(act, NCH, hide)

        @block.vector
        def _(dve):
            dve.sem_inc(out, 2)
            nc.vector.memset(R[0][C:C + 1, :], 1.0)
            nc.vector.memset(R[1][C:C + 1, :], 1.0).then_inc(summed, 1)
            nc.vector.memset(Y[1][:, :], 0.0).then_inc(summed, 1)

            def add_up(i, k):
                c = 2 * i + k
                dve.wait_ge(hidden, c + 1)
                dve.wait_ge(loaded[k], 16 * i + 16)
                dve.wait_ge(mixed, c + 1)
                dve.wait_ge(summed, c + 2)
                nc.vector.tensor_tensor_scan(Y[k][:, :], CB[k][:, :], R[k][:, :], Y[1 - k][:, CH - 1:CH],
                                             ALU.mult, ALU.add).then_inc(summed, 1)

            def divide(i, k):
                c = 2 * i + k
                rows = banks[k][:, 0:CT * (C + 1)].rearrange("p (t c) -> p t c", c=C + 1)
                dve.wait_ge(mixed, c + 3)
                dve.wait_ge(out, c + 1)
                nc.vector.reciprocal(RC[k][:, :], rows[:, :, C]).then_inc(inverse, 1)
                dve.wait_ge(inverse, c + 1)
                if later(i):
                    dve.wait_ge(scattered[k], 16 * CT * i)
                nc.vector.tensor_tensor(OE[k][:, :, :], rows[:, :, 0:C], RC[k][:, :].unsqueeze(2).to_broadcast([P, CT, C]),
                                        ALU.mult).then_inc(out, 1)

            two_by_two(dve, NCH, add_up, divide, peel=True)

        @block.tensor
        def _(pe):
            pe.sem_inc(mixed, 2)

            def mix(i, k):
                c = 2 * i + k
                pe.wait_ge(summed, c + 3)
                pe.wait_ge(out, c + 1)
                for j in range(CT):
                    last = nc.tensor.matmul(banks[k][:, j * (C + 1):(j + 1) * (C + 1)], Y[k][:, j * P:(j + 1) * P],
                                            m["w2a"][:, :], start=True, stop=True)
                last.then_inc(mixed, 1)

            two_by_two(pe, NCH, mix)

        @block.gpsimd
        def _(pool):
            scatter_loop(nc, pool, m, m["MEAN"], IDX, OE, scattered, picked, begun, out)


def node_hidden(nc, block, held, m):
    stage = "nh"
    with ExitStack() as ctx:
        X = [[ctx.enter_context(nc.sbuf_tensor(f"{stage}_{n}_rows{k}", [P, SUP, C], F32)) for k in range(2)] for n in ("h", "mean")]
        HC = [ctx.enter_context(nc.sbuf_tensor(f"{stage}_hidden{k}", [P, SUB // 2 * P], F32)) for k in range(2)]
        MC = [ctx.enter_context(nc.sbuf_tensor(f"{stage}_means{k}", [P, SUB // 2 * P], F32)) for k in range(2)]
        loaded = pair(held, nc, stage, "loaded")
        turned, hidden, means, z, saved = sems(held, nc, stage, "turned", "hidden", "means", "z", "saved")
        banks, ZN = m["bank"], m["ZN"]
        NB = SUP // SUB
        USES = 2 * NB
        W = SUB // 2 * P


        @block.sync
        def _(sp):
            def load(i, k, tail=False):
                start = start_of(sp, i, k, SUP)
                sp.wait_ge(z, USES * i + k * NB + NB)
                for n, table in enumerate((m["H2"], m["MEAN"])):
                    if tail:
                        sp.dma_start(X[n][k][0:TAIL, 0, :], table[P * GRID:N, :]).then_inc(loaded[k], 16)
                    else:
                        sp.dma_start(X[n][k][:, :, :], grid_view(table)[:, bass.ds(start, SUP), :]).then_inc(loaded[k], 16)

            two_by_two(sp, NSUP, load, tail=True)

        @block.tensor
        def _(pe):
            pe.sem_inc(z, USES)

            def turn(i, k, q, tail):
                u = k * NB + q
                r = u % 2
                if q == 0:
                    pe.wait_ge(loaded[k], 32 * i + 32)
                pe.wait_ge(hidden, USES * i + u + 1)
                pe.wait_ge(means, USES * i + u + 1)
                for n in range(2):
                    bank = banks[2 * r + n]
                    if tail:
                        last = nc.tensor.transpose(bank[0:C, 0:TAIL], X[n][k][0:TAIL, 0, :], m["ident"][0:TAIL, 0:TAIL])
                    for j in range(0 if tail else SUB // 2):
                        two = X[n][k][:, q * SUB + 2 * j:q * SUB + 2 * j + 2, :].rearrange("p t c -> p (t c)")
                        last = nc.tensor.transpose(bank[:, j * P:(j + 1) * P], two, m["ident"][:, :])
                last.then_inc(turned, 1)

            def project(i, k, q, tail):
                u = k * NB + q
                r = u % 2
                pe.wait_ge(hidden, USES * i + u + 3)
                pe.wait_ge(saved, USES * i + u + 1)
                p, w = (C, TAIL) if tail else (P, W)
                nc.tensor.matmul(banks[4 + r][0:p, 0:w], m["w1h"][0:p, 0:p], HC[r][0:p, 0:w], start=True, stop=False)
                pe.wait_ge(means, USES * i + u + 3)
                last = nc.tensor.matmul(banks[4 + r][0:p, 0:w], m["w1m"][0:p, 0:p], MC[r][0:p, 0:w], start=False, stop=True)
                last.then_inc(z, 1)

            def step(i, k, tail=False):
                n = 1 if tail else NB
                for q in range(n + 1):
                    if q < n:
                        turn(i, k, q, tail)
                    if q:
                        project(i, k, q - 1, tail)

            two_by_two(pe, NSUP, step, tail=True)

        @block.scalar
        def _(act):
            act.sem_inc(hidden, 2)
            act.sem_inc(saved, 2)

            def copy(i, k, q, tail):
                u = k * NB + q
                r = u % 2
                p, w = (C, TAIL) if tail else (P, W)
                act.wait_ge(turned, USES * i + u + 1)
                act.wait_ge(z, USES * i + u - 1 + USES)
                nc.scalar.activation(HC[r][0:p, 0:w], banks[2 * r][0:p, 0:w], ACT.Copy).then_inc(hidden, 1)

            def save(i, k, q, tail):
                u = k * NB + q
                r = u % 2
                act.wait_ge(z, USES * i + u + 1 + USES)
                p, w = (C, TAIL) if tail else (P, W)
                nc.scalar.activation(ZN[0:p, bass.ds((USES * i + u) * W, w)], banks[4 + r][0:p, 0:w], ACT.Identity,
                                     bias=m["b1b"][0:p, 0:1]).then_inc(saved, 1)

            def step(i, k, tail=False):
                n = 1 if tail else NB
                for q in range(n + 1):
                    if q < n:
                        copy(i, k, q, tail)
                    if q:
                        save(i, k, q - 1, tail)

            two_by_two(act, NSUP, step, tail=True)

        @block.vector
        def _(dve):
            dve.sem_inc(means, 2)

            def copy(i, k, q, tail):
                u = k * NB + q
                r = u % 2
                p, w = (C, TAIL) if tail else (P, W)
                dve.wait_ge(turned, USES * i + u + 1)
                dve.wait_ge(z, USES * i + u - 1 + USES)
                nc.vector.tensor_copy(MC[r][0:p, 0:w], banks[2 * r + 1][0:p, 0:w]).then_inc(means, 1)

            def count(i, k, q, tail):
                u = k * NB + q
                dve.wait_ge(saved, USES * i + u + 3)
                if tail:
                    nc.vector.bn_stats(m["stats"][0:C, 2 * NSUB, :], ZN[0:C, NSUB * W:NSUB * W + TAIL])
                else:
                    nc.vector.bn_stats(m["stats"][:, bass.ds(USES * i + u, 1), :], ZN[:, bass.ds((USES * i + u) * W, W)])

            def step(i, k, tail=False):
                n = 1 if tail else NB
                for q in range(n + 1):
                    if q < n:
                        copy(i, k, q, tail)
                    if q:
                        count(i, k, q - 1, tail)

            two_by_two(dve, NSUP, step, tail=True)


def node_out(nc, block, held, m, out_table):
    stage = "no"
    with ExitStack() as ctx:
        X = [ctx.enter_context(nc.sbuf_tensor(f"{stage}_rows{k}", [P, SUP, C], F32)) for k in range(2)]
        Y = [ctx.enter_context(nc.sbuf_tensor(f"{stage}_out{k}", [P, SUP, C], F32)) for k in range(2)]
        HC = [ctx.enter_context(nc.sbuf_tensor(f"{stage}_hidden{k}", [P, SUB // 2 * P], F32)) for k in range(4)]
        loaded, stored = pair(held, nc, stage, "loaded"), pair(held, nc, stage, "stored")
        hidden, mixed, biased, out = sems(held, nc, stage, "hidden", "mixed", "biased", "out")
        banks, AB, ZN = m["bank"], m["AB"], m["ZN"]
        NB = SUP // SUB
        USES = 2 * NB
        W = SUB // 2 * P

        def before(u, ring):
            return u - ring if u >= ring else u % ring + (USES - 1 - u % ring) // ring * ring - USES

        def rows(table, start, tail):
            if tail:
                return table[P * GRID:N, :].rearrange("(p t) c -> p t c", t=1)
            return grid_view(table)[:, bass.ds(start, SUP), :]


        @block.sync
        def _(sp):
            def load(i, k, tail=False):
                p, t = (TAIL, 1) if tail else (P, SUP)
                start = start_of(sp, i, k, SUP)
                sp.wait_ge(out, USES * i + k * NB + NB)
                sp.dma_start(X[k][0:p, 0:t, :], rows(m["XA"], start, tail)).then_inc(loaded[k], 16)

            two_by_two(sp, NSUP, load, tail=True)

        @block.scalar
        def _(act):
            def step(i, k, tail=False):
                for q in range(1 if tail else NB):
                    u = k * NB + q
                    act.wait_ge(mixed, USES * i + before(u, 4) + 1 + USES)
                    p, w = (C, TAIL) if tail else (P, W)
                    nc.scalar.activation(HC[u % 4][0:p, 0:w], ZN[0:p, bass.ds((USES * i + u) * W, w)], ACT.Relu,
                                         bias=AB[0:p, 1:2], scale=AB[0:p, 0:1]).then_inc(hidden, 1)

            two_by_two(act, NSUP, step, tail=True)

        @block.tensor
        def _(pe):
            pe.sem_inc(mixed, USES)

            def step(i, k, tail=False):
                for q in range(1 if tail else NB):
                    u = k * NB + q
                    pe.wait_ge(hidden, USES * i + u + 1)
                    pe.wait_ge(out, USES * i + before(u, 4) + 1 + USES)
                    if tail:
                        last = nc.tensor.matmul(banks[u % 4][0:TAIL, 0:C], HC[u % 4][0:C, 0:TAIL], m["w2b"][0:C, 0:C],
                                                start=True, stop=True)
                    for j in range(0 if tail else SUB // 2):
                        last = nc.tensor.matmul(banks[u % 4][:, j * P:(j + 1) * P], HC[u % 4][:, j * P:(j + 1) * P],
                                                m["w2b"][:, :], start=True, stop=True)
                    last.then_inc(mixed, 1)

            two_by_two(pe, NSUP, step, tail=True)

        @block.vector
        def _(dve):
            dve.sem_inc(out, USES)

            def bias(i, k, tail=False):
                p, t = (TAIL, 1) if tail else (P, SUP)
                dve.wait_ge(loaded[k], 16 * i + 16)
                nc.vector.tensor_tensor(X[k][0:p, 0:t, :], X[k][0:p, 0:t, :],
                                        m["b2b"][0:p, :].unsqueeze(1).to_broadcast([p, t, C]), ALU.add).then_inc(biased, 1)

            def step(i, k, tail=False):
                if later(i):
                    dve.wait_ge(stored[k], 16 * i)
                dve.wait_ge(biased, 2 * i + k + 1)
                for q in range(1 if tail else NB):
                    u = k * NB + q
                    dve.wait_ge(mixed, USES * i + u + 1 + USES)
                    p, t = (TAIL, 1) if tail else (P, SUB)
                    nc.vector.tensor_tensor(
                        Y[k][0:p, q * SUB:q * SUB + t, :], banks[u % 4][0:p, 0:t * C].rearrange("p (t c) -> p t c", c=C),
                        X[k][0:p, q * SUB:q * SUB + t, :], ALU.add).then_inc(out, 1)

            staggered(dve, NSUP + 1, (step, 0), (bias, 1), peel=True)

        @block.gpsimd
        def _(pool):
            def store(i, k, tail=False):
                p, t = (TAIL, 1) if tail else (P, SUP)
                start = start_of(pool, i, k, SUP)
                pool.wait_ge(out, USES * i + k * NB + (1 if tail else NB) + USES)
                pool.dma_start(rows(out_table, start, tail), Y[k][0:p, 0:t, :]).then_inc(stored[k], 16)

            two_by_two(pool, NSUP, store, tail=True)
            for k in range(2):
                pool.wait_ge(stored[k], 16 * (NSUP // 2 + 1))


def kernel(x, src, dst, edge_attr_16, edge_attr_64, L0_gnn_Wl, L0_gnn_Wr, L0_gnn_We, L0_gnn_att, L0_gnn_gat_bias, L0_gnn_gn_weight,
           L0_gnn_gn_bias, L0_gnn_gn_mean_scale, L1_gnn_u, L1_gnn_W1a, L1_gnn_b1a, L1_gnn_g1, L1_gnn_be1, L1_gnn_W2a, L1_gnn_b2a,
           L1_gnn_W1b, L1_gnn_b1b, L1_gnn_g2, L1_gnn_be2, L1_gnn_W2b, L1_gnn_b2b):
    import concourse.bacc as bacc
    from concourse.bass_utils import run_bass_kernel_spmd

    def padded(values, fill, before=0):
        row = np.full(EP, fill, np.int32)
        row[:before] = -1
        some = np.asarray(values)[:EP - before]
        row[before:before + some.size] = some
        return row

    def by_tile(row):
        return np.ascontiguousarray(row.reshape(TILES, P).T)

    def by_row(row):
        return np.ascontiguousarray(row.reshape(RG, RT, P).transpose(1, 0, 2))

    src, dst = np.asarray(src), np.asarray(dst)
    own, behind = padded(dst, FAR), padded(dst[1:], FAR)
    behind[E - 1:] = FAR
    ahead = padded(dst, FAR, before=1)
    ea16T = np.zeros((DE, EP), np.float32)
    ea16T[:, :E] = np.asarray(edge_attr_16).T
    ea64T = np.zeros((C, EP), np.float32)
    ea64T[:, :E] = np.asarray(edge_attr_64).T
    arrays = {
        "x": x, "gidx": np.ascontiguousarray(np.stack([by_tile(padded(src, 0)), by_tile(padded(dst, 0))], axis=2)),
        "dst_pt": np.ascontiguousarray(np.stack([by_tile(r) for r in (own, behind, ahead)], axis=1)),
        "dst_rows": np.ascontiguousarray(np.stack([by_row(r) for r in (own, behind, ahead)], axis=1)),
        "ea16T": ea16T, "ea64T": ea64T,
        "Wl": L0_gnn_Wl, "Wr": L0_gnn_Wr, "We": L0_gnn_We, "att": L0_gnn_att, "gat_bias": L0_gnn_gat_bias,
        "gn_weight": L0_gnn_gn_weight, "gn_bias": L0_gnn_gn_bias, "gn_mean_scale": L0_gnn_gn_mean_scale,
        "W1a": L1_gnn_W1a, "W2a": L1_gnn_W2a, "W1b": L1_gnn_W1b, "W2b": L1_gnn_W2b,
    }
    for name, row in (("b1a", L1_gnn_b1a), ("g1", L1_gnn_g1), ("be1", L1_gnn_be1), ("b2a", L1_gnn_b2a), ("b1b", L1_gnn_b1b),
                      ("g2", L1_gnn_g2), ("be2", L1_gnn_be2), ("b2b", L1_gnn_b2b)):
        arrays[name] = np.asarray(row).reshape(1, C)
    nc = bacc.Bacc("TRN2", target_bir_lowering=False, num_devices=1)
    aps, given = {}, {}
    for name, value in arrays.items():
        value = np.ascontiguousarray(value)
        given[f"in_{name}"] = value
        aps[name] = nc.dram_tensor(f"in_{name}", value.shape, mybir.dt.from_np(value.dtype), kind="ExternalInput").ap()
    out = nc.dram_tensor("out", (N, C), F32, kind="ExternalOutput").ap()
    build(nc, aps, out)
    return run_bass_kernel_spmd(nc, [given], core_ids=[0]).results[0]["out"]
```
